# Optimizing a Trainium2 kernel written in Bass

```python
import numpy as np
import jax
import jax.numpy as jnp

def _softmax(x, axis=-1):
    return jax.nn.softmax(x, axis=axis)

def _gelu(x):
    return jax.nn.gelu(x, approximate=True)

def _silu(x):
    return jax.nn.silu(x)

def _sigmoid(x):
    return jax.nn.sigmoid(x)

def _layernorm(x, axis=-1, eps=1e-05):
    m = jnp.mean(x, axis=axis, keepdims=True)
    v = jnp.var(x, axis=axis, keepdims=True)
    return (x - m) / jnp.sqrt(v + eps)

def _scatter_add(tgt, idx, src, axis=0):
    return tgt.at[idx].add(src)

def _segment_sum(src, seg, n):
    return jax.ops.segment_sum(src, seg, n)
kernel_name = 'mk_gnn_ffn_d2_gnn_r16_7563ce'

def setup_inputs(seed: int=0):
    np.random.seed(seed)
    _w = jnp.asarray

    def _rec_inputs():
        import jax
        import jax.numpy as jnp
        _gk = jax.random.key(seed)
        x = -0.0001126 + 1 * jax.random.normal(jax.random.fold_in(_gk, 1), (625, 768), jnp.float32)
        _s = jax.random.randint(jax.random.fold_in(_gk, 2), (10000,), 0, 625, jnp.int32)
        _d = jax.random.randint(jax.random.fold_in(_gk, 3), (10000,), 0, 625, jnp.int32)
        _loop = jnp.arange(625, dtype=jnp.int32)
        src = jnp.concatenate([_s, _d, _loop])
        dst = jnp.concatenate([_d, _s, _loop])
        _o = jnp.argsort(dst, stable=True)
        src = src[_o]
        dst = dst[_o]
        return (x, src, dst)
    x, src, dst = _rec_inputs()

    def _L0_gnn_setup():
        import jax, jax.numpy as jnp
        import numpy as np
        N_NODES = 625
        key = jax.random.key(seed)
        k1, k2, k3 = jax.random.split(key, 3)
        x = jax.random.normal(k1, (N_NODES, 768), dtype=jnp.float32)
        edge_index = jax.random.randint(k2, (2, 6250), 0, N_NODES, dtype=jnp.int32)
        W = jax.random.normal(k3, (768, 768), dtype=jnp.float32) * (1.0 / np.sqrt(768))
        b = jnp.zeros((768,), dtype=jnp.float32)
        return {'x': x, 'edge_index': edge_index, 'W': W, 'b': b}
    _L0_gnn_all = _L0_gnn_setup()
    _L0_gnn_in = {k: v for k, v in _L0_gnn_all.items() if k in ('W', 'b')}
    del _L0_gnn_all

    def _L0_ffn_setup():
        import jax, jax.numpy as jnp
        import numpy as np
        B, S, D, H = (1, 128, 768, 12)
        E, K, I = (8, 2, 1024)
        IS = 2 * I
        EPS = 1e-05
        ROUTE_SCALE = 1.0

        def rmsnorm(x, w, eps=EPS):
            xf = x.astype(jnp.float32)
            return (xf * jax.lax.rsqrt(jnp.mean(xf * xf, axis=-1, keepdims=True) + eps)).astype(x.dtype) * w

        def _forward(x, norm1_w, norm3_w, gate_w, w1, b1, w2, b2, w3, b3, fc1_w, fc1_b, fc2_w, fc2_b):
            b, s, d = x.shape
            hd = d // H
            xn = rmsnorm(x, norm1_w)
            qkv = xn.reshape(b, s, H, hd).transpose(0, 2, 1, 3)
            scores = jnp.einsum('bhqd,bhkd->bhqk', qkv, qkv) / np.sqrt(hd)
            attn = jax.nn.softmax(scores, axis=-1)
            ao = jnp.einsum('bhqk,bhkd->bhqd', attn, qkv)
            attn_out = ao.transpose(0, 2, 1, 3).reshape(b, s, d)
            out = x + attn_out
            xf = rmsnorm(out, norm3_w).reshape(-1, d)
            n = xf.shape[0]
            logits = xf @ gate_w.T
            sc = jax.nn.softmax(logits.astype(jnp.float32), axis=-1)
            _, idx = jax.lax.top_k(sc, K)
            weights = jnp.take_along_axis(sc, idx, axis=-1)
            weights = jnp.clip(weights, 1e-07) * ROUTE_SCALE
            weights = weights.astype(xf.dtype)
            cmb = jnp.zeros((n, E), xf.dtype).at[jnp.arange(n)[:, None], idx].add(weights)
            a = jnp.einsum('nd,eid->nei', xf, w1) + b1
            g = jnp.einsum('nd,eid->nei', xf, w3) + b3
            h = jax.nn.silu(a) * g
            eo = jnp.einsum('nei,edi->ned', h, w2) + b2
            y = jnp.einsum('ned,ne->nd', eo, cmb)
            z = jax.nn.silu(xf @ fc1_w.T + fc1_b) @ fc2_w.T + fc2_b
            moe_out = (y + z).reshape(b, s, d)
            return out + moe_out
        key = jax.random.key(seed)
        ks = jax.random.split(key, 8)
        sc = 0.02
        return {'x': jax.random.normal(ks[0], (B, S, D), jnp.float32), 'norm1_w': jnp.ones((D,), jnp.float32), 'norm3_w': jnp.ones((D,), jnp.float32), 'gate_w': jax.random.normal(ks[1], (E, D), jnp.float32) * sc, 'w1': jax.random.normal(ks[2], (E, I, D), jnp.float32) * sc, 'b1': jnp.zeros((E, I), jnp.float32), 'w2': jax.random.normal(ks[3], (E, D, I), jnp.float32) * sc, 'b2': jnp.zeros((E, D), jnp.float32), 'w3': jax.random.normal(ks[4], (E, I, D), jnp.float32) * sc, 'b3': jnp.zeros((E, I), jnp.float32), 'fc1_w': jax.random.normal(ks[5], (IS, D), jnp.float32) * sc, 'fc1_b': jnp.zeros((IS,), jnp.float32), 'fc2_w': jax.random.normal(ks[6], (D, IS), jnp.float32) * sc, 'fc2_b': jnp.zeros((D,), jnp.float32)}
    _L0_ffn_all = _L0_ffn_setup()
    _L0_ffn_in = {k: v for k, v in _L0_ffn_all.items() if k in ('norm1_w', 'norm3_w', 'gate_w', 'w1', 'b1', 'w2', 'b2', 'w3', 'b3', 'fc1_w', 'fc1_b', 'fc2_w', 'fc2_b')}
    del _L0_ffn_all

    def _L1_gnn_setup():
        import jax, jax.numpy as jnp
        import numpy as np
        N = 3125
        E = 15625
        H = 12
        D = 64
        NEG_SLOPE = 0.2
        key = jax.random.key(seed)
        k1, k2, k3, k4, k5, k6, k7 = jax.random.split(key, 7)
        h = jax.random.normal(k1, (N, H * D), dtype=jnp.float32)
        src = jnp.concatenate([jnp.arange(N, dtype=jnp.int32), jax.random.randint(k2, (E - N,), 0, N, dtype=jnp.int32)])
        dst = jnp.concatenate([jnp.arange(N, dtype=jnp.int32), jax.random.randint(k3, (E - N,), 0, N, dtype=jnp.int32)])
        xav = 1.414 / np.sqrt(D)
        W_fc = jax.random.normal(k4, (D, D), dtype=jnp.float32) * xav
        attn_l = jax.random.normal(k5, (H, D), dtype=jnp.float32) * 0.15
        attn_r = jax.random.normal(k6, (H, D), dtype=jnp.float32) * 0.15
        W_res = jax.random.normal(k7, (D, D), dtype=jnp.float32) * xav
        return {'h': h, 'W_fc': W_fc, 'attn_l': attn_l, 'attn_r': attn_r, 'W_res': W_res, 'src': src, 'dst': dst}
    _L1_gnn_all = _L1_gnn_setup()
    _L1_gnn_in = {k: v for k, v in _L1_gnn_all.items() if k in ('W_fc', 'attn_l', 'attn_r', 'W_res')}
    del _L1_gnn_all

    def _L1_ffn_setup():
        import jax, jax.numpy as jnp
        import numpy as np
        D_MODEL = 768
        D_EXPERT = 1536
        N_EXPERTS = 8
        TOP_K = 2
        EPS = 1e-06

        def _rms_norm(x, w):
            var = jnp.mean(jnp.square(x), axis=-1, keepdims=True)
            return x * jax.lax.rsqrt(var + EPS) * w
        key = jax.random.key(seed)
        ks = jax.random.split(key, 6)
        s_in = 1.0 / np.sqrt(D_MODEL)
        s_mid = 1.0 / np.sqrt(D_EXPERT)
        return {'x': jax.random.normal(ks[0], (2, 128, D_MODEL), dtype=jnp.float32), 'norm_w': jnp.ones((D_MODEL,), dtype=jnp.float32), 'router_w': jax.random.normal(ks[1], (N_EXPERTS, D_MODEL), dtype=jnp.float32) * s_in, 'gate_w': jax.random.normal(ks[2], (N_EXPERTS, D_EXPERT, D_MODEL), dtype=jnp.float32) * s_in, 'up_w': jax.random.normal(ks[3], (N_EXPERTS, D_EXPERT, D_MODEL), dtype=jnp.float32) * s_in, 'down_w': jax.random.normal(ks[4], (N_EXPERTS, D_MODEL, D_EXPERT), dtype=jnp.float32) * s_mid}
    _L1_ffn_all = _L1_ffn_setup()
    _L1_ffn_in = {k: v for k, v in _L1_ffn_all.items() if k in ('norm_w', 'router_w', 'gate_w', 'up_w', 'down_w')}
    del _L1_ffn_all
    return {'x': x, 'src': src, 'dst': dst, 'L0_gnn_W': _L0_gnn_in['W'], 'L0_gnn_b': _L0_gnn_in['b'], 'L0_ffn_norm1_w': _L0_ffn_in['norm1_w'], 'L0_ffn_norm3_w': _L0_ffn_in['norm3_w'], 'L0_ffn_gate_w': _L0_ffn_in['gate_w'], 'L0_ffn_w1': _L0_ffn_in['w1'], 'L0_ffn_b1': _L0_ffn_in['b1'], 'L0_ffn_w2': _L0_ffn_in['w2'], 'L0_ffn_b2': _L0_ffn_in['b2'], 'L0_ffn_w3': _L0_ffn_in['w3'], 'L0_ffn_b3': _L0_ffn_in['b3'], 'L0_ffn_fc1_w': _L0_ffn_in['fc1_w'], 'L0_ffn_fc1_b': _L0_ffn_in['fc1_b'], 'L0_ffn_fc2_w': _L0_ffn_in['fc2_w'], 'L0_ffn_fc2_b': _L0_ffn_in['fc2_b'], 'L1_gnn_W_fc': _L1_gnn_in['W_fc'], 'L1_gnn_attn_l': _L1_gnn_in['attn_l'], 'L1_gnn_attn_r': _L1_gnn_in['attn_r'], 'L1_gnn_W_res': _L1_gnn_in['W_res'], 'L1_ffn_norm_w': _L1_ffn_in['norm_w'], 'L1_ffn_router_w': _L1_ffn_in['router_w'], 'L1_ffn_gate_w': _L1_ffn_in['gate_w'], 'L1_ffn_up_w': _L1_ffn_in['up_w'], 'L1_ffn_down_w': _L1_ffn_in['down_w']}

def reference(x, src, dst, L0_gnn_W, L0_gnn_b, L0_ffn_norm1_w, L0_ffn_norm3_w, L0_ffn_gate_w, L0_ffn_w1, L0_ffn_b1, L0_ffn_w2, L0_ffn_b2, L0_ffn_w3, L0_ffn_b3, L0_ffn_fc1_w, L0_ffn_fc1_b, L0_ffn_fc2_w, L0_ffn_fc2_b, L1_gnn_W_fc, L1_gnn_attn_l, L1_gnn_attn_r, L1_gnn_W_res, L1_ffn_norm_w, L1_ffn_router_w, L1_ffn_gate_w, L1_ffn_up_w, L1_ffn_down_w):
    import jax
    import jax.numpy as jnp

    def _L0_gnn_ref(x, edge_index, W, b):
        import jax, jax.numpy as jnp
        import numpy as np
        N_NODES = 625
        n = x.shape[0]
        loops = jnp.arange(n, dtype=edge_index.dtype)
        row = jnp.concatenate([edge_index[0], loops])
        col = jnp.concatenate([edge_index[1], loops])
        ones = jnp.ones(row.shape[0], dtype=x.dtype)
        deg = jax.ops.segment_sum(ones, col, num_segments=n)
        dinv = jnp.where(deg > 0, jax.lax.rsqrt(deg), 0.0)
        norm = dinv[row] * dinv[col]
        h = x @ W
        msg = h[row] * norm[:, None]
        out = jax.ops.segment_sum(msg, col, num_segments=n) + b
        return out

    def _L0_ffn_ref(x, norm1_w, norm3_w, gate_w, w1, b1, w2, b2, w3, b3, fc1_w, fc1_b, fc2_w, fc2_b):
        import jax, jax.numpy as jnp
        import numpy as np
        B, S, D, H = (1, 128, 768, 12)
        E, K, I = (8, 2, 1024)
        IS = 2 * I
        EPS = 1e-05
        ROUTE_SCALE = 1.0

        def rmsnorm(x, w, eps=EPS):
            xf = x.astype(jnp.float32)
            return (xf * jax.lax.rsqrt(jnp.mean(xf * xf, axis=-1, keepdims=True) + eps)).astype(x.dtype) * w

        def _forward(x, norm1_w, norm3_w, gate_w, w1, b1, w2, b2, w3, b3, fc1_w, fc1_b, fc2_w, fc2_b):
            b, s, d = x.shape
            hd = d // H
            xn = rmsnorm(x, norm1_w)
            qkv = xn.reshape(b, s, H, hd).transpose(0, 2, 1, 3)
            scores = jnp.einsum('bhqd,bhkd->bhqk', qkv, qkv) / np.sqrt(hd)
            attn = jax.nn.softmax(scores, axis=-1)
            ao = jnp.einsum('bhqk,bhkd->bhqd', attn, qkv)
            attn_out = ao.transpose(0, 2, 1, 3).reshape(b, s, d)
            out = x + attn_out
            xf = rmsnorm(out, norm3_w).reshape(-1, d)
            n = xf.shape[0]
            logits = xf @ gate_w.T
            sc = jax.nn.softmax(logits.astype(jnp.float32), axis=-1)
            _, idx = jax.lax.top_k(sc, K)
            weights = jnp.take_along_axis(sc, idx, axis=-1)
            weights = jnp.clip(weights, 1e-07) * ROUTE_SCALE
            weights = weights.astype(xf.dtype)
            cmb = jnp.zeros((n, E), xf.dtype).at[jnp.arange(n)[:, None], idx].add(weights)
            a = jnp.einsum('nd,eid->nei', xf, w1) + b1
            g = jnp.einsum('nd,eid->nei', xf, w3) + b3
            h = jax.nn.silu(a) * g
            eo = jnp.einsum('nei,edi->ned', h, w2) + b2
            y = jnp.einsum('ned,ne->nd', eo, cmb)
            z = jax.nn.silu(xf @ fc1_w.T + fc1_b) @ fc2_w.T + fc2_b
            moe_out = (y + z).reshape(b, s, d)
            return out + moe_out
        return _forward(x, norm1_w, norm3_w, gate_w, w1, b1, w2, b2, w3, b3, fc1_w, fc1_b, fc2_w, fc2_b)

    def _L1_gnn_ref(h, W_fc, attn_l, attn_r, W_res, src, dst):
        import jax, jax.numpy as jnp
        import numpy as np
        N = 3125
        E = 15625
        H = 12
        D = 64
        NEG_SLOPE = 0.2
        n = h.shape[0]
        hh = h.reshape(n, H, D)
        ft = jnp.einsum('nhd,ed->nhe', hh, W_fc)
        a1 = jnp.einsum('nhd,hd->nh', ft, attn_l)
        a2 = jnp.einsum('nhd,hd->nh', ft, attn_r)
        e = jax.nn.leaky_relu(a1[src] + a2[dst], negative_slope=NEG_SLOPE)
        m = jax.ops.segment_max(e, dst, num_segments=n)
        ee = jnp.exp(e - m[dst])
        denom = jax.ops.segment_sum(ee, dst, num_segments=n)
        alpha = ee / denom[dst]
        agg = jax.ops.segment_sum(alpha[:, :, None] * ft[src], dst, num_segments=n)
        res = jnp.einsum('nhd,ed->nhe', hh, W_res)
        return jax.nn.relu((res + agg).reshape(n, H * D))

    def _L1_ffn_ref(x, norm_w, router_w, gate_w, up_w, down_w):
        import jax, jax.numpy as jnp
        import numpy as np
        D_MODEL = 768
        D_EXPERT = 1536
        N_EXPERTS = 8
        TOP_K = 2
        EPS = 1e-06

        def _rms_norm(x, w):
            var = jnp.mean(jnp.square(x), axis=-1, keepdims=True)
            return x * jax.lax.rsqrt(var + EPS) * w
        residual = x
        B, S, D = x.shape
        xn = _rms_norm(x, norm_w)
        xf = xn.reshape(-1, D)
        logits = xf @ router_w.T
        probs = jax.nn.softmax(logits, axis=-1)
        _, top_idx = jax.lax.top_k(probs, TOP_K)
        sel = jax.nn.one_hot(top_idx, N_EXPERTS, dtype=probs.dtype).sum(axis=1)
        comb_w = probs * sel
        g = jnp.einsum('td,efd->tef', xf, gate_w)
        u = jnp.einsum('td,efd->tef', xf, up_w)
        h = jax.nn.silu(g) * u
        h = h * comb_w[:, :, None]
        y = jnp.einsum('tef,edf->td', h, down_w)
        return y.reshape(B, S, D) + residual
    edge_index = jnp.stack([src, dst])
    x = x + _L0_gnn_ref(_layernorm(x, axis=-1), edge_index, L0_gnn_W, L0_gnn_b)
    x = x + _L0_ffn_ref(_layernorm(x, axis=-1)[None], L0_ffn_norm1_w, L0_ffn_norm3_w, L0_ffn_gate_w, L0_ffn_w1, L0_ffn_b1, L0_ffn_w2, L0_ffn_b2, L0_ffn_w3, L0_ffn_b3, L0_ffn_fc1_w, L0_ffn_fc1_b, L0_ffn_fc2_w, L0_ffn_fc2_b)[0]
    x = x + _L1_gnn_ref(_layernorm(x, axis=-1), L1_gnn_W_fc, L1_gnn_attn_l, L1_gnn_attn_r, L1_gnn_W_res, src, dst)
    x = x + _L1_ffn_ref(_layernorm(x, axis=-1)[None], L1_ffn_norm_w, L1_ffn_router_w, L1_ffn_gate_w, L1_ffn_up_w, L1_ffn_down_w)[0]
    return x

_drawn_inputs = setup_inputs


def setup_inputs(seed=0):
    import zlib

    import numpy as np

    out = dict(_drawn_inputs(seed))
    spreads = {'L0_gnn_b': (0.0, 0.1),
     'L0_ffn_norm1_w': (1.0, 0.2),
     'L0_ffn_norm3_w': (1.0, 0.6),
     'L0_ffn_b1': (0.0, 0.8),
     'L0_ffn_b2': (0.0, 0.623),
     'L0_ffn_b3': (0.0, 0.8),
     'L0_ffn_fc1_b': (0.0, 1.837),
     'L0_ffn_fc2_b': (0.0, 0.8),
     'L1_ffn_norm_w': (1.0, 0.546)}
    factors = {'L0_ffn_gate_w': 3.413,
     'L0_ffn_w1': 3.915,
     'L0_ffn_w2': 3.826,
     'L0_ffn_w3': 3.895,
     'L1_gnn_attn_r': 8.0}
    for name, (base, spread) in spreads.items():
        noise = np.random.default_rng([zlib.crc32(name.encode()), seed]).standard_normal(out[name].shape)
        drawn = base * np.exp(spread * noise) if base else spread * noise
        out[name] = jnp.asarray(drawn.astype(out[name].dtype))
    for name, factor in factors.items():
        out[name] = (out[name] * factor).astype(out[name].dtype)
    return out
```

```python
import concourse.bass as bass
from concourse import mybir
from contextlib import ExitStack

F32 = mybir.dt.float32
F16 = mybir.dt.float16
BF16 = mybir.dt.bfloat16
I32 = mybir.dt.int32
ALU = mybir.AluOpType
ACT = mybir.ActivationFunctionType
AX = mybir.AxisListType

T, D, H = 625, 768, 12
HD = D // H
EDGES = 20625
NE = 8
I0, IS, I1 = 1024, 2048, 1536

P, NT = 125, 5
KC = D // 128
EC = EDGES // P
EU = 3
B = 256
NPMAX = NE + 4
NTAB = NPMAX + 1
GS = 214
NG = 3
RING = 4
WS = 64.0
NEG = -1e30
BANK = 512

C_ZERO, C_ALL = 2, 11
F_GRAPH, F_MHA, F_ROUTE0, F_SHARED, F_EXP0, F_LAYER0, F_GAT, F_ROUTE1, F_EXP1 = range(1, 10)
R_Z0, R_HS, R_XN0, R_XF0, R_Z1, R_XF1 = range(1, 7)
N_MHA = H * NT
N_RD = N_MHA + 1


class Phase:

    def __init__(self, sem, name, ic, gated, bias, n, rows):
        self.ic, self.gated, self.bias, self.n, self.rows = ic, gated, bias, n, rows
        self.wide = D * (3 if gated else 2)
        self.cols = self.wide + (2 if bias else 0)
        self.raw = [sem(f"{name}_unit_loaded{r}") for r in range(RING)]
        self.hi = sem(f"{name}_unit_high")
        self.lo = sem(f"{name}_unit_low")
        self.up = sem(f"{name}_up_done")
        self.silu = sem(f"{name}_silu_done")
        self.hseq = sem(f"{name}_hidden_steps")
        self.h = sem(f"{name}_hidden_split")
        self.down = sem(f"{name}_down_done")
        self.xrows = sem(f"{name}_rows_loaded")
        self.xt = sem(f"{name}_rows_transposed")
        self.xhi = sem(f"{name}_x_high")
        self.xlo = sem(f"{name}_x_low")
        self.ya = sem(f"{name}_out_tile0")
        self.yv = sem(f"{name}_out_tile1")
        self.stored = sem(f"{name}_out_stored")
        self.yfree = sem(f"{name}_out_free")


def bass_gnn_moe_stack(nc, x, src, dst, gnn_w, vecs, gate0, gate1, units0, units_s, units1,
                       bias_out, w_heads, attn_lr, out):
    ctx = ExitStack()
    with ctx:
        def sb(name, shape, dt=F32):
            return ctx.enter_context(nc.sbuf_tensor(name, shape, dt))

        def sem(name):
            return ctx.enter_context(nc.semaphore(name))

        x_slots = nc.dram_tensor("x_slots", [NTAB * B, D], F32, kind="Internal").ap()
        y_slots = nc.dram_tensor("y_slots", [NPMAX * B, D], F32, kind="Internal").ap()
        x_shared = nc.dram_tensor("x_shared", [(NG + 1) * GS, D], F32, kind="Internal").ap()
        y_shared = nc.dram_tensor("y_shared", [NG * GS, D], F32, kind="Internal").ap()

        xres = sb("xres", [P, NT, D])
        z = sb("z", [P, NT, D])
        xf = sb("xf", [P, NT, D])
        big = sb("big", [128, 7500])
        ext = sb("ext", [128, 6500])
        cds = sb("cds", [P, NT, T])
        mask = sb("mask", [P, NT, T], BF16)
        raw01 = sb("raw01", [128, 2, 3 * D + 2])
        wh = sb("wh", [128, RING, 3 * D], F16)
        wl = sb("wl", [128, RING, 3 * D], F16)
        ident = sb("ident", [128, 128])
        ones = sb("ones", [128, 128])
        tri = sb("tri", [P, P])
        vec = sb("vec", [P, 2, D])
        gates = sb("gates", [128, 2, KC, NE])
        bout = sb("bout", [NE + 1, D])
        edges_i = sb("edges_i", [P, 2, EC], I32)
        edges_f = sb("edges_f", [P, 2, EC])
        st = sb("st", [P, NT, 2, 6])
        mv = sb("mv", [P, NT, 2])
        rs = sb("rs", [P, 4, NT])
        dinv = sb("dinv", [P, NT])
        sm = sb("sm", [P, 16, NT, NE])
        s8 = sb("s8", [P, 8, NE])
        cst8 = sb("cst8", [P, 3, NT, NE])
        tabf = sb("tabf", [1, 3, NTAB, NE])
        tab1 = sb("tab1", [1, 4, NTAB + 1])
        tabi = sb("tabi", [1, 2, NTAB + 1], I32)
        slots_f = sb("slots_f", [P, 2, NT])
        slots_i = sb("slots_i", [P, 2, NT], I32)
        wts = sb("wts", [P, 2, NT])
        cmb = sb("cmb", [P, NT, NE + 1])
        cmbT = sb("cmbT", [NE + 1, T])
        cols = sb("cols", [P, 12, NT])
        a12 = sb("a12", [P, 2, NT, H + 1])

        region = lambda t, a, n: t[:, a:a + n]
        tD = region(big, 0, KC * T).rearrange("p (c n) -> p c n", c=KC)
        CT = big[0:P, 3750:3750 + NT * T].rearrange("p (t n) -> p t n", t=NT)
        a1T = big[0:H, 3750:4375]
        a1m = big[0:H, 4375:5625].rearrange("p (s n) -> p s n", s=2)
        cur = big[:, 3750:5000].rearrange("p (s n) -> p s n", s=2)
        xrows = region(big, 0, 2 * D).rearrange("p (t d) -> p t d", t=2)
        yrows = region(big, 1536, 2 * D).rearrange("p (t d) -> p t d", t=2)
        xTh = region(big, 3072, 768).bitcast(F16).rearrange("p (c n) -> p c n", c=KC)
        xTl = region(big, 3840, 768).bitcast(F16).rearrange("p (c n) -> p c n", c=KC)
        sbuf = region(big, 4608, 512).rearrange("p (s n) -> p s n", s=2)
        tbuf = region(big, 5120, 512).rearrange("p (s n) -> p s n", s=2)
        hh = region(big, 5632, 256).bitcast(F16).rearrange("p (s n) -> p s n", s=2)
        hl = region(big, 5888, 256).bitcast(F16).rearrange("p (s n) -> p s n", s=2)
        bsm = region(big, 6144, 8).rearrange("p (s n) -> p s n", s=RING)
        wg = region(ext, 0, KC * D).rearrange("p (c n) -> p c n", c=KC)
        hot = ext[0:P, 4608:4608 + 1875].bitcast(F16).rearrange("p (s a n) -> p s a n", s=EU, a=2)
        prob = ext[0:P, 0:1250].rearrange("p (s n) -> p s n", s=2)
        probT = ext[0:P, 1250:2500].rearrange("p (s k n) -> p s k n", s=2, k=NT)
        relu1 = ext[0:P, 2500:3750].rearrange("p (s n) -> p s n", s=2)
        relu2 = ext[0:P, 3750:5000].rearrange("p (s n) -> p s n", s=2)
        junk = ext[0:P, 5000:5625]
        wheads = region(ext, 5632, 256)
        alr = ext[0:P, 0:2 * D].rearrange("p (a n) -> p a n", a=2)
        prod = ext[0:P, 1536:1536 + 2 * D].rearrange("p (a n) -> p a n", a=2)
        rows = ext[0:P, 0:6 * D].rearrange("p (s k n) -> p s k n", s=2, k=3)
        raw = [raw01[:, 0, :], raw01[:, 1, :], region(ext, 0, 3 * D + 2), region(ext, 2400, 3 * D + 2)]
        iota16 = sb("iota16", [P, T], F16)

        ps = ctx.enter_context(nc.psum_tensor("ps", [128, 8 * BANK], F32))

        def bank(b, n=1):
            return ps[:, b * BANK:(b + n) * BANK]

        def tiles5(two_banks, parts):
            return two_banks[0:parts, 0:NT * 128].rearrange("p (t n) -> p t n", t=NT)[:, :, 0:P]

        s_const = sem("s_const")
        s_fence = sem("s_fence")
        s_x = sem("s_x")
        s_edge = sem("s_edge")
        s_wg = sem("s_wg")
        s_vec = [sem(f"s_vec{i}") for i in range(2)]
        s_small = sem("s_small")
        s_zero = sem("s_zero")
        s_v = sem("s_v")
        s_sq = sem("s_sq")
        s_var = sem("s_var")
        s_hot = sem("s_hot")
        s_cmm = sem("s_cmm")
        s_ct = sem("s_ct")
        s_ctv = sem("s_ctv")
        s_cT = sem("s_cT")
        s_cda = sem("s_cda")
        s_cdv = sem("s_cdv")
        s_rowsok = sem("s_rowsok")
        s_tp = sem("s_tp")
        s_tpe = sem("s_tpe")
        s_hmm = sem("s_hmm")
        s_hev = sem("s_hev")
        s_agg = sem("s_agg")
        s_aggv = sem("s_aggv")
        s_cur = sem("s_cur")
        s_curv = sem("s_curv")
        s_hd = sem("s_hd")
        s_s = sem("s_s")
        s_mx = sem("s_mx")
        s_mxn = sem("s_mxn")
        s_exp = sem("s_exp")
        s_pT = sem("s_pT")
        s_pTe = sem("s_pTe")
        s_pv = sem("s_pv")
        s_pvv = sem("s_pvv")
        s_rd = sem("s_rd")
        s_lg = sem("s_lg")
        s_lge = sem("s_lge")
        s_lx = sem("s_lx")
        s_sel = sem("s_sel")
        s_rk = sem("s_rk")
        s_slot = sem("s_slot")
        s_scat = sem("s_scat")
        s_cmT = sem("s_cmT")
        s_cmTv = sem("s_cmTv")
        s_bo = sem("s_bo")
        s_bov = sem("s_bov")
        s_gat = [sem(f"s_gat{i}") for i in range(2)]
        s_add = sem("s_add")
        s_wh = sem("s_wh")
        s_ft = sem("s_ft")
        s_ftv = sem("s_ftv")
        s_al = sem("s_al")
        s_aT = sem("s_aT")
        s_aTv = sem("s_aTv")
        s_am = sem("s_am")
        s_ab = sem("s_ab")
        s_abf = sem("s_abf")
        s_gm = sem("s_gm")
        s_gb = sem("s_gb")
        s_r = sem("s_r")
        s_rm = sem("s_rm")
        s_ge = sem("s_ge")
        s_pc = sem("s_pc")
        s_gseq = sem("s_gseq")
        s_done = sem("s_done")
        s_tpa = sem("s_tpa")
        s_fta = sem("s_fta")
        s_cm = sem("s_cm")
        ph_s = Phase(sem, "shared", IS // 128, False, True, GS, x_shared)
        ph_0 = Phase(sem, "layer0", I0 // 128, True, True, B, x_slots)
        ph_1 = Phase(sem, "layer1", I1 // 128, True, False, B, x_slots)
        units = {id(ph_s): units_s, id(ph_0): units0, id(ph_1): units1}
        outs = {id(ph_s): y_shared, id(ph_0): y_slots, id(ph_1): y_slots}

        block = ctx.enter_context(nc.Block())

        ENGINES = 4

        def fence(eng, k):
            if k > 1:
                eng.wait_ge(s_fence, ENGINES * (k - 1))
            eng.drain().then_inc(s_fence, 1)
            eng.wait_ge(s_fence, ENGINES * k)

        def passes(eng):
            return eng.value_load(tabi[0:1, 0:1, NTAB:NTAB + 1].rearrange("p a n -> p (a n)"),
                                  min_val=NE, max_val=NPMAX)

        def ffn_sync(sp, ph, n_pass, routed):
            def expert(i):
                if not routed:
                    return 0
                return sp.value_load(tabi[0:1, 0:1, bass.ds(i, 1)].rearrange("p a n -> p (a n)"),
                                     min_val=0, max_val=NE - 1)

            def load(i, e, u):
                g = i * ph.ic + u
                sp.wait_ge(ph.hi, g + 1)
                sp.wait_ge(ph.lo, g + 1)
                w = units[id(ph)]
                unit = w[bass.ds(e, 1), u, :, :].rearrange("a p n -> p (a n)") if routed else w[u, :, :]
                sp.dma_start(raw[u % RING][:, 0:ph.cols], unit).then_inc(ph.raw[u % RING], 16)

            with sp.Fori(0, n_pass) as i:
                e = expert(i)
                for u in range(ph.ic):
                    load(i, e, u)
            e = expert(n_pass)
            for u in range(2):
                load(n_pass, e, u)

        def ffn_pool(pool, ph, n_pass):
            def rows_in(i):
                source = ph.rows[bass.ds(i * ph.n, ph.n), :] if not isinstance(i, int) \
                    else ph.rows[i * ph.n:(i + 1) * ph.n, :]
                pool.dma_start(xrows[0:ph.n // 2, :, :],
                               source.rearrange("(t p) d -> p t d", t=2)).then_inc(ph.xrows, 16)

            rows_in(0)
            with pool.Fori(0, n_pass) as i:
                pool.wait_ge(ph.xt, i * 3 + 3)
                rows_in(i + 1)
                pool.wait_ge(ph.ya, i + 2)
                pool.wait_ge(ph.yv, i + 2)
                pool.dma_start(outs[id(ph)][bass.ds(i * ph.n, ph.n), :].rearrange("(t p) d -> p t d", t=2),
                               yrows[0:ph.n // 2, :, :]).then_inc(ph.stored, 16)
                pool.wait_ge(ph.stored, i * 16 + 16)
                pool.sem_inc(ph.yfree, 1)

        def ffn_scalar(act, ph, n_pass):
            half = ph.n // 2

            def high(i, u):
                g = i * ph.ic + u
                act.wait_ge(ph.raw[u % RING], i * (16 * ph.ic // RING) + 16 * (u // RING) + 16)
                act.wait_ge(ph.down, g + 1)
                if ph.bias:
                    nc.scalar.activation(bsm[:, u % RING, 0:1], raw[u % RING][:, ph.wide:ph.wide + 1], ACT.Copy)
                nc.scalar.activation(wh[:, u % RING, 0:ph.wide], raw[u % RING][:, 0:ph.wide], ACT.Copy,
                                     scale=WS).then_inc(ph.hi, 1)

            def x_high(i):
                for k in range(3):
                    act.wait_ge(ph.xt, i * 3 + k + 1)
                    src_ = bank(6 + k % 2).rearrange("p (c n) -> p c n", c=2)[:, :, 0:ph.n]
                    nc.scalar.activation(xTh[:, 2 * k:2 * k + 2, 0:ph.n], src_, ACT.Copy).then_inc(ph.xhi, 1)

            x_high(0)
            high(0, 0)
            high(0, 1)
            with act.Fori(0, n_pass) as i:
                for u in range(ph.ic):
                    g = i * ph.ic + u
                    high(i, u + 2)
                    act.wait_ge(ph.up, g + 1)
                    if ph.bias:
                        act.wait_ge(ph.hi, g + 1 + RING)
                        bias = bsm[:, u % RING, 0:1]
                    else:
                        bias = 0.0
                    a = bank(4 + u % 2)[:, 0:ph.n]
                    nc.scalar.activation(sbuf[:, u % 2, 0:ph.n], a, ACT.Silu, bias=bias,
                                         scale=1.0 / WS).then_inc(ph.silu, 1)
                x_high(i + 1)
                act.wait_ge(ph.down, (i + 1) * ph.ic + RING)
                act.wait_ge(ph.yfree, i + 1)
                nc.scalar.activation(yrows[0:half, 0, :], ps[0:half, 0:D], ACT.Copy,
                                     scale=1.0 / WS).then_inc(ph.ya, 1)

        def ffn_vector(dve, ph, n_pass):
            half = ph.n // 2

            def low(i, u):
                g = i * ph.ic + u
                dve.wait_ge(ph.hi, g + 1 + RING)
                if ph.bias and ph.gated:
                    nc.vector.tensor_scalar(bsm[:, u % RING, 1:2], raw[u % RING][:, ph.wide + 1:ph.wide + 2],
                                            WS, None, ALU.mult)
                nc.vector.scalar_tensor_tensor(
                    out=wl[:, u % RING, 0:ph.wide], in0=raw[u % RING][:, 0:ph.wide], scalar=WS,
                    in1=wh[:, u % RING, 0:ph.wide], op0=ALU.mult, op1=ALU.subtract).then_inc(ph.lo, 1)

            def x_low(i):
                for k in range(3):
                    dve.wait_ge(ph.xhi, i * 3 + k + 1)
                    src_ = bank(6 + k % 2).rearrange("p (c n) -> p c n", c=2)[:, :, 0:ph.n]
                    nc.vector.tensor_tensor(xTl[:, 2 * k:2 * k + 2, 0:ph.n], src_,
                                            xTh[:, 2 * k:2 * k + 2, 0:ph.n], ALU.subtract).then_inc(ph.xlo, 1)

            x_low(0)
            low(0, 0)
            low(0, 1)
            with dve.Fori(0, n_pass) as i:
                for u in range(ph.ic):
                    g = i * ph.ic + u
                    low(i, u + 2)
                    dve.wait_ge(ph.silu, g + 1)
                    s_ = sbuf[:, u % 2, 0:ph.n]
                    h_, l_ = hh[:, u % 2, 0:ph.n], hl[:, u % 2, 0:ph.n]
                    if ph.gated:
                        gate = bank(4 + u % 2)[:, 256:256 + ph.n]
                        t_ = tbuf[:, u % 2, 0:ph.n]
                        if ph.bias:
                            dve.wait_ge(ph.lo, g + 1 + RING)
                            nc.vector.scalar_tensor_tensor(out=t_, in0=gate, scalar=bsm[:, u % RING, 1:2],
                                                           in1=s_, op0=ALU.add, op1=ALU.mult).then_inc(ph.hseq, 1)
                        else:
                            nc.vector.tensor_tensor(t_, gate, s_, ALU.mult).then_inc(ph.hseq, 1)
                        dve.wait_ge(ph.hseq, g * 2 + 1)
                        nc.vector.tensor_scalar(h_, t_, 1.0 / WS, None, ALU.mult).then_inc(ph.hseq, 1)
                        dve.wait_ge(ph.hseq, g * 2 + 2)
                        nc.vector.scalar_tensor_tensor(out=l_, in0=t_, scalar=1.0 / WS, in1=h_, op0=ALU.mult,
                                                       op1=ALU.subtract).then_inc(ph.h, 1)
                    else:
                        nc.vector.tensor_copy(h_, s_).then_inc(ph.hseq, 1)
                        dve.wait_ge(ph.hseq, g + 1)
                        nc.vector.tensor_tensor(l_, s_, h_, ALU.subtract).then_inc(ph.h, 1)
                x_low(i + 1)
                dve.wait_ge(ph.down, (i + 1) * ph.ic + RING)
                dve.wait_ge(ph.yfree, i + 1)
                nc.vector.tensor_scalar(yrows[0:half, 1, :], ps[0:half, 2 * BANK:2 * BANK + D], 1.0 / WS, None,
                                        ALU.mult).then_inc(ph.yv, 1)

        def ffn_tensor(pe, ph, n_pass):
            half = ph.n // 2

            def three(out_, pairs, n_all, n, last=False):
                ins = None
                for k, (l_, r_) in enumerate(pairs):
                    ins = nc.tensor.matmul(out_, l_, r_, start=(n == 0 and k == 0),
                                           stop=(n == n_all - 1 and k == len(pairs) - 1))
                return ins

            def rows_transposed(k, wait):
                if wait is not None:
                    pe.wait_ge(ph.xlo, wait)
                for c in range(2):
                    for t in range(2):
                        ins = nc.tensor.transpose(
                            bank(6 + k % 2)[:, c * 256 + t * half:c * 256 + (t + 1) * half],
                            xrows[0:half, t, (2 * k + c) * 128:(2 * k + c + 1) * 128], ident[0:half, 0:half])
                ins.then_inc(ph.xt, 1)

            def up(i, u):
                g = i * ph.ic + u
                pe.wait_ge(ph.lo, g + 1 + RING)
                pe.wait_ge(ph.h, g + 1)
                for m in range(2 if ph.gated else 1):
                    for c in range(KC):
                        w0 = m * D + c * 128
                        ins = three(bank(4 + u % 2)[:, m * 256:m * 256 + ph.n],
                                    [(wh[:, u % RING, w0:w0 + 128], xTh[:, c, 0:ph.n]),
                                     (wh[:, u % RING, w0:w0 + 128], xTl[:, c, 0:ph.n]),
                                     (wl[:, u % RING, w0:w0 + 128], xTh[:, c, 0:ph.n])], KC, c)
                ins.then_inc(ph.up, 1)

            def down(i, u, first, last):
                g = i * ph.ic + u
                if first:
                    pe.wait_ge(ph.ya, i + 1)
                    pe.wait_ge(ph.yv, i + 1)
                pe.wait_ge(ph.h, g + 3)
                w0 = ph.wide - D
                for t in range(2):
                    for n0, n1 in ((0, BANK), (BANK, D)):
                        o = ps[0:half, 2 * t * BANK + n0:2 * t * BANK + n1]
                        hs, ls = (v[:, u % 2, t * half:(t + 1) * half] for v in (hh, hl))
                        for k, (l_, r_) in enumerate(((hs, wh), (hs, wl), (ls, wh))):
                            ins = nc.tensor.matmul(o, l_, r_[:, u % RING, w0 + n0:w0 + n1],
                                                   start=first and k == 0, stop=last and k == 2)
                ins.then_inc(ph.down, 1)

            pe.wait_ge(ph.xrows, 16)
            rows_transposed(0, None)
            rows_transposed(1, None)
            rows_transposed(2, 1)
            with pe.Fori(0, n_pass) as i:
                pe.wait_ge(ph.xlo, i * 3 + 3)
                for u in range(ph.ic):
                    up(i, u)
                    if u:
                        down(i, u - 1, u == 1, False)
                pe.wait_ge(ph.xrows, i * 16 + 32)
                rows_transposed(0, i * 3 + 3)
                rows_transposed(1, None)
                down(i, ph.ic - 1, False, True)
                rows_transposed(2, i * 3 + 4)

        @block.sync
        def _(sp):
            sp.dma_start(xres[:, :, :], x.rearrange("(t p) d -> p t d", p=P)).then_inc(s_x, 16)
            sp.dma_start(edges_i[:, 0, :], src.rearrange("(p c) -> p c", p=P)).then_inc(s_edge, 16)
            sp.dma_start(edges_i[:, 1, :], dst.rearrange("(p c) -> p c", p=P)).then_inc(s_edge, 16)
            sp.dma_start(wg[:, :, :], gnn_w.rearrange("(c p) n -> p c n", p=128)).then_inc(s_wg, 16)
            for v in range(2):
                sp.dma_start(vec[:, v, :], vecs[v, :].partition_broadcast(P)).then_inc(s_vec[v], 16)
            sp.dma_start(gates[:, 0, :, :], gate0.rearrange("(c p) e -> p c e", p=128)).then_inc(s_small, 16)
            sp.dma_start(gates[:, 1, :, :], gate1.rearrange("(c p) e -> p c e", p=128)).then_inc(s_small, 16)
            sp.dma_start(bout[:, :], bias_out).then_inc(s_small, 16)
            sp.wait_ge(s_const, C_ZERO)
            sp.dma_start(x_slots.rearrange("(t p) d -> p t d", p=128),
                         raw01[:, 0:1, 0:D].to_broadcast([128, NTAB * B // 128, D])).then_inc(s_zero, 16)
            sp.dma_start(x_shared.rearrange("(t p) d -> p t d", p=GS // 2),
                         raw01[0:GS // 2, 0:1, 0:D].to_broadcast([GS // 2, 2 * NG + 2, D])).then_inc(s_zero, 16)
            sp.dma_start(y_slots[NE * B:NPMAX * B, :].rearrange("(t p) d -> p t d", p=128),
                         raw01[:, 0:1, 0:D].to_broadcast([128, (NPMAX - NE) * B // 128, D])).then_inc(s_zero, 16)
            sp.wait_ge(s_zero, 48)

            sp.wait_ge(s_fence, ENGINES * F_GRAPH)
            sp.dma_start(vec[:, 0, :], vecs[2, :].partition_broadcast(P)).then_inc(s_vec[0], 16)
            sp.wait_ge(s_fence, ENGINES * F_MHA)
            sp.dma_start(vec[:, 1, :], vecs[3, :].partition_broadcast(P)).then_inc(s_vec[1], 16)
            sp.wait_ge(s_rowsok, R_XF0)
            sp.dma_start(x_shared[0:T, :].rearrange("(t p) d -> p t d", p=P), xf[:, :, :]).then_inc(s_lx, 16)
            ffn_sync(sp, ph_s, NG, False)
            sp.wait_ge(s_fence, ENGINES * F_SHARED)
            ffn_sync(sp, ph_0, passes(sp), True)
            sp.wait_ge(s_wh, 1)
            for q in range(2):
                for m in range(2):
                    sp.dma_start(wheads[64 * q:64 * q + 64, 128 * m + 64 * q:128 * m + 64 * q + 64],
                                 w_heads[:, m, :]).then_inc(s_al, 16)
            for a in range(2):
                sp.dma_start(alr[:, a, :], attn_lr[a, :].partition_broadcast(P)).then_inc(s_al, 16)
            sp.wait_ge(s_fence, ENGINES * F_ROUTE1)
            ffn_sync(sp, ph_1, passes(sp), True)
            sp.wait_ge(s_add, 2 * NT)
            sp.dma_start(out.rearrange("(t p) d -> p t d", p=P), xres[:, :, :]).then_inc(s_done, 16)
            sp.wait_ge(s_done, 16)

        @block.gpsimd
        def _(pool):
            for ph in (ph_s, ph_0, ph_1):
                pool.sem_inc(ph.hi, RING)
                pool.sem_inc(ph.lo, RING)
                pool.sem_inc(ph.down, RING)
                pool.sem_inc(ph.h, 2)
                pool.sem_inc(ph.ya, 1)
                pool.sem_inc(ph.yv, 1)
                pool.sem_inc(ph.yfree, 1)
            for s_ in (s_ge, s_exp, s_pT, s_pTe, s_pv, s_pvv):
                pool.sem_inc(s_, 2)
            pool.sem_inc(s_r, 2 * NT)
            pool.sem_inc(s_rm, 2)
            nc.gpsimd.iota(iota16[:, :], pattern=[[1, T]], base=0, channel_multiplier=0,
                           allow_small_or_imprecise_dtypes=True).then_inc(s_const, 1)
            nc.gpsimd.memset(raw01[:, 0, 0:D], 0.0).then_inc(s_const, 1)
            nc.gpsimd.memset(ident[:, :], 0.0).then_inc(s_const, 1)
            nc.gpsimd.memset(ones[:, :], 1.0).then_inc(s_const, 1)
            pool.wait_ge(s_const, 4)
            nc.gpsimd.affine_select(out=ident[:, :], in_=ident[:, :], compare_op=ALU.not_equal, fill=1.0, base=0,
                                    pattern=[[-1, 128]], channel_multiplier=1).then_inc(s_const, 1)
            nc.gpsimd.affine_select(out=tri[:, :], in_=ones[0:P, 0:P], compare_op=ALU.is_gt, fill=0.0, base=0,
                                    pattern=[[1, P]], channel_multiplier=-1).then_inc(s_const, 1)
            for k, (base, step) in enumerate(((0, 1), (0, B), ((NE - 1) * B, -B))):
                nc.gpsimd.iota(cst8[:, k, :, :], pattern=[[0, NT], [step, NE]], base=base, channel_multiplier=0,
                               allow_small_or_imprecise_dtypes=True).then_inc(s_const, 1)
            nc.gpsimd.iota(tabf[:, 0, :, :], pattern=[[1, NTAB], [0, NE]], base=-NE, channel_multiplier=0,
                           allow_small_or_imprecise_dtypes=True).then_inc(s_const, 1)
            nc.gpsimd.iota(tab1[:, 0, :], pattern=[[1, NTAB + 1]], base=0, channel_multiplier=0,
                           allow_small_or_imprecise_dtypes=True).then_inc(s_const, 1)

            def scatter(layer):
                pool.wait_ge(s_slot, layer + 1)
                pool.wait_ge(s_zero, 48)
                for k in range(2):
                    for t in range(NT):
                        pool.indirect_dma_start(
                            out=x_slots, out_offset=bass.IndirectOffsetOnAxis(ap=slots_i[:, k, t:t + 1], axis=0),
                            in_=xf[:, t, :], in_offset=None).then_inc(s_scat, 16)
                pool.wait_ge(s_scat, (layer + 1) * 16 * 2 * NT)

            def gather(layer):
                for t in range(NT):
                    s = t % 2
                    if t >= 2 or layer:
                        pool.wait_ge(s_add, layer * NT + t - 1 if t >= 2 else NT)
                    for k in range(2):
                        pool.indirect_dma_start(
                            out=rows[:, s, k, :], out_offset=None, in_=y_slots,
                            in_offset=bass.IndirectOffsetOnAxis(ap=slots_i[:, k, t:t + 1], axis=0)
                        ).then_inc(s_gat[s], 16)
                    if layer == 0:
                        pool.dma_start(rows[:, s, 2, :], y_shared[t * P:(t + 1) * P, :]).then_inc(s_gat[s], 16)

            fence(pool, F_GRAPH)
            fence(pool, F_MHA)
            pool.wait_ge(s_lx, 16)
            scatter(0)
            fence(pool, F_ROUTE0)
            ffn_pool(pool, ph_s, NG)
            fence(pool, F_SHARED)
            ffn_pool(pool, ph_0, passes(pool))
            fence(pool, F_EXP0)
            gather(0)
            fence(pool, F_LAYER0)
            with pool.Fori(0, H * NT // 10) as j:
                for m in range(10):
                    n = j * 10 + m
                    pool.wait_ge(s_ge, n + 3)
                    nc.gpsimd.tensor_tensor(prob[:, m % 2, :], prob[:, m % 2, :], cds[:, m % 5, :],
                                            ALU.mult).then_inc(s_pc, 1)
            fence(pool, F_GAT)
            scatter(1)
            fence(pool, F_ROUTE1)
            ffn_pool(pool, ph_1, passes(pool))
            fence(pool, F_EXP1)
            gather(1)

        @block.scalar
        def _(act):
            count = {"sq": 0, "tpa": 0}

            def root():
                count["sq"] += 1
                act.wait_ge(s_var, count["sq"])
                nc.scalar.activation(rs[:, 1, :], rs[:, 0, :], ACT.Sqrt).then_inc(s_sq, 1)

            def squares():
                count["sq"] += 1
                act.wait_ge(s_var, count["sq"])
                for t in range(NT):
                    ins = nc.scalar.activation(xf[:, t, :], z[:, t, :], ACT.Square, accum_out=rs[:, 0, t:t + 1])
                ins.then_inc(s_sq, 1)

            def transposed_out():
                for c in range(1, KC, 2):
                    act.wait_ge(s_tp, KC * (count["tpa"] // 3) + c + 1)
                    nc.scalar.activation(tD[:, c, :].rearrange("p (t n) -> p t n", t=NT),
                                         tiles5(bank(6, 2), 128), ACT.Copy).then_inc(s_tpa, 1)
                    count["tpa"] += 1

            root()
            transposed_out()
            for t in range(NT):
                act.wait_ge(s_hmm, t + 1)
                nc.scalar.activation(xf[:, t, :], ps[0:P, (t % 2) * 1024:(t % 2) * 1024 + D], ACT.Copy)\
                    .then_inc(s_hev, 1)
            act.wait_ge(s_cmm, EC)
            for i in range(NT):
                nc.scalar.activation(CT[:, i, 0:4 * P], ps[0:P, i * BANK:i * BANK + 4 * P], ACT.Copy)\
                    .then_inc(s_ct, 1)
            for i in range(NT):
                act.wait_ge(s_cT, i + 1)
                nc.scalar.activation(cds[:, i, :].rearrange("p (k n) -> p k n", k=NT),
                                     tiles5(bank(4 + 2 * (i % 2), 2), P), ACT.Copy).then_inc(s_cda, 1)
            root()
            fence(act, F_GRAPH)

            root()
            squares()
            root()
            transposed_out()
            with act.Fori(0, H // 2) as j:
                def exp(m):
                    n = j * 10 + m
                    act.wait_ge(s_mx, n + 1)
                    act.wait_ge(s_pT, n + 1)
                    nc.scalar.activation(prob[:, m % 2, :], ps[0:P, (m % 2) * 1024:(m % 2) * 1024 + T], ACT.Exp,
                                         bias=cols[:, m // 5, m % 5:m % 5 + 1],
                                         accum_out=cols[:, 2 + m // 5, m % 5:m % 5 + 1]).then_inc(s_exp, 1)

                def prob_out(m):
                    n = j * 10 + m
                    act.wait_ge(s_pT, n + 3)
                    act.wait_ge(s_pv, n + 1)
                    nc.scalar.activation(probT[:, m % 2, :, :], tiles5(bank(4 + 2 * (m % 2), 2), P), ACT.Copy)\
                        .then_inc(s_pTe, 1)

                for m in range(10):
                    exp(m)
                    if m:
                        prob_out(m - 1)
                prob_out(9)
            fence(act, F_MHA)

            def route():
                transposed_out()
                act.wait_ge(s_lge, count_route[0] + 1)
                nc.scalar.activation(sm[:, 1, :, :], sm[:, 0, :, :], ACT.Exp).then_inc(s_sel, 1)
                count_route[0] += 1

            count_route = [0]
            squares()
            root()
            route()
            fence(act, F_ROUTE0)
            ffn_scalar(act, ph_s, NG)
            fence(act, F_SHARED)
            ffn_scalar(act, ph_0, passes(act))
            fence(act, F_EXP0)
            fence(act, F_LAYER0)

            root()
            transposed_out()
            for n in range(NT * KC):
                act.wait_ge(s_ftv, n + 1)
                t, c = divmod(n, KC)
                nc.scalar.activation(z[:, t, 128 * c:128 * c + 128], bank(n % 4)[0:P, 128:256], ACT.Copy)\
                    .then_inc(s_fta, 1)
            with act.Fori(0, H // 2) as j:
                def clamp(m):
                    n = j * 10 + m
                    q = m // 5
                    if m % 5 == 0:
                        act.wait_ge(s_gb, j * 2 + q + 1)
                    act.wait_ge(s_rm, n + 1)
                    act.wait_ge(s_ge, n + 1)
                    ab = ps[0:P, q * 1024:q * 1024 + T]
                    nc.scalar.activation(relu1[:, m % 2, :], ab, ACT.Relu, scale=-1.0,
                                         bias=cols[:, 2 + q, m % 5:m % 5 + 1])
                    nc.scalar.activation(relu2[:, m % 2, :], ab, ACT.Relu, scale=-0.2,
                                         bias=cols[:, 4 + q, m % 5:m % 5 + 1]).then_inc(s_r, 1)

                def gexp(m):
                    n = j * 10 + m
                    act.wait_ge(s_rm, n + 3)
                    act.wait_ge(s_pT, N_MHA + n + 1)
                    nc.scalar.activation(prob[:, m % 2, :], relu1[:, m % 2, :], ACT.Exp, scale=-1.0)\
                        .then_inc(s_ge, 1)

                for m in range(10):
                    clamp(m)
                    if m:
                        gexp(m - 1)
                gexp(9)
            root()
            squares()
            root()
            route()
            fence(act, F_GAT)
            fence(act, F_ROUTE1)
            ffn_scalar(act, ph_1, passes(act))
            fence(act, F_EXP1)

        @block.vector
        def _(dve):
            count = {"v": 0, "sq": 0, "tp": 0, "route": 0}

            def step(ins):
                count["v"] += 1
                ins.then_inc(s_v, 1)
                dve.wait_ge(s_v, count["v"])

            def root_of(dst_):
                count["sq"] += 1
                dve.wait_ge(s_sq, count["sq"])
                step(nc.vector.reciprocal(dst_, rs[:, 1, :]))
                step(nc.vector.tensor_tensor(rs[:, 2, :], dst_, dst_, ALU.mult))
                step(nc.vector.tensor_tensor(rs[:, 2, :], rs[:, 2, :], rs[:, 0, :], ALU.mult))
                step(nc.vector.tensor_scalar(rs[:, 2, :], rs[:, 2, :], -0.5, 1.5, ALU.mult, ALU.add))
                step(nc.vector.tensor_tensor(dst_, dst_, rs[:, 2, :], ALU.mult))

            def layernorm():
                for t in range(NT):
                    for k in range(2):
                        ins = nc.vector.bn_stats(st[:, t, k, :], xres[:, t, k * D // 2:(k + 1) * D // 2])
                step(ins)
                for t in range(NT):
                    ins = nc.vector.bn_aggr(mv[:, t, :], st[:, t, :, :].rearrange("p a b -> p (a b)"))
                step(ins)
                nc.vector.tensor_scalar(rs[:, 0, :], mv[:, :, 1], 1e-5, None, ALU.add).then_inc(s_var, 1)
                root_of(rs[:, 3, :])
                for t in range(NT):
                    ins = nc.vector.tensor_scalar(z[:, t, :], xres[:, t, :], mv[:, t, 0:1], rs[:, 3, t:t + 1],
                                                  ALU.subtract, ALU.mult)
                step(ins)

            def rmsnorm(eps, v, n_vec):
                nc.vector.tensor_scalar(rs[:, 2, :], rs[:, 3, :], 1.0, None, ALU.mult).then_inc(s_var, 1)
                count["sq"] += 1
                dve.wait_ge(s_sq, count["sq"])
                nc.vector.tensor_scalar(rs[:, 0, :], rs[:, 0, :], 1.0 / D, eps, ALU.mult, ALU.add)\
                    .then_inc(s_var, 1)
                root_of(rs[:, 3, :])
                dve.wait_ge(s_vec[v], n_vec)
                for t in range(NT):
                    ins = nc.vector.scalar_tensor_tensor(out=xf[:, t, :], in0=z[:, t, :], scalar=rs[:, 3, t:t + 1],
                                                         in1=vec[:, v, :], op0=ALU.mult, op1=ALU.mult)
                ins.then_inc(s_rowsok, 1)

            def transposed_out():
                for c in range(0, KC, 2):
                    dve.wait_ge(s_tp, KC * (count["tp"] // 3) + c + 1)
                    nc.vector.tensor_copy(tD[:, c, :].rearrange("p (t n) -> p t n", t=NT),
                                          tiles5(bank(4, 2), 128)).then_inc(s_tpe, 1)
                    count["tp"] += 1

            dve.wait_ge(s_edge, 32)
            nc.vector.tensor_copy(edges_f[:, :, :], edges_i[:, :, :])
            dve.wait_ge(s_x, 16)
            layernorm()
            nc.vector.memset(a12[:, :, :, :], 0.0).then_inc(s_rowsok, 1)
            transposed_out()
            dve.wait_ge(s_vec[0], 16)
            for t in range(NT):
                ins = nc.vector.tensor_tensor(xres[:, t, :], xres[:, t, :], vec[:, 0, :], ALU.add)
            step(ins)
            dve.wait_ge(s_const, C_ALL)

            def one_hot(j, s, first=False):
                c = j * EU + s
                if not first:
                    dve.wait_ge(s_cmm, c - EU + 1)
                for a in range(2):
                    col = edges_f[:, a, bass.ds(c, 1)] if not isinstance(c, int) else edges_f[:, a, c:c + 1]
                    ins = nc.vector.tensor_scalar(hot[:, s, a, :], iota16[:, :], col, None, ALU.is_equal)
                ins.then_inc(s_hot, 1)

            for s in range(EU):
                one_hot(0, s, True)
            with dve.Fori(1, EC // EU) as j:
                for s in range(EU):
                    one_hot(j, s)
            dve.wait_ge(s_cmm, EC)
            nc.vector.tensor_copy(CT[:, 0:4, 4 * P:T], bank(5)[0:P, 0:4 * P].rearrange("p (t n) -> p t n", t=4))
            nc.vector.tensor_copy(CT[:, 4, 4 * P:T], bank(6)[0:P, 0:P]).then_inc(s_ctv, 1)
            for i in range(NT):
                dve.wait_ge(s_cda, i + 1)
                nc.vector.tensor_scalar(mask[:, i, :], cds[:, i, :], 0.0, NEG, ALU.is_equal, ALU.mult)
                ins = nc.vector.tensor_reduce(rs[:, 0, i:i + 1], cds[:, i, :], AX.X, ALU.add)
                ins.then_inc(s_cdv, 1)
            dve.wait_ge(s_cdv, NT)
            nc.vector.tensor_scalar(rs[:, 0, :], rs[:, 0, :], 1.0, None, ALU.add).then_inc(s_var, 1)
            root_of(dinv[:, :])
            dve.wait_ge(s_hev, NT)
            for t in range(NT):
                ins = nc.vector.tensor_scalar(xf[:, t, :], xf[:, t, :], dinv[:, t:t + 1], None, ALU.mult)
            count["v"] += 1
            ins.then_inc(s_v, 1)
            dve.wait_ge(s_v, count["v"])
            nc.vector.memset(wl[0:1, 0, 0:2], 0.0).then_inc(s_rowsok, 1)
            for i in range(NT):
                dve.wait_ge(s_agg, i + 1)
                step(nc.vector.tensor_tensor(z[:, i, :], ps[0:P, (i % 2) * 1024:(i % 2) * 1024 + D], xf[:, i, :],
                                             ALU.add))
                nc.vector.scalar_tensor_tensor(out=xres[:, i, :], in0=z[:, i, :], scalar=dinv[:, i:i + 1],
                                               in1=xres[:, i, :], op0=ALU.mult, op1=ALU.add).then_inc(s_aggv, 1)
            dve.wait_ge(s_aggv, NT)
            fence(dve, F_GRAPH)

            layernorm()
            rmsnorm(1e-5, 1, 16)
            transposed_out()
            with dve.Fori(0, H // 2) as j:
                def chunk(scale, s):
                    return nc.vector.tensor_scalar(cur[:, s, :], tD[:, bass.ds(j, 1), :].rearrange("p a n -> p (a n)"),
                                                   scale, None, ALU.mult)

                def top(m):
                    n = j * 10 + m
                    dve.wait_ge(s_s, n + 1)
                    nc.vector.tensor_reduce(cols[:, m // 5, m % 5:m % 5 + 1],
                                            ps[0:P, (m % 2) * 1024:(m % 2) * 1024 + T], AX.X, ALU.max,
                                            negate=True).then_inc(s_mx, 1)

                def fin(m):
                    n = j * 10 + m
                    q, t = divmod(m, 5)
                    dve.wait_ge(s_pv, n + 3)
                    nc.vector.reciprocal(cols[:, 4 + q, t:t + 1], cols[:, 2 + q, t:t + 1]).then_inc(s_rd, 1)
                    dve.wait_ge(s_rd, n + 1)
                    at = z[:, t, bass.ds(j * 128 + 64 * q, HD)]
                    nc.vector.scalar_tensor_tensor(out=at, in0=bank(5 + 2 * (m % 2))[0:P, 256:256 + HD],
                                                   scalar=cols[:, 4 + q, t:t + 1], in1=at, op0=ALU.mult,
                                                   op1=ALU.add).then_inc(s_pvv, 1)

                dve.wait_ge(s_tpa, 2 * 3)
                dve.wait_ge(s_tpe, 2 * 3)
                chunk(1.0, 0)
                chunk(HD ** -0.5, 1).then_inc(s_cur, 1)
                for m in range(10):
                    top(m)
                    if m >= 2:
                        fin(m - 2)
                fin(8)
                fin(9)
            dve.wait_ge(s_pvv, N_MHA + 2)
            fence(dve, F_MHA)

            def route(layer):
                transposed_out()
                bc = lambda a: a.unsqueeze(2).to_broadcast([P, NT, NE])
                per_t = lambda a: a.unsqueeze(1).to_broadcast([P, NT, NE])
                tmp, p, oh, sel, cand = sm[:, 0], sm[:, 1], [sm[:, 2], sm[:, 3]], sm[:, 4], sm[:, 5]
                p2, slot = sm[:, 6], sm[:, 7]
                top, best = rs[:, 0, :], rs[:, 1, :]
                dve.wait_ge(s_lg, layer + 1)
                lg = bank(0)[0:P, 0:NT * NE].rearrange("p (t e) -> p t e", t=NT)
                step(nc.vector.tensor_reduce(top, lg, AX.X, ALU.max))
                nc.vector.tensor_tensor(tmp, lg, bc(top), ALU.subtract).then_inc(s_lge, 1)
                dve.wait_ge(s_sel, layer + 1)
                step(nc.vector.tensor_reduce(top, p, AX.X, ALU.add))
                step(nc.vector.reciprocal(top, top))
                step(nc.vector.tensor_tensor(p, p, bc(top), ALU.mult))
                for k in range(2):
                    of = p if k == 0 else p2
                    step(nc.vector.tensor_reduce(wts[:, k, :], of, AX.X, ALU.max))
                    step(nc.vector.tensor_tensor(cand, of, bc(wts[:, k, :]), ALU.is_equal))
                    step(nc.vector.tensor_scalar(cand, cand, -float(NE), float(NE), ALU.mult, ALU.add))
                    step(nc.vector.tensor_tensor(cand, cand, cst8[:, 0], ALU.add))
                    step(nc.vector.tensor_reduce(best, cand, AX.X, ALU.min))
                    step(nc.vector.tensor_tensor(oh[k], cst8[:, 0], bc(best), ALU.is_equal))
                    if k == 0:
                        step(nc.vector.scalar_tensor_tensor(out=p2, in0=oh[0], scalar=-2.0, in1=p, op0=ALU.mult,
                                                            op1=ALU.add))
                nc.vector.tensor_tensor(sel, oh[0], oh[1], ALU.add).then_inc(s_rd, 1)
                if layer == 0:
                    step(nc.vector.tensor_scalar(wts[:, :, :], wts[:, :, :], 1e-7, None, ALU.max))
                    step(nc.vector.memset(cmb[:, :, :], 1.0))
                    step(nc.vector.tensor_tensor(tmp, oh[0], bc(wts[:, 0, :]), ALU.mult))
                    step(nc.vector.tensor_tensor(cand, oh[1], bc(wts[:, 1, :]), ALU.mult))
                    nc.vector.tensor_tensor(cmb[:, :, 0:NE], tmp, cand, ALU.add).then_inc(s_cm, 1)
                dve.wait_ge(s_rk, layer + 1)
                rank = bank(0)[0:P, 64:64 + NT * NE].rearrange("p (t e) -> p t e", t=NT)
                step(nc.vector.tensor_copy(s8[:, 0, :], bank(0)[0:P, 128:128 + NE]))
                step(nc.vector.tensor_scalar(s8[:, 1, :], s8[:, 0, :], float(B), None, ALU.is_gt))
                step(nc.vector.scalar_tensor_tensor(out=s8[:, 1, :], in0=s8[:, 0, :], scalar=2.0 * B, in1=s8[:, 1, :],
                                                    op0=ALU.is_gt, op1=ALU.add))
                at = 1
                for k, d in enumerate((1, 2, 4)):
                    step(nc.vector.tensor_copy(s8[:, 2 + k, :], s8[:, at, :]))
                    step(nc.vector.tensor_tensor(s8[:, 2 + k, d:NE], s8[:, at, d:NE], s8[:, at, 0:NE - d], ALU.add))
                    at = 2 + k
                step(nc.vector.tensor_tensor(s8[:, 5, :], s8[:, at, :], s8[:, 1, :], ALU.subtract))
                step(nc.vector.scalar_tensor_tensor(out=s8[:, 6, :], in0=s8[:, 5, :], scalar=float(B),
                                                    in1=cst8[:, 2, 0, :], op0=ALU.mult, op1=ALU.add))
                step(nc.vector.tensor_scalar(cand, rank, float(B), None, ALU.is_ge))
                step(nc.vector.tensor_tensor(cand, cand, per_t(s8[:, 6, :]), ALU.mult))
                step(nc.vector.tensor_tensor(slot, rank, cst8[:, 1], ALU.add))
                step(nc.vector.tensor_tensor(slot, slot, cand, ALU.add))
                for k in range(2):
                    step(nc.vector.tensor_tensor(cand, slot, oh[k], ALU.mult))
                    step(nc.vector.tensor_reduce(slots_f[:, k, :], cand, AX.X, ALU.add))
                step(nc.vector.tensor_copy(slots_i[:, :, :], slots_f[:, :, :]))
                step(nc.vector.tensor_tensor(tabf[:, 1, :, :], s8[0:1, at:at + 1, :].to_broadcast([1, NTAB, NE]),
                                             tabf[:, 0, :, :], ALU.is_le))
                step(nc.vector.tensor_reduce(tab1[:, 1, 0:NTAB], tabf[:, 1, :, :], AX.X, ALU.add))
                step(nc.vector.tensor_scalar(tab1[:, 1, 0:NTAB], tab1[:, 1, 0:NTAB], float(NE - 1), None, ALU.min))
                step(nc.vector.tensor_scalar(tab1[:, 2, :], tab1[:, 0, :], float(NE), None, ALU.is_lt))
                step(nc.vector.tensor_tensor(tab1[:, 2, :], tab1[:, 2, :], tab1[:, 0, :], ALU.mult))
                step(nc.vector.tensor_tensor(tab1[:, 1, 0:NTAB], tab1[:, 1, 0:NTAB], tab1[:, 2, 0:NTAB], ALU.add))
                step(nc.vector.tensor_scalar(tab1[:, 1, NTAB:NTAB + 1], s8[0:1, at, NE - 1:NE], float(NE), None,
                                             ALU.add))
                step(nc.vector.tensor_copy(tabi[:, 0, :], tab1[:, 1, :]))
                nc.vector.memset(wl[0:1, 0, 0:2], 0.0).then_inc(s_slot, 1)

            def combine(layer):
                if layer == 0:
                    dve.wait_ge(s_cmT, 1)
                    nc.vector.tensor_copy(cmbT[:, :].rearrange("e (t n) -> e t n", t=NT),
                                          tiles5(bank(0, 2), NE + 1)).then_inc(s_cmTv, 1)
                for t in range(NT):
                    s = t % 2
                    n_rows = 16 * (3 if layer == 0 else 2)
                    before = 0 if layer == 0 else 48 * (3 if s == 0 else 2)
                    dve.wait_ge(s_gat[s], before + n_rows * (t // 2 + 1))
                    if layer == 0:
                        dve.wait_ge(s_bo, t + 1)
                        step(nc.vector.tensor_tensor(z[:, t, :], z[:, t, :],
                                                     ps[0:P, (1 + s) * 1024:(1 + s) * 1024 + D], ALU.add))
                        step(nc.vector.tensor_tensor(z[:, t, :], z[:, t, :], rows[:, s, 2, :], ALU.add))
                    for k in range(2):
                        step(nc.vector.scalar_tensor_tensor(out=z[:, t, :], in0=rows[:, s, k, :],
                                                            scalar=wts[:, k, t:t + 1], in1=z[:, t, :],
                                                            op0=ALU.mult, op1=ALU.add))
                    nc.vector.tensor_tensor(xres[:, t, :], xres[:, t, :], z[:, t, :], ALU.add).then_inc(s_add, 1)

            rmsnorm(1e-5, 0, 32)
            dve.wait_ge(s_rowsok, R_XF0)
            dve.wait_ge(s_small, 48)
            route(0)
            fence(dve, F_ROUTE0)
            ffn_vector(dve, ph_s, NG)
            fence(dve, F_SHARED)
            ffn_vector(dve, ph_0, passes(dve))
            fence(dve, F_EXP0)
            combine(0)
            dve.wait_ge(s_add, NT)
            step(nc.vector.memset(wheads, 0.0))
            nc.vector.memset(wl[0:1, 0, 0:2], 0.0).then_inc(s_wh, 1)
            fence(dve, F_LAYER0)

            layernorm()
            nc.vector.memset(wl[0:1, 0, 0:2], 0.0).then_inc(s_rowsok, 1)
            transposed_out()
            for n in range(NT * KC):
                dve.wait_ge(s_ft, n + 1)
                t, c = divmod(n, KC)
                nc.vector.tensor_copy(xf[:, t, 128 * c:128 * c + 128], bank(n % 4)[0:P, 0:128]).then_inc(s_ftv, 1)
            dve.wait_ge(s_ftv, NT * KC)
            dve.wait_ge(s_al, 16 * 6)
            for t in range(NT):
                step(nc.vector.tensor_tensor(prod, xf[:, t:t + 1, :].to_broadcast([P, 2, D]), alr, ALU.mult))
                step(nc.vector.tensor_reduce(a12[:, :, t, 0:H],
                                             prod.rearrange("p a (h e) -> p a h e", h=H), AX.X, ALU.add))
            nc.vector.memset(wl[0:1, 0, 0:2], 0.0).then_inc(s_am, 1)
            dve.wait_ge(s_aT, 1)
            step(nc.vector.tensor_copy(a1T.rearrange("h (t n) -> h t n", t=NT), tiles5(bank(4, 2), H)))

            def own_row(h, q):
                col = ident[0:H, bass.ds(h, 1)] if not isinstance(h, int) else ident[0:H, h:h + 1]
                nc.vector.tensor_scalar(a1m[:, q, :], a1T, col, None, ALU.mult).then_inc(s_am, 1)

            def edge_top(h, q, t):
                nc.vector.tensor_tensor_reduce(out=junk, in0=ps[0:P, q * 1024:q * 1024 + T], in1=mask[:, t, :],
                                               scale=1.0, scalar=-3e38, op0=ALU.add, op1=ALU.max,
                                               accum_out=cols[:, q, t:t + 1]).then_inc(s_gm, 1)

            def shifts(h, q):
                a2 = a12[:, 1, :, bass.ds(h, 1)] if not isinstance(h, int) else a12[:, 1, :, h:h + 1]
                a2 = a2.rearrange("p t a -> p (t a)")
                dve.wait_ge(s_gm, h * NT + NT)
                nc.vector.tensor_tensor(cols[:, 8, :], cols[:, q, :], a2, ALU.add).then_inc(s_gseq, 1)
                dve.wait_ge(s_gseq, h * 3 + 1)
                nc.vector.scalar_tensor_tensor(out=cols[:, 9, :], in0=cols[:, 8, :], scalar=0.2, in1=cols[:, 8, :],
                                               op0=ALU.mult, op1=ALU.max).then_inc(s_gseq, 1)
                dve.wait_ge(s_gseq, h * 3 + 2)
                nc.vector.tensor_tensor(cols[:, 2 + q, :], cols[:, 9, :], a2, ALU.subtract).then_inc(s_gseq, 1)
                nc.vector.scalar_tensor_tensor(out=cols[:, 4 + q, :], in0=a2, scalar=-0.2, in1=cols[:, 9, :],
                                               op0=ALU.mult, op1=ALU.add).then_inc(s_gb, 1)

            own_row(0, 0)
            dve.wait_ge(s_ab, 1)
            for t in range(NT):
                if t:
                    dve.wait_ge(s_gm, t)
                edge_top(0, 0, t)
            shifts(0, 0)
            with dve.Fori(0, H // 2) as j:
                def merge(m):
                    n = j * 10 + m
                    dve.wait_ge(s_r, n + 1 + 2 * NT)
                    nc.vector.tensor_tensor(relu1[:, m % 2, :], relu1[:, m % 2, :], relu2[:, m % 2, :],
                                            ALU.min).then_inc(s_rm, 1)

                def prob_out(m):
                    n = j * 10 + m
                    dve.wait_ge(s_pT, N_MHA + n + 3)
                    dve.wait_ge(s_pv, N_MHA + n + 1)
                    nc.vector.tensor_copy(probT[:, m % 2, :, :], tiles5(bank(4 + 2 * (m % 2), 2), P))\
                        .then_inc(s_pTe, 1)

                def fin(m):
                    n = j * 10 + m
                    q, t = divmod(m, 5)
                    dve.wait_ge(s_pv, N_MHA + n + 3)
                    nc.vector.tensor_scalar(cols[:, 10 + q, t:t + 1],
                                            bank(5 + 2 * (m % 2))[0:P, 256 + HD:257 + HD], 1e-37, None, ALU.max)\
                        .then_inc(s_rd, 1)
                    dve.wait_ge(s_rd, N_RD + n * 2 + 1)
                    nc.vector.reciprocal(cols[:, 10 + q, t:t + 1], cols[:, 10 + q, t:t + 1]).then_inc(s_rd, 1)
                    dve.wait_ge(s_rd, N_RD + n * 2 + 2)
                    at = z[:, t, bass.ds(j * 128 + 64 * q, HD)]
                    nc.vector.scalar_tensor_tensor(out=at, in0=bank(5 + 2 * (m % 2))[0:P, 256:256 + HD],
                                                   scalar=cols[:, 10 + q, t:t + 1], in1=at, op0=ALU.mult,
                                                   op1=ALU.add).then_inc(s_pvv, 1)

                for m in range(13):
                    if m % 5 == 0 and m < 10:
                        own_row(j * 2 + m // 5 + 1, 1 - m // 5)
                    if 2 <= m < 12:
                        prob_out(m - 2)
                    if 3 <= m:
                        fin(m - 3)
                    if m < 10:
                        q, t = divmod(m, 5)
                        h = j * 2 + q + 1
                        if t == 0:
                            dve.wait_ge(s_ab, h + 1)
                        dve.wait_ge(s_gm, h * NT + t)
                        merge(m)
                        edge_top(h, 1 - q, t)
                        if t == NT - 1:
                            shifts(h, 1 - q)
            dve.wait_ge(s_pvv, 2 * N_MHA + 2)
            for t in range(NT):
                ins = nc.vector.scalar_tensor_tensor(out=xres[:, t, :], in0=z[:, t, :], scalar=0.0,
                                                     in1=xres[:, t, :], op0=ALU.max, op1=ALU.add)
            step(ins)
            layernorm()
            rmsnorm(1e-6, 1, 32)
            dve.wait_ge(s_rowsok, R_XF1)
            route(1)
            fence(dve, F_GAT)
            fence(dve, F_ROUTE1)
            ffn_vector(dve, ph_1, passes(dve))
            fence(dve, F_EXP1)
            combine(1)

        @block.tensor
        def _(pe):
            count = {"tp": 0}

            def transpose_rows(rows_):
                for c in range(KC):
                    k = count["tp"]
                    done = s_tpe if c % 2 == 0 else s_tpa
                    if k >= 2:
                        pe.wait_ge(done, (k - c) // 2 + c // 2)
                    o = bank(4 + 2 * (c % 2), 2)
                    for t in range(NT):
                        ins = nc.tensor.transpose(o[:, t * 128:t * 128 + P], rows_[:, t, c * 128:(c + 1) * 128],
                                                  ident[0:P, 0:P])
                    ins.then_inc(s_tp, 1)
                    count["tp"] += 1

            def transposed(k):
                pe.wait_ge(s_tpe, 3 * k)
                pe.wait_ge(s_tpa, 3 * k)

            pe.wait_ge(s_const, C_ALL)
            pe.wait_ge(s_rowsok, R_Z0)
            transpose_rows(z)
            transposed(1)
            pe.wait_ge(s_wg, 16)
            for t in range(NT):
                if t >= 2:
                    pe.wait_ge(s_hev, t - 1)
                for n0, n1 in ((0, BANK), (BANK, D)):
                    for c in range(KC):
                        ins = nc.tensor.matmul(ps[0:P, (t % 2) * 1024 + n0:(t % 2) * 1024 + n1],
                                               tD[:, c, t * P:(t + 1) * P], wg[:, c, n0:n1],
                                               start=c == 0, stop=c == KC - 1)
                ins.then_inc(s_hmm, 1)

            def edge_chunk(j, s, first, last):
                pe.wait_ge(s_hot, j * EU + s + 1)
                for i in range(NT):
                    src_ = hot[:, s, 0, i * P:(i + 1) * P]
                    nc.tensor.matmul(ps[0:P, i * BANK:i * BANK + 4 * P], src_, hot[:, s, 1, 0:4 * P],
                                     start=first, stop=last, skip_group_check=True)
                    at = 5 * BANK + i * P if i < 4 else 6 * BANK
                    ins = nc.tensor.matmul(ps[0:P, at:at + P], src_, hot[:, s, 1, 4 * P:T],
                                           start=first and i in (0, 4), stop=last, skip_group_check=True)
                ins.then_inc(s_cmm, 1)

            pe.wait_ge(s_hev, NT)
            for s in range(EU):
                edge_chunk(0, s, s == 0, False)
            with pe.Fori(1, EC // EU - 1) as j:
                for s in range(EU):
                    edge_chunk(j, s, False, False)
            for s in range(EU):
                edge_chunk(EC // EU - 1, s, False, s == EU - 1)
            pe.wait_ge(s_ct, NT)
            pe.wait_ge(s_ctv, 1)
            for i in range(NT):
                if i >= 2:
                    pe.wait_ge(s_cda, i - 1)
                o = bank(4 + 2 * (i % 2), 2)
                for k in range(NT):
                    ins = nc.tensor.transpose(o[0:P, k * 128:k * 128 + P], CT[:, k, i * P:(i + 1) * P],
                                              ident[0:P, 0:P])
                ins.then_inc(s_cT, 1)
            pe.wait_ge(s_rowsok, R_HS)
            for i in range(NT):
                if i >= 2:
                    pe.wait_ge(s_aggv, i - 1)
                for n0, n1 in ((0, BANK), (BANK, D)):
                    for k in range(NT):
                        ins = nc.tensor.matmul(ps[0:P, (i % 2) * 1024 + n0:(i % 2) * 1024 + n1],
                                               CT[:, k, i * P:(i + 1) * P], xf[:, k, n0:n1],
                                               start=k == 0, stop=k == NT - 1)
                ins.then_inc(s_agg, 1)
            fence(pe, F_GRAPH)

            def weighted_rows(m, n, col, base):
                pe.wait_ge(s_pTe, base + n + 3)
                for k in range(NT):
                    ins = nc.tensor.matmul(bank(5 + 2 * (m % 2))[0:P, 256:256 + HD], probT[:, m % 2, k, :],
                                           xf[:, k, bass.ds(col, HD)], start=k == 0, stop=k == NT - 1)
                if base:
                    for k in range(NT):
                        ins = nc.tensor.matmul(bank(5 + 2 * (m % 2))[0:P, 256 + HD:257 + HD], probT[:, m % 2, k, :],
                                               ones[0:P, 0:1], start=k == 0, stop=k == NT - 1)
                ins.then_inc(s_pv, 1)

            def prob_transposed(m, n, base):
                pe.wait_ge(s_pTe, base + n + 1)
                pe.wait_ge(s_pvv, base + n + 1)
                o = bank(4 + 2 * (m % 2), 2)
                for k in range(NT):
                    ins = nc.tensor.transpose(o[0:P, k * 128:k * 128 + P], prob[:, m % 2, k * P:(k + 1) * P],
                                              ident[0:P, 0:P])
                ins.then_inc(s_pT, 1)

            pe.wait_ge(s_rowsok, R_XN0)
            transpose_rows(xf)
            with pe.Fori(0, H // 2) as j:
                def scores(m):
                    n = j * 10 + m
                    q, t = divmod(m, 5)
                    pe.wait_ge(s_exp, n + 1)
                    for n0, n1 in ((0, BANK), (BANK, T)):
                        ins = nc.tensor.matmul(ps[0:P, (m % 2) * 1024 + n0:(m % 2) * 1024 + n1],
                                               cur[64 * q:64 * q + 64, 1, t * P:(t + 1) * P],
                                               cur[64 * q:64 * q + 64, 0, n0:n1], start=True, stop=True)
                    ins.then_inc(s_s, 1)

                pe.wait_ge(s_cur, j + 1)
                scores(0)
                for m in range(10):
                    if m < 9:
                        scores(m + 1)
                    pe.wait_ge(s_exp, j * 10 + m + 3)
                    prob_transposed(m, j * 10 + m, 0)
                    if m:
                        weighted_rows(m - 1, j * 10 + m - 1, j * 128 + 64 * ((m - 1) // 5), 0)
                weighted_rows(9, j * 10 + 9, j * 128 + 64, 0)
            fence(pe, F_MHA)

            def route(layer, n_transposed, ok):
                pe.wait_ge(s_rowsok, ok)
                transpose_rows(xf)
                transposed(n_transposed)
                pe.wait_ge(s_small, 48)
                for t in range(NT):
                    for c in range(KC):
                        ins = nc.tensor.matmul(bank(0)[0:P, t * NE:(t + 1) * NE], tD[:, c, t * P:(t + 1) * P],
                                               gates[:, layer, c, :], start=c == 0, stop=c == KC - 1)
                ins.then_inc(s_lg, 1)
                pe.wait_ge(s_rd, 60 + 1 if layer == 0 else N_RD + 2 * N_MHA + 1)
                for t in range(NT + 1):
                    o = bank(0)[0:P, 64 + t * NE:64 + (t + 1) * NE] if t < NT else bank(0)[0:P, 128:128 + NE]
                    for k in range(min(t, NT)):
                        ins = nc.tensor.matmul(o, ones[0:P, 0:P], sm[:, 4, k, :], start=k == 0,
                                               stop=t == NT and k == NT - 1)
                    if t < NT:
                        ins = nc.tensor.matmul(o, tri[:, :], sm[:, 4, t, :], start=t == 0, stop=True)
                ins.then_inc(s_rk, 1)

            route(0, 3, R_XF0)
            fence(pe, F_ROUTE0)
            ffn_tensor(pe, ph_s, NG)
            fence(pe, F_SHARED)
            ffn_tensor(pe, ph_0, passes(pe))
            fence(pe, F_EXP0)
            pe.wait_ge(s_cm, 1)
            for t in range(NT):
                ins = nc.tensor.transpose(bank(0, 2)[0:NE + 1, t * 128:t * 128 + P], cmb[:, t, :], ident[0:P, 0:P])
            ins.then_inc(s_cmT, 1)
            pe.wait_ge(s_cmTv, 1)
            for t in range(NT):
                if t >= 2:
                    pe.wait_ge(s_add, t - 1)
                for n0, n1 in ((0, BANK), (BANK, D)):
                    ins = nc.tensor.matmul(ps[0:P, (1 + t % 2) * 1024 + n0:(1 + t % 2) * 1024 + n1],
                                           cmbT[:, t * P:(t + 1) * P], bout[:, n0:n1], start=True, stop=True)
                ins.then_inc(s_bo, 1)
            fence(pe, F_LAYER0)

            pe.wait_ge(s_rowsok, R_Z1)
            transpose_rows(z)
            transposed(4)
            pe.wait_ge(s_al, 16 * 6)
            for n in range(NT * KC):
                t, c = divmod(n, KC)
                if n >= 4:
                    pe.wait_ge(s_fta, n - 3)
                nc.tensor.matmul(bank(n % 4)[0:P, 0:256], tD[:, c, t * P:(t + 1) * P], wheads,
                                 start=True, stop=True).then_inc(s_ft, 1)
            pe.wait_ge(s_am, 1)
            for t in range(NT):
                ins = nc.tensor.transpose(bank(4, 2)[0:H, t * 128:t * 128 + P], a12[:, 0, t, 0:H],
                                          ident[0:P, 0:P])
            ins.then_inc(s_aT, 1)

            def source_term(h, q):
                pe.wait_ge(s_am, h + 2)
                pe.wait_ge(s_r, h * NT + NT)
                for n0, n1 in ((0, BANK), (BANK, T)):
                    ins = nc.tensor.matmul(ps[0:P, q * 1024 + n0:q * 1024 + n1], ones[0:H, 0:P],
                                           a1m[:, q, n0:n1], start=True, stop=True)
                ins.then_inc(s_ab, 1)

            pe.wait_ge(s_fta, NT * KC)
            source_term(0, 0)
            with pe.Fori(0, H // 2) as j:
                for m in range(10):
                    q, t = divmod(m, 5)
                    if t == 0:
                        source_term(j * 2 + q + 1, 1 - q)
                    pe.wait_ge(s_pc, j * 10 + m + 1)
                    prob_transposed(m, j * 10 + m, N_MHA)
                    if m:
                        weighted_rows(m - 1, j * 10 + m - 1, j * 128 + 64 * ((m - 1) // 5), N_MHA)
                weighted_rows(9, j * 10 + 9, j * 128 + 64, N_MHA)
            route(1, 5, R_XF1)
            fence(pe, F_GAT)
            fence(pe, F_ROUTE1)
            ffn_tensor(pe, ph_1, passes(pe))
            fence(pe, F_EXP1)


def kernel(x, src, dst, L0_gnn_W, L0_gnn_b, L0_ffn_norm1_w, L0_ffn_norm3_w, L0_ffn_gate_w, L0_ffn_w1, L0_ffn_b1,
           L0_ffn_w2, L0_ffn_b2, L0_ffn_w3, L0_ffn_b3, L0_ffn_fc1_w, L0_ffn_fc1_b, L0_ffn_fc2_w, L0_ffn_fc2_b,
           L1_gnn_W_fc, L1_gnn_attn_l, L1_gnn_attn_r, L1_gnn_W_res, L1_ffn_norm_w, L1_ffn_router_w,
           L1_ffn_gate_w, L1_ffn_up_w, L1_ffn_down_w):
    import numpy as np
    import concourse.bacc as bacc
    from concourse.bass_utils import run_bass_kernel_spmd

    def up_cols(w):
        w = np.asarray(w)
        lead = w.shape[:-2]
        w = w.reshape(*lead, w.shape[-2] // 128, 128, KC, 128)
        n = len(lead)
        w = w.transpose(*range(n), n, n + 3, n + 2, n + 1)
        return w.reshape(*w.shape[:n + 2], D)

    def down_rows(w):
        w = np.asarray(w)
        w = np.swapaxes(w, -1, -2)
        return w.reshape(*w.shape[:-2], w.shape[-2] // 128, 128, D)

    def bias_col(b):
        b = np.asarray(b)
        return b.reshape(*b.shape[:-1], b.shape[-1] // 128, 128, 1)

    b1s = bias_col(L0_ffn_fc1_b)
    arrays = {
        "x": np.asarray(x), "src": np.asarray(src), "dst": np.asarray(dst), "gnn_w": np.asarray(L0_gnn_W),
        "vecs": np.stack([np.asarray(v) for v in (L0_gnn_b, L0_ffn_norm1_w, L0_ffn_norm3_w, L1_ffn_norm_w)]),
        "gate0": np.asarray(L0_ffn_gate_w).T, "gate1": np.asarray(L1_ffn_router_w).T,
        "units0": np.concatenate([up_cols(L0_ffn_w1), up_cols(L0_ffn_w3), down_rows(L0_ffn_w2),
                                  bias_col(L0_ffn_b1), bias_col(L0_ffn_b3)], -1),
        "units_s": np.concatenate([up_cols(L0_ffn_fc1_w), down_rows(L0_ffn_fc2_w), b1s, b1s], -1),
        "units1": np.concatenate([up_cols(L1_ffn_gate_w), up_cols(L1_ffn_up_w), down_rows(L1_ffn_down_w)], -1),
        "bias_out": np.concatenate([np.asarray(L0_ffn_b2), np.asarray(L0_ffn_fc2_b)[None]], 0),
        "w_heads": np.stack([np.asarray(L1_gnn_W_fc).T, np.asarray(L1_gnn_W_res).T], 1),
        "attn_lr": np.stack([np.asarray(L1_gnn_attn_l).reshape(D), np.asarray(L1_gnn_attn_r).reshape(D)]),
    }
    arrays = {f"in_{k}": np.ascontiguousarray(v) for k, v in arrays.items()}
    nc = bacc.Bacc("TRN2", target_bir_lowering=False, num_devices=1)
    args = [nc.dram_tensor(k, v.shape, mybir.dt.from_np(v.dtype), kind="ExternalInput").ap()
            for k, v in arrays.items()]
    result = nc.dram_tensor("out_0", (T, D), F32, kind="ExternalOutput").ap()
    bass_gnn_moe_stack(nc, *args, result)
    r = run_bass_kernel_spmd(nc, [arrays], core_ids=[0])
    return r.results[0]["out_0"]
```

```python
import concourse.bass as bass
from concourse import mybir
from contextlib import ExitStack

F32 = mybir.dt.float32
F16 = mybir.dt.float16
BF16 = mybir.dt.bfloat16
I32 = mybir.dt.int32
ALU = mybir.AluOpType
ACT = mybir.ActivationFunctionType
AX = mybir.AxisListType

T, D, H = 625, 768, 12
HD = D // H
EDGES = 20625
NE = 8
I0, IS, I1 = 1024, 2048, 1536

P, NT = 125, 5
KC = D // 128
EC = EDGES // P
EU = 3
B = 176
NPMAX = NE + (2 * T - NE) // B
NTAB = NPMAX + 1
GS = 214
NG = 3
RING = 4
WS = 64.0
NEG = -1e30
BANK = 512

C_ZERO, C_ALL = 2, 11
F_GRAPH, F_MHA, F_ROUTE0, F_SHARED, F_EXP0, F_LAYER0, F_GAT, F_ROUTE1, F_EXP1 = range(1, 10)
R_Z0, R_HS, R_XN0, R_XF0, R_Z1, R_XF1 = range(1, 7)
N_ATT = H * NT
N_RD = 1


class Phase:

    def __init__(self, sem, name, ic, gated, bias, n, rows):
        self.ic, self.gated, self.bias, self.n, self.rows = ic, gated, bias, n, rows
        self.wide = D * (3 if gated else 2)
        self.cols = self.wide + (2 if bias else 0)
        self.raw = [sem(f"{name}_unit_loaded{r}") for r in range(RING)]
        self.hi = sem(f"{name}_unit_high")
        self.lo = sem(f"{name}_unit_low")
        self.up = sem(f"{name}_up_done")
        self.silu = sem(f"{name}_silu_done")
        self.hseq = sem(f"{name}_hidden_steps")
        self.h = sem(f"{name}_hidden_split")
        self.down = sem(f"{name}_down_done")
        self.xrows = sem(f"{name}_rows_loaded")
        self.xt = sem(f"{name}_rows_transposed")
        self.xhi = sem(f"{name}_x_high")
        self.xlo = sem(f"{name}_x_low")
        self.ya = sem(f"{name}_out_tile0")
        self.yv = sem(f"{name}_out_tile1")
        self.stored = sem(f"{name}_out_stored")
        self.yfree = sem(f"{name}_out_free")


def bass_gnn_moe_stack(nc, x, src, dst, gnn_w, vecs, gate0, gate1, units0, units_s, units1,
                       bias_out, w_heads, attn_lr, out):
    ctx = ExitStack()
    with ctx:
        def sb(name, shape, dt=F32):
            return ctx.enter_context(nc.sbuf_tensor(name, shape, dt))

        def sem(name):
            return ctx.enter_context(nc.semaphore(name))

        x_slots = nc.dram_tensor("x_slots", [NTAB * B, D], F32, kind="Internal").ap()
        y_slots = nc.dram_tensor("y_slots", [NPMAX * B, D], F32, kind="Internal").ap()
        x_shared = nc.dram_tensor("x_shared", [(NG + 1) * GS, D], F32, kind="Internal").ap()
        y_shared = nc.dram_tensor("y_shared", [NG * GS, D], F32, kind="Internal").ap()

        xres = sb("xres", [P, NT, D])
        z = sb("z", [P, NT, D])
        xfb = sb("xfb", [P, NT, H * (HD + 1)])
        big = sb("big", [128, 7500])
        ext = sb("ext", [128, 6500])
        cds = sb("cds", [P, NT, T])
        mask = sb("mask", [P, NT, T], BF16)
        raw01 = sb("raw01", [128, 2, 3 * D + 2])
        wh = sb("wh", [128, RING, 3 * D], F16)
        wl = sb("wl", [128, RING, 3 * D], F16)
        ident = sb("ident", [128, 128])
        ones = sb("ones", [128, 128])
        tri = sb("tri", [P, P])
        vec = sb("vec", [P, 2, D])
        gates = sb("gates", [128, 2, KC, NE])
        bout = sb("bout", [NE + 1, D])
        edges_i = sb("edges_i", [P, 2, EC], I32)
        edges_f = sb("edges_f", [P, 2, EC])
        st = sb("st", [P, NT, 2, 6])
        mv = sb("mv", [P, NT, 2])
        rs = sb("rs", [P, 4, NT])
        dinv = sb("dinv", [P, NT])
        sm = sb("sm", [P, 16, NT, NE])
        s8 = sb("s8", [P, 8, NE])
        cst8 = sb("cst8", [P, 3, NT, NE])
        tabf = sb("tabf", [1, 3, NTAB, NE])
        tab1 = sb("tab1", [1, 4, NTAB + 1])
        tabi = sb("tabi", [1, 2, NTAB + 1], I32)
        slots_f = sb("slots_f", [P, 2, NT])
        slots_i = sb("slots_i", [P, 2, NT], I32)
        wts = sb("wts", [P, 2, NT])
        dot = sb("dot", [1, 1])
        cmb = sb("cmb", [P, NT, NE + 1])
        cmbT = sb("cmbT", [NE + 1, T])
        cols = sb("cols", [P, 12, NT])
        a12 = sb("a12", [P, 2, NT, H + 1])

        region = lambda t, a, n: t[:, a:a + n]
        xf = xfb[:, :, 0:D]
        ft = xfb[:, :, :].rearrange("p t (h e) -> p t h e", h=H)
        tD = region(big, 0, KC * T).rearrange("p (c n) -> p c n", c=KC)
        CT = big[0:P, 3750:3750 + NT * T].rearrange("p (t n) -> p t n", t=NT)
        a1T = big[0:H, 3750:4375]
        a1m = big[0:H, 4375:5625].rearrange("p (s n) -> p s n", s=2)
        xrows = region(big, 0, 2 * D).rearrange("p (t d) -> p t d", t=2)
        yrows = region(big, 1536, 2 * D).rearrange("p (t d) -> p t d", t=2)
        xTh = region(big, 3072, 768).bitcast(F16).rearrange("p (c n) -> p c n", c=KC)
        xTl = region(big, 3840, 768).bitcast(F16).rearrange("p (c n) -> p c n", c=KC)
        sbuf = region(big, 4608, 512).rearrange("p (s n) -> p s n", s=2)
        tbuf = region(big, 5120, 512).rearrange("p (s n) -> p s n", s=2)
        hh = region(big, 5632, 256).bitcast(F16).rearrange("p (s n) -> p s n", s=2)
        hl = region(big, 5888, 256).bitcast(F16).rearrange("p (s n) -> p s n", s=2)
        bsm = region(big, 6144, 8).rearrange("p (s n) -> p s n", s=RING)
        wg = region(ext, 0, KC * D).rearrange("p (c n) -> p c n", c=KC)
        hot = ext[0:P, 4608:4608 + 1875].bitcast(F16).rearrange("p (s a n) -> p s a n", s=EU, a=2)
        vst = [(wh if t < 3 else wl)[0:P, :, :].rearrange("p a n -> p (a n)")
               [:, (t % 3) * H * 256:(t % 3 + 1) * H * 256].rearrange("p (h c e) -> p h c e", h=H, c=4)
               for t in range(NT)]
        sides = region(big, 3840, 1875).bitcast(F16).rearrange("p (s q n) -> p s q n", s=3, q=2)
        outT = region(big, 5715, T)
        outn = big[0:P, 6340:6340 + NT * HD].rearrange("p (t e) -> p t e", t=NT)
        pT = ext[0:P, 0:6250].bitcast(F16).rearrange("p (s q k n) -> p s q k n", s=2, q=2, k=NT)
        ident16 = sb("ident16", [128, 128], F16)
        both = sb("both", [128, HD])
        prob = ext[0:P, 0:NT * T].rearrange("p (s n) -> p s n", s=NT)
        probT = ext[0:P, NT * T:2 * NT * T].rearrange("p (s k n) -> p s k n", s=NT, k=NT)
        relu1 = raw01[0:P, :, :].rearrange("p a n -> p (a n)")[:, 0:NT * T].rearrange("p (s n) -> p s n", s=NT)
        relu2 = wh[0:P, :, :].rearrange("p a n -> p (a n)").bitcast(F32)[:, 0:NT * T]\
            .rearrange("p (s n) -> p s n", s=NT)
        wl32 = wl[:, :, :].rearrange("p a n -> p (a n)").bitcast(F32)
        junk = wl32[0:P, 0:T]
        wheads = wl32[:, 640:896]
        alr = ext[0:P, 0:2 * D].rearrange("p (a n) -> p a n", a=2)
        prod = ext[0:P, 1536:1536 + 2 * D].rearrange("p (a n) -> p a n", a=2)
        rows = ext[0:P, 0:6 * D].rearrange("p (s k n) -> p s k n", s=2, k=3)
        raw = [raw01[:, 0, :], raw01[:, 1, :], region(ext, 0, 3 * D + 2), region(ext, 2400, 3 * D + 2)]
        iota16 = sb("iota16", [P, T], F16)

        ps = ctx.enter_context(nc.psum_tensor("ps", [128, 8 * BANK], F32))

        def bank(b, n=1):
            return ps[:, b * BANK:(b + n) * BANK]

        def tiles5(two_banks, parts):
            return two_banks[0:parts, 0:NT * 128].rearrange("p (t n) -> p t n", t=NT)[:, :, 0:P]

        prob32 = relu1

        def heads_twice(t):
            v = xf[:, t, :].rearrange("p (h e) -> p h e", h=H)
            return v.unsqueeze(2).to_broadcast([P, H, 2, HD])

        def score_bank(m, n0=0, n1=T):
            at = (0, 1, 0, 0, 1)[m % 5] * 1024
            return ps[0:P, at + n0:at + n1]

        def side_bank(s, t=None):
            v = bank(2, 2).bitcast(F16)[:, s * NT * 128:(s + 1) * NT * 128].rearrange("p (t n) -> p t n", t=NT)
            return v[:, :, 0:P] if t is None else v[:, t, 0:P]

        s_const = sem("s_const")
        s_fence = sem("s_fence")
        s_x = sem("s_x")
        s_edge = sem("s_edge")
        s_wg = sem("s_wg")
        s_vec = [sem(f"s_vec{i}") for i in range(2)]
        s_small = sem("s_small")
        s_zero = sem("s_zero")
        s_v = sem("s_v")
        s_sq = sem("s_sq")
        s_var = sem("s_var")
        s_hot = sem("s_hot")
        s_cmm = sem("s_cmm")
        s_ct = sem("s_ct")
        s_ctv = sem("s_ctv")
        s_cT = sem("s_cT")
        s_cda = sem("s_cda")
        s_cdv = sem("s_cdv")
        s_rowsok = sem("s_rowsok")
        s_tp = sem("s_tp")
        s_tpe = sem("s_tpe")
        s_hmm = sem("s_hmm")
        s_hev = sem("s_hev")
        s_agg = sem("s_agg")
        s_aggv = sem("s_aggv")
        s_vh = sem("s_vh")
        s_vl = sem("s_vl")
        s_sides = sem("s_sides")
        s_sidea = sem("s_sidea")
        s_sidev = sem("s_sidev")
        s_mT = sem("s_mT")
        s_mTh = sem("s_mTh")
        s_mTl = sem("s_mTl")
        s_mpv = sem("s_mpv")
        s_mout = sem("s_mout")
        s_mback = sem("s_mback")
        s_mrec = sem("s_mrec")
        s_mfin = sem("s_mfin")
        s_madd = sem("s_madd")
        s_s = sem("s_s")
        s_mx = sem("s_mx")
        s_exp = sem("s_exp")
        s_pT = sem("s_pT")
        s_pv = sem("s_pv")
        s_pvv = sem("s_pvv")
        s_rd = sem("s_rd")
        s_lg = sem("s_lg")
        s_lge = sem("s_lge")
        s_lx = sem("s_lx")
        s_sel = sem("s_sel")
        s_rk = sem("s_rk")
        s_slot = sem("s_slot")
        s_scat = sem("s_scat")
        s_cmT = sem("s_cmT")
        s_cmTv = sem("s_cmTv")
        s_bo = sem("s_bo")
        s_bov = sem("s_bov")
        s_gat = [sem(f"s_gat{i}") for i in range(2)]
        s_add = sem("s_add")
        s_wh = sem("s_wh")
        s_ft = sem("s_ft")
        s_ftv = sem("s_ftv")
        s_al = sem("s_al")
        s_aT = sem("s_aT")
        s_aTv = sem("s_aTv")
        s_am = sem("s_am")
        s_ab = sem("s_ab")
        s_abf = sem("s_abf")
        s_gm = sem("s_gm")
        s_gb = sem("s_gb")
        s_r = sem("s_r")
        s_rm = sem("s_rm")
        s_ge = sem("s_ge")
        s_pc = sem("s_pc")
        s_gseq = sem("s_gseq")
        s_done = sem("s_done")
        s_tpa = sem("s_tpa")
        s_fta = sem("s_fta")
        s_evv = sem("s_evv")
        s_eva = sem("s_eva")
        s_cm = sem("s_cm")
        ph_s = Phase(sem, "shared", IS // 128, False, True, GS, x_shared)
        ph_0 = Phase(sem, "layer0", I0 // 128, True, True, B, x_slots)
        ph_1 = Phase(sem, "layer1", I1 // 128, True, False, B, x_slots)
        units = {id(ph_s): units_s, id(ph_0): units0, id(ph_1): units1}
        outs = {id(ph_s): y_shared, id(ph_0): y_slots, id(ph_1): y_slots}

        block = ctx.enter_context(nc.Block())

        ENGINES = 4

        def fence(eng, k):
            if k > 1:
                eng.wait_ge(s_fence, ENGINES * (k - 1))
            eng.drain().then_inc(s_fence, 1)
            eng.wait_ge(s_fence, ENGINES * k)

        def passes(eng):
            return eng.value_load(tabi[0:1, 0:1, NTAB:NTAB + 1].rearrange("p a n -> p (a n)"),
                                  min_val=NE, max_val=NPMAX)

        def ffn_sync(sp, ph, n_pass, routed):
            def expert(i):
                if not routed:
                    return 0
                return sp.value_load(tabi[0:1, 0:1, bass.ds(i, 1)].rearrange("p a n -> p (a n)"),
                                     min_val=0, max_val=NE - 1)

            def load(i, e, u):
                g = i * ph.ic + u
                sp.wait_ge(ph.hi, g + 1)
                sp.wait_ge(ph.lo, g + 1)
                w = units[id(ph)]
                unit = w[bass.ds(e, 1), u, :, :].rearrange("a p n -> p (a n)") if routed else w[u, :, :]
                sp.dma_start(raw[u % RING][:, 0:ph.cols], unit).then_inc(ph.raw[u % RING], 16)

            with sp.Fori(0, n_pass) as i:
                e = expert(i)
                for u in range(ph.ic):
                    load(i, e, u)
            e = expert(n_pass)
            for u in range(2):
                load(n_pass, e, u)

        def ffn_pool(pool, ph, n_pass):
            def rows_in(i):
                source = ph.rows[bass.ds(i * ph.n, ph.n), :] if not isinstance(i, int) \
                    else ph.rows[i * ph.n:(i + 1) * ph.n, :]
                pool.dma_start(xrows[0:ph.n // 2, :, :],
                               source.rearrange("(t p) d -> p t d", t=2)).then_inc(ph.xrows, 16)

            rows_in(0)
            with pool.Fori(0, n_pass) as i:
                pool.wait_ge(ph.xt, i * 3 + 3)
                rows_in(i + 1)
                pool.wait_ge(ph.ya, i + 2)
                pool.wait_ge(ph.yv, i + 2)
                pool.dma_start(outs[id(ph)][bass.ds(i * ph.n, ph.n), :].rearrange("(t p) d -> p t d", t=2),
                               yrows[0:ph.n // 2, :, :]).then_inc(ph.stored, 16)
                pool.wait_ge(ph.stored, i * 16 + 16)
                pool.sem_inc(ph.yfree, 1)

        def ffn_scalar(act, ph, n_pass):
            half = ph.n // 2

            def high(i, u):
                g = i * ph.ic + u
                act.wait_ge(ph.raw[u % RING], i * (16 * ph.ic // RING) + 16 * (u // RING) + 16)
                act.wait_ge(ph.down, g + 1)
                if ph.bias:
                    nc.scalar.activation(bsm[:, u % RING, 0:1], raw[u % RING][:, ph.wide:ph.wide + 1], ACT.Copy)
                nc.scalar.activation(wh[:, u % RING, 0:ph.wide], raw[u % RING][:, 0:ph.wide], ACT.Copy,
                                     scale=WS).then_inc(ph.hi, 1)

            def x_high(i):
                for k in range(3):
                    act.wait_ge(ph.xt, i * 3 + k + 1)
                    src_ = bank(6 + k % 2).rearrange("p (c n) -> p c n", c=2)[:, :, 0:ph.n]
                    nc.scalar.activation(xTh[:, 2 * k:2 * k + 2, 0:ph.n], src_, ACT.Copy).then_inc(ph.xhi, 1)

            x_high(0)
            high(0, 0)
            high(0, 1)
            with act.Fori(0, n_pass) as i:
                for u in range(ph.ic):
                    g = i * ph.ic + u
                    high(i, u + 2)
                    act.wait_ge(ph.up, g + 1)
                    if ph.bias:
                        act.wait_ge(ph.hi, g + 1 + RING)
                        bias = bsm[:, u % RING, 0:1]
                    else:
                        bias = 0.0
                    a = bank(4 + u % 2)[:, 0:ph.n]
                    nc.scalar.activation(sbuf[:, u % 2, 0:ph.n], a, ACT.Silu, bias=bias,
                                         scale=1.0 / WS).then_inc(ph.silu, 1)
                x_high(i + 1)
                act.wait_ge(ph.down, (i + 1) * ph.ic + RING)
                act.wait_ge(ph.yfree, i + 1)
                nc.scalar.activation(yrows[0:half, 0, :], ps[0:half, 0:D], ACT.Copy,
                                     scale=1.0 / WS).then_inc(ph.ya, 1)

        def ffn_vector(dve, ph, n_pass):
            half = ph.n // 2

            def low(i, u):
                g = i * ph.ic + u
                dve.wait_ge(ph.hi, g + 1 + RING)
                if ph.bias and ph.gated:
                    nc.vector.tensor_scalar(bsm[:, u % RING, 1:2], raw[u % RING][:, ph.wide + 1:ph.wide + 2],
                                            WS, None, ALU.mult)
                nc.vector.scalar_tensor_tensor(
                    out=wl[:, u % RING, 0:ph.wide], in0=raw[u % RING][:, 0:ph.wide], scalar=WS,
                    in1=wh[:, u % RING, 0:ph.wide], op0=ALU.mult, op1=ALU.subtract).then_inc(ph.lo, 1)

            def x_low(i):
                for k in range(3):
                    dve.wait_ge(ph.xhi, i * 3 + k + 1)
                    src_ = bank(6 + k % 2).rearrange("p (c n) -> p c n", c=2)[:, :, 0:ph.n]
                    nc.vector.tensor_tensor(xTl[:, 2 * k:2 * k + 2, 0:ph.n], src_,
                                            xTh[:, 2 * k:2 * k + 2, 0:ph.n], ALU.subtract).then_inc(ph.xlo, 1)

            x_low(0)
            low(0, 0)
            low(0, 1)
            with dve.Fori(0, n_pass) as i:
                for u in range(ph.ic):
                    g = i * ph.ic + u
                    low(i, u + 2)
                    dve.wait_ge(ph.silu, g + 1)
                    s_ = sbuf[:, u % 2, 0:ph.n]
                    h_, l_ = hh[:, u % 2, 0:ph.n], hl[:, u % 2, 0:ph.n]
                    if ph.gated:
                        gate = bank(4 + u % 2)[:, 256:256 + ph.n]
                        t_ = tbuf[:, u % 2, 0:ph.n]
                        if ph.bias:
                            dve.wait_ge(ph.lo, g + 1 + RING)
                            nc.vector.scalar_tensor_tensor(out=t_, in0=gate, scalar=bsm[:, u % RING, 1:2],
                                                           in1=s_, op0=ALU.add, op1=ALU.mult).then_inc(ph.hseq, 1)
                        else:
                            nc.vector.tensor_tensor(t_, gate, s_, ALU.mult).then_inc(ph.hseq, 1)
                        dve.wait_ge(ph.hseq, g * 2 + 1)
                        nc.vector.tensor_scalar(h_, t_, 1.0 / WS, None, ALU.mult).then_inc(ph.hseq, 1)
                        dve.wait_ge(ph.hseq, g * 2 + 2)
                        nc.vector.scalar_tensor_tensor(out=l_, in0=t_, scalar=1.0 / WS, in1=h_, op0=ALU.mult,
                                                       op1=ALU.subtract).then_inc(ph.h, 1)
                    else:
                        nc.vector.tensor_copy(h_, s_).then_inc(ph.hseq, 1)
                        dve.wait_ge(ph.hseq, g + 1)
                        nc.vector.tensor_tensor(l_, s_, h_, ALU.subtract).then_inc(ph.h, 1)
                x_low(i + 1)
                dve.wait_ge(ph.down, (i + 1) * ph.ic + RING)
                dve.wait_ge(ph.yfree, i + 1)
                nc.vector.tensor_scalar(yrows[0:half, 1, :], ps[0:half, 2 * BANK:2 * BANK + D], 1.0 / WS, None,
                                        ALU.mult).then_inc(ph.yv, 1)

        def ffn_tensor(pe, ph, n_pass):
            half = ph.n // 2

            def three(out_, pairs, n_all, n, last=False):
                ins = None
                for k, (l_, r_) in enumerate(pairs):
                    ins = nc.tensor.matmul(out_, l_, r_, start=(n == 0 and k == 0),
                                           stop=(n == n_all - 1 and k == len(pairs) - 1))
                return ins

            def rows_transposed(k, wait):
                if wait is not None:
                    pe.wait_ge(ph.xlo, wait)
                for c in range(2):
                    for t in range(2):
                        ins = nc.tensor.transpose(
                            bank(6 + k % 2)[:, c * 256 + t * half:c * 256 + (t + 1) * half],
                            xrows[0:half, t, (2 * k + c) * 128:(2 * k + c + 1) * 128], ident[0:half, 0:half])
                ins.then_inc(ph.xt, 1)

            def up(i, u):
                g = i * ph.ic + u
                pe.wait_ge(ph.lo, g + 1 + RING)
                pe.wait_ge(ph.h, g + 1)
                for m in range(2 if ph.gated else 1):
                    for c in range(KC):
                        w0 = m * D + c * 128
                        ins = three(bank(4 + u % 2)[:, m * 256:m * 256 + ph.n],
                                    [(wh[:, u % RING, w0:w0 + 128], xTh[:, c, 0:ph.n]),
                                     (wh[:, u % RING, w0:w0 + 128], xTl[:, c, 0:ph.n]),
                                     (wl[:, u % RING, w0:w0 + 128], xTh[:, c, 0:ph.n])], KC, c)
                ins.then_inc(ph.up, 1)

            def down(i, u, first, last):
                g = i * ph.ic + u
                if first:
                    pe.wait_ge(ph.ya, i + 1)
                    pe.wait_ge(ph.yv, i + 1)
                pe.wait_ge(ph.h, g + 3)
                w0 = ph.wide - D
                for t in range(2):
                    for n0, n1 in ((0, BANK), (BANK, D)):
                        o = ps[0:half, 2 * t * BANK + n0:2 * t * BANK + n1]
                        hs, ls = (v[:, u % 2, t * half:(t + 1) * half] for v in (hh, hl))
                        for k, (l_, r_) in enumerate(((hs, wh), (hs, wl), (ls, wh))):
                            ins = nc.tensor.matmul(o, l_, r_[:, u % RING, w0 + n0:w0 + n1],
                                                   start=first and k == 0, stop=last and k == 2)
                ins.then_inc(ph.down, 1)

            pe.wait_ge(ph.xrows, 16)
            rows_transposed(0, None)
            rows_transposed(1, None)
            rows_transposed(2, 1)
            with pe.Fori(0, n_pass) as i:
                pe.wait_ge(ph.xlo, i * 3 + 3)
                for u in range(ph.ic):
                    up(i, u)
                    if u:
                        down(i, u - 1, u == 1, False)
                pe.wait_ge(ph.xrows, i * 16 + 32)
                rows_transposed(0, i * 3 + 3)
                rows_transposed(1, None)
                down(i, ph.ic - 1, False, True)
                rows_transposed(2, i * 3 + 4)

        def head_cols(rows_, j, q, width=HD):
            c = j * (2 * width) + width * q
            return rows_[:, c:c + width] if isinstance(c, int) else rows_[:, bass.ds(c, width)]

        def lagged(op, j, m, lag, first):
            if m >= lag:
                op(j, m - lag)
            elif not first:
                op(j - 1, m - lag + 10)

        @block.sync
        def _(sp):
            sp.dma_start(xres[:, :, :], x.rearrange("(t p) d -> p t d", p=P)).then_inc(s_x, 16)
            sp.dma_start(edges_i[:, 0, :], src.rearrange("(p c) -> p c", p=P)).then_inc(s_edge, 16)
            sp.dma_start(edges_i[:, 1, :], dst.rearrange("(p c) -> p c", p=P)).then_inc(s_edge, 16)
            sp.dma_start(wg[:, :, :], gnn_w.rearrange("(c p) n -> p c n", p=128)).then_inc(s_wg, 16)
            for v in range(2):
                sp.dma_start(vec[:, v, :], vecs[v, :].partition_broadcast(P)).then_inc(s_vec[v], 16)
            sp.dma_start(gates[:, 0, :, :], gate0.rearrange("(c p) e -> p c e", p=128)).then_inc(s_small, 16)
            sp.dma_start(gates[:, 1, :, :], gate1.rearrange("(c p) e -> p c e", p=128)).then_inc(s_small, 16)
            sp.dma_start(bout[:, :], bias_out).then_inc(s_small, 16)
            sp.wait_ge(s_const, C_ZERO)
            sp.dma_start(x_slots.rearrange("(t p) d -> p t d", p=B // 2),
                         raw01[0:B // 2, 0:1, 0:D].to_broadcast([B // 2, 2 * NTAB, D])).then_inc(s_zero, 16)
            sp.dma_start(x_shared.rearrange("(t p) d -> p t d", p=GS // 2),
                         raw01[0:GS // 2, 0:1, 0:D].to_broadcast([GS // 2, 2 * NG + 2, D])).then_inc(s_zero, 16)
            sp.dma_start(y_slots[NE * B:NPMAX * B, :].rearrange("(t p) d -> p t d", p=B // 2),
                         raw01[0:B // 2, 0:1, 0:D].to_broadcast([B // 2, 2 * (NPMAX - NE), D])).then_inc(s_zero, 16)
            sp.wait_ge(s_zero, 48)

            sp.wait_ge(s_fence, ENGINES * F_GRAPH)
            sp.dma_start(vec[:, 0, :], vecs[2, :].partition_broadcast(P)).then_inc(s_vec[0], 16)
            sp.wait_ge(s_fence, ENGINES * F_MHA)
            sp.dma_start(vec[:, 1, :], vecs[3, :].partition_broadcast(P)).then_inc(s_vec[1], 16)
            sp.wait_ge(s_rowsok, R_XF0)
            sp.dma_start(x_shared[0:T, :].rearrange("(t p) d -> p t d", p=P), xf[:, :, :]).then_inc(s_lx, 16)
            ffn_sync(sp, ph_s, NG, False)
            sp.wait_ge(s_fence, ENGINES * F_SHARED)
            ffn_sync(sp, ph_0, passes(sp), True)
            sp.wait_ge(s_wh, 1)
            for q in range(2):
                for m in range(2):
                    sp.dma_start(wheads[64 * q:64 * q + 64, 128 * m + 64 * q:128 * m + 64 * q + 64],
                                 w_heads[:, m, :]).then_inc(s_al, 16)
            for a in range(2):
                sp.dma_start(alr[:, a, :], attn_lr[a, :].partition_broadcast(P)).then_inc(s_al, 16)
            sp.wait_ge(s_fence, ENGINES * F_ROUTE1)
            ffn_sync(sp, ph_1, passes(sp), True)
            sp.wait_ge(s_add, 2 * NT)
            sp.dma_start(out.rearrange("(t p) d -> p t d", p=P), xres[:, :, :]).then_inc(s_done, 16)
            sp.wait_ge(s_done, 16)

        @block.gpsimd
        def _(pool):
            for ph in (ph_s, ph_0, ph_1):
                pool.sem_inc(ph.hi, RING)
                pool.sem_inc(ph.lo, RING)
                pool.sem_inc(ph.down, RING)
                pool.sem_inc(ph.h, 2)
                pool.sem_inc(ph.ya, 1)
                pool.sem_inc(ph.yv, 1)
                pool.sem_inc(ph.yfree, 1)
            for s_ in (s_ge, s_pT, s_pv, s_rm):
                pool.sem_inc(s_, NT)
            for s_ in (s_exp, s_pvv):
                pool.sem_inc(s_, 2)
            for s_ in (s_mTl, s_mfin, s_madd):
                pool.sem_inc(s_, 1)
            pool.sem_inc(s_mpv, 2 * NT)
            pool.sem_inc(s_evv, 1)
            pool.sem_inc(s_eva, 1)
            pool.sem_inc(s_r, 2 * NT)
            nc.gpsimd.iota(iota16[:, :], pattern=[[1, T]], base=0, channel_multiplier=0,
                           allow_small_or_imprecise_dtypes=True).then_inc(s_const, 1)
            nc.gpsimd.memset(raw01[:, 0, 0:D], 0.0).then_inc(s_const, 1)
            nc.gpsimd.memset(ident[:, :], 0.0).then_inc(s_const, 1)
            nc.gpsimd.memset(ones[:, :], 1.0).then_inc(s_const, 1)
            pool.wait_ge(s_const, 4)
            nc.gpsimd.affine_select(out=ident[:, :], in_=ident[:, :], compare_op=ALU.not_equal, fill=1.0, base=0,
                                    pattern=[[-1, 128]], channel_multiplier=1).then_inc(s_const, 1)
            nc.gpsimd.affine_select(out=tri[:, :], in_=ones[0:P, 0:P], compare_op=ALU.is_gt, fill=0.0, base=0,
                                    pattern=[[1, P]], channel_multiplier=-1).then_inc(s_const, 1)
            for k, (base, step) in enumerate(((0, 1), (0, B), ((NE - 1) * B, -B))):
                nc.gpsimd.iota(cst8[:, k, :, :], pattern=[[0, NT], [step, NE]], base=base, channel_multiplier=0,
                               allow_small_or_imprecise_dtypes=True).then_inc(s_const, 1)
            nc.gpsimd.iota(tabf[:, 0, :, :], pattern=[[1, NTAB], [0, NE]], base=-NE, channel_multiplier=0,
                           allow_small_or_imprecise_dtypes=True).then_inc(s_const, 1)
            nc.gpsimd.iota(tab1[:, 0, :], pattern=[[1, NTAB + 1]], base=0, channel_multiplier=0,
                           allow_small_or_imprecise_dtypes=True).then_inc(s_const, 1)

            def scatter(layer):
                pool.wait_ge(s_slot, layer + 1)
                pool.wait_ge(s_zero, 48)
                for k in range(2):
                    for t in range(NT):
                        pool.indirect_dma_start(
                            out=x_slots, out_offset=bass.IndirectOffsetOnAxis(ap=slots_i[:, k, t:t + 1], axis=0),
                            in_=xf[:, t, :], in_offset=None).then_inc(s_scat, 16)
                pool.wait_ge(s_scat, (layer + 1) * 16 * 2 * NT)

            def gather(layer):
                for t in range(NT):
                    s = t % 2
                    if t >= 2 or layer:
                        pool.wait_ge(s_add, layer * NT + t - 1 if t >= 2 else NT)
                    for k in range(2):
                        pool.indirect_dma_start(
                            out=rows[:, s, k, :], out_offset=None, in_=y_slots,
                            in_offset=bass.IndirectOffsetOnAxis(ap=slots_i[:, k, t:t + 1], axis=0)
                        ).then_inc(s_gat[s], 16)
                    if layer == 0:
                        pool.dma_start(rows[:, s, 2, :], y_shared[t * P:(t + 1) * P, :]).then_inc(s_gat[s], 16)

            fence(pool, F_GRAPH)
            with pool.Fori(0, H) as h:
                pool.wait_ge(s_mfin, h + 2)
                at = z[:, :, bass.ds(h * HD, HD)]
                nc.gpsimd.tensor_tensor(at, at, outn, ALU.add).then_inc(s_madd, 1)
            fence(pool, F_MHA)
            pool.wait_ge(s_lx, 16)
            scatter(0)
            fence(pool, F_ROUTE0)
            ffn_pool(pool, ph_s, NG)
            fence(pool, F_SHARED)
            ffn_pool(pool, ph_0, passes(pool))
            fence(pool, F_EXP0)
            gather(0)
            fence(pool, F_LAYER0)
            with pool.Fori(0, H * NT // 10) as j:
                for m in range(10):
                    n = j * 10 + m
                    pool.wait_ge(s_ge, n + 1 + NT)
                    nc.gpsimd.tensor_tensor(prob[:, m % 5, :], prob[:, m % 5, :], cds[:, m % 5, :],
                                            ALU.mult).then_inc(s_pc, 1)
            fence(pool, F_GAT)
            scatter(1)
            fence(pool, F_ROUTE1)
            ffn_pool(pool, ph_1, passes(pool))
            fence(pool, F_EXP1)
            gather(1)

        @block.scalar
        def _(act):
            count = {"sq": 0, "tpa": 0}

            def root():
                count["sq"] += 1
                act.wait_ge(s_var, count["sq"])
                nc.scalar.activation(rs[:, 1, :], rs[:, 0, :], ACT.Sqrt).then_inc(s_sq, 1)

            def squares():
                count["sq"] += 1
                act.wait_ge(s_var, count["sq"])
                for t in range(NT):
                    ins = nc.scalar.activation(xf[:, t, :], z[:, t, :], ACT.Square, accum_out=rs[:, 0, t:t + 1])
                ins.then_inc(s_sq, 1)

            def transposed_out():
                for c in range(1, KC, 2):
                    act.wait_ge(s_tp, KC * (count["tpa"] // 3) + c + 1)
                    nc.scalar.activation(tD[:, c, :].rearrange("p (t n) -> p t n", t=NT),
                                         tiles5(bank(6, 2), 128), ACT.Copy).then_inc(s_tpa, 1)
                    count["tpa"] += 1

            root()
            transposed_out()
            for t in range(NT):
                act.wait_ge(s_hmm, t + 1)
                nc.scalar.activation(xf[:, t, :], ps[0:P, (t % 2) * 1024:(t % 2) * 1024 + D], ACT.Copy)\
                    .then_inc(s_hev, 1)
            act.wait_ge(s_cmm, EC)
            for i in range(NT):
                nc.scalar.activation(CT[:, i, 0:4 * P], ps[0:P, i * BANK:i * BANK + 4 * P], ACT.Copy)\
                    .then_inc(s_ct, 1)
            for i in range(NT):
                act.wait_ge(s_cT, i + 1)
                nc.scalar.activation(cds[:, i, :].rearrange("p (k n) -> p k n", k=NT),
                                     tiles5(bank(4 + 2 * (i % 2), 2), P), ACT.Copy).then_inc(s_cda, 1)
            root()
            fence(act, F_GRAPH)

            root()
            squares()
            root()
            act.wait_ge(s_rowsok, R_XN0)
            for t in range(NT):
                nc.scalar.activation(vst[t][:, :, 0:2, :], heads_twice(t), ACT.Copy).then_inc(s_vh, 1)
            act.wait_ge(s_zero, 48)

            def sides_out(h, q):
                act.wait_ge(s_sides, h + 1)
                for s, scale in ((0, 0.5), (1, 0.25)):
                    ins = nc.scalar.activation(sides[:, s, q, :].rearrange("p (t n) -> p t n", t=NT),
                                               side_bank(s), ACT.Copy, scale=scale)
                ins.then_inc(s_sidea, 1)

            def exp(j, m):
                act.wait_ge(s_mx, j * 10 + m + 1)
                nc.scalar.activation(prob32[:, m % 2, :], score_bank(m), ACT.Exp,
                                     bias=cols[:, m // 5, m % 5:m % 5 + 1],
                                     accum_out=cols[:, 2 + m // 5, m % 5:m % 5 + 1]).then_inc(s_exp, 1)

            def high(j, m):
                q, t = divmod(m, 5)
                act.wait_ge(s_mT, j * 10 + m + 1)
                act.wait_ge(s_mpv, j * 10 + 5 * q + 5)
                nc.scalar.activation(pT[:, 0, q, :, t * P:(t + 1) * P], tiles5(bank(4, 2), P), ACT.Copy)\
                    .then_inc(s_mTh, 1)

            def sum_out(j, m):
                act.wait_ge(s_mpv, j * 10 + 5 * (m // 5) + 10)
                nc.scalar.activation(outT, bank(6, 2)[:, 0:T], ACT.Copy).then_inc(s_mout, 1)

            def mha_turn(j, first, last):
                for m in range(10):
                    q, t = divmod(m, 5)
                    if t == NT - 1 and not (first and q == 0):
                        sum_out(j, m)
                    lagged(high, j, m, 1, first)
                    exp(j, m)
                    if t == 2 and not (last and q == 1):
                        sides_out(j * 2 + q + 1, 1 - q)

            sides_out(0, 0)
            mha_turn(0, True, False)
            with act.Fori(1, H // 2 - 1) as j:
                mha_turn(j, False, False)
            mha_turn(H // 2 - 1, False, True)
            high(H // 2 - 1, 9)
            sum_out(H // 2, 0)
            fence(act, F_MHA)

            def route():
                transposed_out()
                act.wait_ge(s_lge, count_route[0] + 1)
                nc.scalar.activation(sm[:, 1, :, :], sm[:, 0, :, :], ACT.Exp).then_inc(s_sel, 1)
                count_route[0] += 1

            count_route = [0]
            squares()
            root()
            route()
            fence(act, F_ROUTE0)
            ffn_scalar(act, ph_s, NG)
            fence(act, F_SHARED)
            ffn_scalar(act, ph_0, passes(act))
            fence(act, F_EXP0)
            fence(act, F_LAYER0)

            root()
            transposed_out()
            for n in range(NT * KC):
                act.wait_ge(s_ftv, n + 1)
                t, c = divmod(n, KC)
                nc.scalar.activation(z[:, t, 128 * c:128 * c + 128], bank(n % 4)[0:P, 128:256], ACT.Copy)\
                    .then_inc(s_fta, 1)
            def clamp(j, m):
                n = j * 10 + m
                q = m // 5
                if m % 5 == 0:
                    act.wait_ge(s_gb, j * 2 + q + 1)
                act.wait_ge(s_rm, n + 1)
                act.wait_ge(s_ge, n + 1)
                ab = ps[0:P, q * 1024:q * 1024 + T]
                nc.scalar.activation(relu1[:, m % 5, :], ab, ACT.Relu, scale=-1.0,
                                     bias=cols[:, 2 + q, m % 5:m % 5 + 1])
                nc.scalar.activation(relu2[:, m % 5, :], ab, ACT.Relu, scale=-0.2,
                                     bias=cols[:, 4 + q, m % 5:m % 5 + 1]).then_inc(s_r, 1)

            def gexp(j, m):
                n = j * 10 + m
                act.wait_ge(s_rm, n + 1 + NT)
                act.wait_ge(s_pT, n + 1)
                nc.scalar.activation(prob[:, m % 5, :], relu1[:, m % 5, :], ACT.Exp, scale=-1.0).then_inc(s_ge, 1)

            def odd_out(j, m):
                if m % 2 == 0:
                    return
                n = j * 10 + m
                act.wait_ge(s_pT, n + 1 + NT)
                act.wait_ge(s_pv, n + 1)
                nc.scalar.activation(probT[:, m % 5, :, :], tiles5(bank(4, 2), P), ACT.Copy).then_inc(s_eva, 1)

            def gat_turn(j, first):
                for m in range(10):
                    lagged(odd_out, j, m, 4, first)
                    lagged(gexp, j, m, 2, first)
                    clamp(j, m)

            gat_turn(0, True)
            with act.Fori(1, H // 2) as j:
                gat_turn(j, False)
            for m in range(10, 14):
                if m < 12:
                    gexp(H // 2 - 1, m - 2)
                odd_out(H // 2 - 1, m - 4)
            root()
            squares()
            root()
            route()
            fence(act, F_GAT)
            fence(act, F_ROUTE1)
            ffn_scalar(act, ph_1, passes(act))
            fence(act, F_EXP1)

        @block.vector
        def _(dve):
            count = {"v": 0, "sq": 0, "tp": 0, "route": 0}

            def step(ins):
                count["v"] += 1
                ins.then_inc(s_v, 1)
                dve.wait_ge(s_v, count["v"])

            def root_of(dst_):
                count["sq"] += 1
                dve.wait_ge(s_sq, count["sq"])
                step(nc.vector.reciprocal(dst_, rs[:, 1, :]))
                step(nc.vector.tensor_tensor(rs[:, 2, :], dst_, dst_, ALU.mult))
                step(nc.vector.tensor_tensor(rs[:, 2, :], rs[:, 2, :], rs[:, 0, :], ALU.mult))
                step(nc.vector.tensor_scalar(rs[:, 2, :], rs[:, 2, :], -0.5, 1.5, ALU.mult, ALU.add))
                step(nc.vector.tensor_tensor(dst_, dst_, rs[:, 2, :], ALU.mult))

            def layernorm():
                for t in range(NT):
                    for k in range(2):
                        ins = nc.vector.bn_stats(st[:, t, k, :], xres[:, t, k * D // 2:(k + 1) * D // 2])
                step(ins)
                for t in range(NT):
                    ins = nc.vector.bn_aggr(mv[:, t, :], st[:, t, :, :].rearrange("p a b -> p (a b)"))
                step(ins)
                nc.vector.tensor_scalar(rs[:, 0, :], mv[:, :, 1], 1e-5, None, ALU.add).then_inc(s_var, 1)
                root_of(rs[:, 3, :])
                for t in range(NT):
                    ins = nc.vector.tensor_scalar(z[:, t, :], xres[:, t, :], mv[:, t, 0:1], rs[:, 3, t:t + 1],
                                                  ALU.subtract, ALU.mult)
                step(ins)

            def rmsnorm(eps, v, n_vec):
                nc.vector.tensor_scalar(rs[:, 2, :], rs[:, 3, :], 1.0, None, ALU.mult).then_inc(s_var, 1)
                count["sq"] += 1
                dve.wait_ge(s_sq, count["sq"])
                nc.vector.tensor_scalar(rs[:, 0, :], rs[:, 0, :], 1.0 / D, eps, ALU.mult, ALU.add)\
                    .then_inc(s_var, 1)
                root_of(rs[:, 3, :])
                dve.wait_ge(s_vec[v], n_vec)
                for t in range(NT):
                    ins = nc.vector.scalar_tensor_tensor(out=xf[:, t, :], in0=z[:, t, :], scalar=rs[:, 3, t:t + 1],
                                                         in1=vec[:, v, :], op0=ALU.mult, op1=ALU.mult)
                ins.then_inc(s_rowsok, 1)

            def transposed_out():
                for c in range(0, KC, 2):
                    dve.wait_ge(s_tp, KC * (count["tp"] // 3) + c + 1)
                    nc.vector.tensor_copy(tD[:, c, :].rearrange("p (t n) -> p t n", t=NT),
                                          tiles5(bank(4, 2), 128)).then_inc(s_tpe, 1)
                    count["tp"] += 1

            dve.wait_ge(s_edge, 32)
            nc.vector.tensor_copy(edges_f[:, :, :], edges_i[:, :, :])
            dve.wait_ge(s_x, 16)
            layernorm()
            nc.vector.memset(a12[:, :, :, :], 0.0).then_inc(s_rowsok, 1)
            transposed_out()
            dve.wait_ge(s_vec[0], 16)
            dve.wait_ge(s_const, C_ALL)
            nc.vector.tensor_copy(ident16[:, :], ident[:, :])
            for a in range(2):
                nc.vector.tensor_copy(both[64 * a:64 * a + 64, :], ident[64 * a:64 * a + 64, 64 * a:64 * a + 64])
            for t in range(NT):
                ins = nc.vector.tensor_tensor(xres[:, t, :], xres[:, t, :], vec[:, 0, :], ALU.add)
            step(ins)

            def one_hot(j, s, first=False):
                c = j * EU + s
                if not first:
                    dve.wait_ge(s_cmm, c - EU + 1)
                for a in range(2):
                    col = edges_f[:, a, bass.ds(c, 1)] if not isinstance(c, int) else edges_f[:, a, c:c + 1]
                    ins = nc.vector.tensor_scalar(hot[:, s, a, :], iota16[:, :], col, None, ALU.is_equal)
                ins.then_inc(s_hot, 1)

            for s in range(EU):
                one_hot(0, s, True)
            with dve.Fori(1, EC // EU) as j:
                for s in range(EU):
                    one_hot(j, s)
            dve.wait_ge(s_cmm, EC)
            nc.vector.tensor_copy(CT[:, 0:4, 4 * P:T], bank(5)[0:P, 0:4 * P].rearrange("p (t n) -> p t n", t=4))
            nc.vector.tensor_copy(CT[:, 4, 4 * P:T], bank(6)[0:P, 0:P]).then_inc(s_ctv, 1)
            for i in range(NT):
                dve.wait_ge(s_cda, i + 1)
                nc.vector.tensor_scalar(mask[:, i, :], cds[:, i, :], 0.0, NEG, ALU.is_equal, ALU.mult)
                ins = nc.vector.tensor_reduce(rs[:, 0, i:i + 1], cds[:, i, :], AX.X, ALU.add)
                ins.then_inc(s_cdv, 1)
            dve.wait_ge(s_cdv, NT)
            nc.vector.tensor_scalar(rs[:, 0, :], rs[:, 0, :], 1.0, None, ALU.add).then_inc(s_var, 1)
            root_of(dinv[:, :])
            dve.wait_ge(s_hev, NT)
            for t in range(NT):
                ins = nc.vector.tensor_scalar(xf[:, t, :], xf[:, t, :], dinv[:, t:t + 1], None, ALU.mult)
            count["v"] += 1
            ins.then_inc(s_v, 1)
            dve.wait_ge(s_v, count["v"])
            nc.vector.memset(dot[0:1, 0:1], 0.0).then_inc(s_rowsok, 1)
            for i in range(NT):
                dve.wait_ge(s_agg, i + 1)
                step(nc.vector.tensor_tensor(z[:, i, :], ps[0:P, (i % 2) * 1024:(i % 2) * 1024 + D], xf[:, i, :],
                                             ALU.add))
                nc.vector.scalar_tensor_tensor(out=xres[:, i, :], in0=z[:, i, :], scalar=dinv[:, i:i + 1],
                                               in1=xres[:, i, :], op0=ALU.mult, op1=ALU.add).then_inc(s_aggv, 1)
            dve.wait_ge(s_aggv, NT)
            fence(dve, F_GRAPH)

            layernorm()
            rmsnorm(1e-5, 1, 16)
            for t in range(NT):
                dve.wait_ge(s_vh, t + 1)
                nc.vector.tensor_tensor(vst[t][:, :, 2:4, :], heads_twice(t), vst[t][:, :, 0:2, :],
                                        ALU.subtract).then_inc(s_vl, 1)

            def side_out(h, q):
                dve.wait_ge(s_sidea, h + 1)
                nc.vector.tensor_scalar(sides[:, 2, q, :].rearrange("p (t n) -> p t n", t=NT), side_bank(2),
                                        0.25, None, ALU.mult).then_inc(s_sidev, 1)

            def top(j, m):
                dve.wait_ge(s_s, j * 10 + m + 1)
                nc.vector.tensor_reduce(cols[:, m // 5, m % 5:m % 5 + 1], score_bank(m), AX.X, ALU.max,
                                        negate=True).then_inc(s_mx, 1)

            def low(j, m):
                q, t = divmod(m, 5)
                dve.wait_ge(s_mTh, j * 10 + m + 1)
                nc.vector.tensor_tensor(pT[:, 1, q, :, t * P:(t + 1) * P], tiles5(bank(4, 2), P),
                                        pT[:, 0, q, :, t * P:(t + 1) * P], ALU.subtract).then_inc(s_mTl, 1)

            def sums_inverted(h, q):
                dve.wait_ge(s_exp, h * 5 + 7)
                nc.vector.reciprocal(cols[:, 4 + q, :], cols[:, 2 + q, :]).then_inc(s_mrec, 1)

            def fin(h, q):
                dve.wait_ge(s_mback, h + 1)
                dve.wait_ge(s_mrec, h + 1)
                dve.wait_ge(s_madd, h + 1)
                nc.vector.tensor_tensor(outn, bank(6)[0:P, 0:NT * HD].rearrange("p (t e) -> p t e", t=NT),
                                        cols[:, 4 + q, :].unsqueeze(2).to_broadcast([P, NT, HD]), ALU.mult)\
                    .then_inc(s_mfin, 1)

            def mha_turn(j, first, last):
                for m in range(10):
                    q, t = divmod(m, 5)
                    if t == 0 and not first:
                        fin(j * 2 + q - 2, q)
                    top(j, m)
                    if t == 3 and not (last and q == 1):
                        side_out(j * 2 + q + 1, 1 - q)
                    lagged(low, j, m, 1, first)
                    if t == 1 and not (first and q == 0):
                        sums_inverted(j * 2 + q - 1, 1 - q)

            side_out(0, 0)
            mha_turn(0, True, False)
            with dve.Fori(1, H // 2 - 1) as j:
                mha_turn(j, False, False)
            mha_turn(H // 2 - 1, False, True)
            fin(H - 2, 0)
            low(H // 2 - 1, 9)
            sums_inverted(H - 1, 1)
            fin(H - 1, 1)
            fence(dve, F_MHA)

            def route(layer):
                transposed_out()
                bc = lambda a: a.unsqueeze(2).to_broadcast([P, NT, NE])
                per_t = lambda a: a.unsqueeze(1).to_broadcast([P, NT, NE])
                tmp, p, oh, sel, cand = sm[:, 0], sm[:, 1], [sm[:, 2], sm[:, 3]], sm[:, 4], sm[:, 5]
                p2, slot = sm[:, 6], sm[:, 7]
                top, best = rs[:, 0, :], rs[:, 1, :]
                dve.wait_ge(s_lg, layer + 1)
                lg = bank(0)[0:P, 0:NT * NE].rearrange("p (t e) -> p t e", t=NT)
                step(nc.vector.tensor_reduce(top, lg, AX.X, ALU.max))
                nc.vector.tensor_tensor(tmp, lg, bc(top), ALU.subtract).then_inc(s_lge, 1)
                dve.wait_ge(s_sel, layer + 1)
                step(nc.vector.tensor_reduce(top, p, AX.X, ALU.add))
                step(nc.vector.reciprocal(top, top))
                step(nc.vector.tensor_tensor(p, p, bc(top), ALU.mult))
                for k in range(2):
                    of = p if k == 0 else p2
                    step(nc.vector.tensor_reduce(wts[:, k, :], of, AX.X, ALU.max))
                    step(nc.vector.tensor_tensor(cand, of, bc(wts[:, k, :]), ALU.is_equal))
                    step(nc.vector.tensor_scalar(cand, cand, -float(NE), float(NE), ALU.mult, ALU.add))
                    step(nc.vector.tensor_tensor(cand, cand, cst8[:, 0], ALU.add))
                    step(nc.vector.tensor_reduce(best, cand, AX.X, ALU.min))
                    step(nc.vector.tensor_tensor(oh[k], cst8[:, 0], bc(best), ALU.is_equal))
                    if k == 0:
                        step(nc.vector.scalar_tensor_tensor(out=p2, in0=oh[0], scalar=-2.0, in1=p, op0=ALU.mult,
                                                            op1=ALU.add))
                nc.vector.tensor_tensor(sel, oh[0], oh[1], ALU.add).then_inc(s_rd, 1)
                if layer == 0:
                    step(nc.vector.tensor_scalar(wts[:, :, :], wts[:, :, :], 1e-7, None, ALU.max))
                    step(nc.vector.memset(cmb[:, :, :], 1.0))
                    step(nc.vector.tensor_tensor(tmp, oh[0], bc(wts[:, 0, :]), ALU.mult))
                    step(nc.vector.tensor_tensor(cand, oh[1], bc(wts[:, 1, :]), ALU.mult))
                    nc.vector.tensor_tensor(cmb[:, :, 0:NE], tmp, cand, ALU.add).then_inc(s_cm, 1)
                dve.wait_ge(s_rk, layer + 1)
                rank = bank(0)[0:P, 64:64 + NT * NE].rearrange("p (t e) -> p t e", t=NT)
                step(nc.vector.tensor_copy(s8[:, 0, :], bank(0)[0:P, 128:128 + NE]))
                step(nc.vector.tensor_scalar(s8[:, 1, :], s8[:, 0, :], float(B), None, ALU.is_gt))
                for k in range(2, (T - 1) // B + 1):
                    step(nc.vector.scalar_tensor_tensor(out=s8[:, 1, :], in0=s8[:, 0, :], scalar=float(k * B),
                                                        in1=s8[:, 1, :], op0=ALU.is_gt, op1=ALU.add))
                at = 1
                for k, d in enumerate((1, 2, 4)):
                    step(nc.vector.tensor_copy(s8[:, 2 + k, :], s8[:, at, :]))
                    step(nc.vector.tensor_tensor(s8[:, 2 + k, d:NE], s8[:, at, d:NE], s8[:, at, 0:NE - d], ALU.add))
                    at = 2 + k
                step(nc.vector.tensor_tensor(s8[:, 5, :], s8[:, at, :], s8[:, 1, :], ALU.subtract))
                step(nc.vector.scalar_tensor_tensor(out=s8[:, 6, :], in0=s8[:, 5, :], scalar=float(B),
                                                    in1=cst8[:, 2, 0, :], op0=ALU.mult, op1=ALU.add))
                step(nc.vector.tensor_scalar(cand, rank, float(B), None, ALU.is_ge))
                step(nc.vector.tensor_tensor(cand, cand, per_t(s8[:, 6, :]), ALU.mult))
                step(nc.vector.tensor_tensor(slot, rank, cst8[:, 1], ALU.add))
                step(nc.vector.tensor_tensor(slot, slot, cand, ALU.add))
                for k in range(2):
                    step(nc.vector.tensor_tensor(cand, slot, oh[k], ALU.mult))
                    step(nc.vector.tensor_reduce(slots_f[:, k, :], cand, AX.X, ALU.add))
                step(nc.vector.tensor_copy(slots_i[:, :, :], slots_f[:, :, :]))
                step(nc.vector.tensor_tensor(tabf[:, 1, :, :], s8[0:1, at:at + 1, :].to_broadcast([1, NTAB, NE]),
                                             tabf[:, 0, :, :], ALU.is_le))
                step(nc.vector.tensor_reduce(tab1[:, 1, 0:NTAB], tabf[:, 1, :, :], AX.X, ALU.add))
                step(nc.vector.tensor_scalar(tab1[:, 1, 0:NTAB], tab1[:, 1, 0:NTAB], float(NE - 1), None, ALU.min))
                step(nc.vector.tensor_scalar(tab1[:, 2, :], tab1[:, 0, :], float(NE), None, ALU.is_lt))
                step(nc.vector.tensor_tensor(tab1[:, 2, :], tab1[:, 2, :], tab1[:, 0, :], ALU.mult))
                step(nc.vector.tensor_tensor(tab1[:, 1, 0:NTAB], tab1[:, 1, 0:NTAB], tab1[:, 2, 0:NTAB], ALU.add))
                step(nc.vector.tensor_scalar(tab1[:, 1, NTAB:NTAB + 1], s8[0:1, at, NE - 1:NE], float(NE), None,
                                             ALU.add))
                step(nc.vector.tensor_copy(tabi[:, 0, :], tab1[:, 1, :]))
                nc.vector.memset(dot[0:1, 0:1], 0.0).then_inc(s_slot, 1)

            def combine(layer):
                if layer == 0:
                    dve.wait_ge(s_cmT, 1)
                    nc.vector.tensor_copy(cmbT[:, :].rearrange("e (t n) -> e t n", t=NT),
                                          tiles5(bank(0, 2), NE + 1)).then_inc(s_cmTv, 1)
                for t in range(NT):
                    s = t % 2
                    n_rows = 16 * (3 if layer == 0 else 2)
                    before = 0 if layer == 0 else 48 * (3 if s == 0 else 2)
                    dve.wait_ge(s_gat[s], before + n_rows * (t // 2 + 1))
                    if layer == 0:
                        dve.wait_ge(s_bo, t + 1)
                        step(nc.vector.tensor_tensor(z[:, t, :], z[:, t, :],
                                                     ps[0:P, (1 + s) * 1024:(1 + s) * 1024 + D], ALU.add))
                        step(nc.vector.tensor_tensor(z[:, t, :], z[:, t, :], rows[:, s, 2, :], ALU.add))
                    for k in range(2):
                        step(nc.vector.scalar_tensor_tensor(out=z[:, t, :], in0=rows[:, s, k, :],
                                                            scalar=wts[:, k, t:t + 1], in1=z[:, t, :],
                                                            op0=ALU.mult, op1=ALU.add))
                    nc.vector.tensor_tensor(xres[:, t, :], xres[:, t, :], z[:, t, :], ALU.add).then_inc(s_add, 1)

            rmsnorm(1e-5, 0, 32)
            dve.wait_ge(s_rowsok, R_XF0)
            dve.wait_ge(s_small, 48)
            route(0)
            fence(dve, F_ROUTE0)
            ffn_vector(dve, ph_s, NG)
            fence(dve, F_SHARED)
            ffn_vector(dve, ph_0, passes(dve))
            fence(dve, F_EXP0)
            combine(0)
            dve.wait_ge(s_add, NT)
            step(nc.vector.memset(wheads, 0.0))
            nc.vector.memset(dot[0:1, 0:1], 0.0).then_inc(s_wh, 1)
            fence(dve, F_LAYER0)

            layernorm()
            nc.vector.memset(ft[:, :, :, HD:HD + 1], 1.0).then_inc(s_rowsok, 1)
            transposed_out()
            for n in range(NT * KC):
                dve.wait_ge(s_ft, n + 1)
                t, c = divmod(n, KC)
                nc.vector.tensor_copy(ft[:, t, 2 * c:2 * c + 2, 0:HD],
                                      bank(n % 4)[0:P, 0:128].rearrange("p (h e) -> p h e", h=2)).then_inc(s_ftv, 1)
            dve.wait_ge(s_ftv, NT * KC)
            dve.wait_ge(s_al, 16 * 6)
            for t in range(NT):
                for a in range(2):
                    ins = nc.vector.tensor_tensor(prod[:, a, :].rearrange("p (h e) -> p h e", h=H),
                                                  ft[:, t, :, 0:HD],
                                                  alr[:, a, :].rearrange("p (h e) -> p h e", h=H), ALU.mult)
                step(ins)
                step(nc.vector.tensor_reduce(a12[:, :, t, 0:H],
                                             prod.rearrange("p a (h e) -> p a h e", h=H), AX.X, ALU.add))
            nc.vector.memset(dot[0:1, 0:1], 0.0).then_inc(s_am, 1)
            dve.wait_ge(s_aT, 1)
            step(nc.vector.tensor_copy(a1T.rearrange("h (t n) -> h t n", t=NT), tiles5(bank(4, 2), H)))

            def own_row(h, q):
                col = ident[0:H, bass.ds(h, 1)] if not isinstance(h, int) else ident[0:H, h:h + 1]
                nc.vector.tensor_scalar(a1m[:, q, :], a1T, col, None, ALU.mult).then_inc(s_am, 1)

            def edge_top(h, q, t):
                nc.vector.tensor_tensor_reduce(out=junk, in0=ps[0:P, q * 1024:q * 1024 + T], in1=mask[:, t, :],
                                               scale=1.0, scalar=-3e38, op0=ALU.add, op1=ALU.max,
                                               accum_out=cols[:, q, t:t + 1]).then_inc(s_gm, 1)

            def shifts(h, q):
                a2 = a12[:, 1, :, bass.ds(h, 1)] if not isinstance(h, int) else a12[:, 1, :, h:h + 1]
                a2 = a2.rearrange("p t a -> p (t a)")
                dve.wait_ge(s_gm, h * NT + NT)
                nc.vector.tensor_tensor(cols[:, 8, :], cols[:, q, :], a2, ALU.add).then_inc(s_gseq, 1)
                dve.wait_ge(s_gseq, h * 3 + 1)
                nc.vector.scalar_tensor_tensor(out=cols[:, 9, :], in0=cols[:, 8, :], scalar=0.2, in1=cols[:, 8, :],
                                               op0=ALU.mult, op1=ALU.max).then_inc(s_gseq, 1)
                dve.wait_ge(s_gseq, h * 3 + 2)
                nc.vector.tensor_tensor(cols[:, 2 + q, :], cols[:, 9, :], a2, ALU.subtract).then_inc(s_gseq, 1)
                nc.vector.scalar_tensor_tensor(out=cols[:, 4 + q, :], in0=a2, scalar=-0.2, in1=cols[:, 9, :],
                                               op0=ALU.mult, op1=ALU.add).then_inc(s_gb, 1)

            own_row(0, 0)
            dve.wait_ge(s_ab, 1)
            for t in range(NT):
                if t:
                    dve.wait_ge(s_gm, t)
                edge_top(0, 0, t)
            shifts(0, 0)
            def merge(j, m):
                n = j * 10 + m
                dve.wait_ge(s_r, n + 1 + 2 * NT)
                nc.vector.tensor_tensor(relu1[:, m % 5, :], relu1[:, m % 5, :], relu2[:, m % 5, :],
                                        ALU.min).then_inc(s_rm, 1)

            def even_out(j, m):
                if m % 2:
                    return
                n = j * 10 + m
                dve.wait_ge(s_pT, n + 1 + NT)
                dve.wait_ge(s_pv, n + 1)
                nc.vector.tensor_copy(probT[:, m % 5, :, :], tiles5(bank(4, 2), P)).then_inc(s_evv, 1)

            def gat_fin(j, m):
                n = j * 10 + m
                q, t = divmod(m, 5)
                dve.wait_ge(s_pv, n + 1 + NT)
                nc.vector.tensor_scalar(cols[:, 10 + q, t:t + 1],
                                        bank(6 + m % 2)[0:P, HD:HD + 1], 1e-37, None, ALU.max)\
                    .then_inc(s_rd, 1)
                dve.wait_ge(s_rd, N_RD + n * 2 + 1)
                nc.vector.reciprocal(cols[:, 10 + q, t:t + 1], cols[:, 10 + q, t:t + 1]).then_inc(s_rd, 1)
                dve.wait_ge(s_rd, N_RD + n * 2 + 2)
                at = head_cols(z[:, t, :], j, q)
                nc.vector.scalar_tensor_tensor(out=at, in0=bank(6 + m % 2)[0:P, 0:HD],
                                               scalar=cols[:, 10 + q, t:t + 1], in1=at, op0=ALU.mult,
                                               op1=ALU.add).then_inc(s_pvv, 1)

            def gat_turn(j, first):
                for m in range(10):
                    q, t = divmod(m, 5)
                    h = j * 2 + q + 1
                    if t == 0:
                        own_row(h, 1 - q)
                    lagged(gat_fin, j, m, 5, first)
                    lagged(even_out, j, m, 4, first)
                    if t == 0:
                        dve.wait_ge(s_ab, h + 1)
                    dve.wait_ge(s_gm, h * NT + t)
                    lagged(merge, j, m, 1, first)
                    edge_top(h, 1 - q, t)
                    if t == NT - 1:
                        shifts(h, 1 - q)

            gat_turn(0, True)
            with dve.Fori(1, H // 2) as j:
                gat_turn(j, False)
            for m in range(10, 15):
                gat_fin(H // 2 - 1, m - 5)
                if m < 14:
                    even_out(H // 2 - 1, m - 4)
                if m < 11:
                    merge(H // 2 - 1, m - 1)
            dve.wait_ge(s_pvv, N_ATT + 2)
            for t in range(NT):
                ins = nc.vector.scalar_tensor_tensor(out=xres[:, t, :], in0=z[:, t, :], scalar=0.0,
                                                     in1=xres[:, t, :], op0=ALU.max, op1=ALU.add)
            step(ins)
            layernorm()
            rmsnorm(1e-6, 1, 32)
            dve.wait_ge(s_rowsok, R_XF1)
            route(1)
            fence(dve, F_GAT)
            fence(dve, F_ROUTE1)
            ffn_vector(dve, ph_1, passes(dve))
            fence(dve, F_EXP1)
            combine(1)

        @block.tensor
        def _(pe):
            count = {"tp": 0}

            def transpose_rows(rows_):
                for c in range(KC):
                    k = count["tp"]
                    done = s_tpe if c % 2 == 0 else s_tpa
                    if k >= 2:
                        pe.wait_ge(done, (k - c) // 2 + c // 2)
                    o = bank(4 + 2 * (c % 2), 2)
                    for t in range(NT):
                        ins = nc.tensor.transpose(o[:, t * 128:t * 128 + P], rows_[:, t, c * 128:(c + 1) * 128],
                                                  ident[0:P, 0:P])
                    ins.then_inc(s_tp, 1)
                    count["tp"] += 1

            def transposed(k):
                pe.wait_ge(s_tpe, 3 * k)
                pe.wait_ge(s_tpa, 3 * k)

            pe.wait_ge(s_const, C_ALL)
            pe.wait_ge(s_rowsok, R_Z0)
            transpose_rows(z)
            transposed(1)
            pe.wait_ge(s_wg, 16)
            for t in range(NT):
                if t >= 2:
                    pe.wait_ge(s_hev, t - 1)
                for n0, n1 in ((0, BANK), (BANK, D)):
                    for c in range(KC):
                        ins = nc.tensor.matmul(ps[0:P, (t % 2) * 1024 + n0:(t % 2) * 1024 + n1],
                                               tD[:, c, t * P:(t + 1) * P], wg[:, c, n0:n1],
                                               start=c == 0, stop=c == KC - 1)
                ins.then_inc(s_hmm, 1)

            def edge_chunk(j, s, first, last):
                pe.wait_ge(s_hot, j * EU + s + 1)
                for i in range(NT):
                    src_ = hot[:, s, 0, i * P:(i + 1) * P]
                    nc.tensor.matmul(ps[0:P, i * BANK:i * BANK + 4 * P], src_, hot[:, s, 1, 0:4 * P],
                                     start=first, stop=last, skip_group_check=True)
                    at = 5 * BANK + i * P if i < 4 else 6 * BANK
                    ins = nc.tensor.matmul(ps[0:P, at:at + P], src_, hot[:, s, 1, 4 * P:T],
                                           start=first and i in (0, 4), stop=last, skip_group_check=True)
                ins.then_inc(s_cmm, 1)

            pe.wait_ge(s_hev, NT)
            for s in range(EU):
                edge_chunk(0, s, s == 0, False)
            with pe.Fori(1, EC // EU - 1) as j:
                for s in range(EU):
                    edge_chunk(j, s, False, False)
            for s in range(EU):
                edge_chunk(EC // EU - 1, s, False, s == EU - 1)
            pe.wait_ge(s_ct, NT)
            pe.wait_ge(s_ctv, 1)
            for i in range(NT):
                if i >= 2:
                    pe.wait_ge(s_cda, i - 1)
                o = bank(4 + 2 * (i % 2), 2)
                for k in range(NT):
                    ins = nc.tensor.transpose(o[0:P, k * 128:k * 128 + P], CT[:, k, i * P:(i + 1) * P],
                                              ident[0:P, 0:P])
                ins.then_inc(s_cT, 1)
            pe.wait_ge(s_rowsok, R_HS)
            for i in range(NT):
                if i >= 2:
                    pe.wait_ge(s_aggv, i - 1)
                for n0, n1 in ((0, BANK), (BANK, D)):
                    for k in range(NT):
                        ins = nc.tensor.matmul(ps[0:P, (i % 2) * 1024 + n0:(i % 2) * 1024 + n1],
                                               CT[:, k, i * P:(i + 1) * P], xf[:, k, n0:n1],
                                               start=k == 0, stop=k == NT - 1)
                ins.then_inc(s_agg, 1)
            fence(pe, F_GRAPH)

            def weighted_rows(j, m, width):
                for k in range(NT):
                    ins = nc.tensor.matmul(bank(6 + m % 2)[0:P, 0:width], probT[:, m % 5, k, :],
                                           head_cols(xfb[:, k, :], j, m // 5, width),
                                           start=k == 0, stop=k == NT - 1)
                ins.then_inc(s_pv, 1)

            def prob_transposed(m):
                for k in range(NT):
                    ins = nc.tensor.transpose(bank(4, 2)[0:P, k * 128:k * 128 + P], prob[:, m % 5, k * P:(k + 1) * P],
                                              ident[0:P, 0:P])
                ins.then_inc(s_pT, 1)

            pe.wait_ge(s_vl, NT)

            def parts(t, h, part):
                v = vst[t][:, bass.ds(h, 1), part:part + 2, :] if not isinstance(h, int) \
                    else vst[t][:, h:h + 1, part:part + 2, :]
                return v.rearrange("p a c e -> p (a c e)")

            def sides_transposed(h):
                for s, part in enumerate((1, 0, 2)):
                    for t in range(NT):
                        ins = nc.tensor.transpose(side_bank(s, t), parts(t, h, part), ident16[0:P, 0:P])
                ins.then_inc(s_sides, 1)

            def scores(j, m, last):
                q, t = divmod(m, 5)
                if t == 0:
                    pe.wait_ge(s_sidev, j * 2 + q + 1)
                if t == 4 and not (last and q == 1):
                    pe.wait_ge(s_sidev, j * 2 + q + 2)
                else:
                    pe.wait_ge(s_exp, j * 10 + m + (1, 1, 1, 2, 1)[t])
                for n0, n1 in ((0, BANK), (BANK, T)):
                    for s in (1, 2):
                        ins = nc.tensor.matmul(score_bank(m, n0, n1), sides[:, 0, q, t * P:(t + 1) * P],
                                               sides[:, s, q, n0:n1], start=s == 1, stop=s == 2)
                ins.then_inc(s_s, 1)

            def mha_transposed(j, m):
                n = j * 10 + m
                pe.wait_ge(s_exp, n + 3)
                pe.wait_ge(s_mTl, n + 1)
                for k in range(NT):
                    ins = nc.tensor.transpose(bank(4, 2)[0:P, k * 128:k * 128 + P],
                                              prob32[:, m % 2, k * P:(k + 1) * P], ident[0:P, 0:P])
                ins.then_inc(s_mT, 1)

            def weighted_chunk(h, q, k):
                if k == 0:
                    pe.wait_ge(s_mfin, h + 1)
                    pe.wait_ge(s_mTl, h * 5 + 6)
                v = parts(k, h, 1)
                for s in range(2):
                    for n0, n1 in ((0, BANK), (BANK, T)):
                        ins = nc.tensor.matmul(bank(6, 2)[:, n0:n1], v, pT[:, s, q, k, n0:n1],
                                               start=k == 0 and s == 0, stop=k == NT - 1 and s == 1)
                ins.then_inc(s_mpv, 1)

            def sum_back(h):
                pe.wait_ge(s_mout, h + 1)
                for t in range(NT):
                    ins = nc.tensor.matmul(bank(6)[0:P, t * HD:(t + 1) * HD], outT[:, t * P:(t + 1) * P],
                                           both[:, :], start=True, stop=True)
                ins.then_inc(s_mback, 1)

            def mha_turn(j, first, last):
                for m in range(10):
                    q, t = divmod(m, 5)
                    h = j * 2 + q
                    scores(j, m, last)
                    if t == 2 and not (last and q == 1):
                        pe.wait_ge(s_exp, j * 10 + m + 2)
                        sides_transposed(h + 1)
                    lagged(mha_transposed, j, m, 1, first)
                    if not (first and q == 0):
                        for k in ((), (0, 1), (2,), (3, 4), ())[t]:
                            weighted_chunk(h - 1, 1 - q, k)
                        if t == NT - 1:
                            sum_back(h - 1)

            sides_transposed(0)
            mha_turn(0, True, False)
            with pe.Fori(1, H // 2 - 1) as j:
                mha_turn(j, False, False)
            mha_turn(H // 2 - 1, False, True)
            mha_transposed(H // 2 - 1, 9)
            for k in range(NT):
                weighted_chunk(H - 1, 1, k)
            sum_back(H - 1)
            fence(pe, F_MHA)

            def route(layer, n_transposed, ok):
                pe.wait_ge(s_rowsok, ok)
                transpose_rows(xf)
                transposed(n_transposed)
                pe.wait_ge(s_small, 48)
                for t in range(NT):
                    for c in range(KC):
                        ins = nc.tensor.matmul(bank(0)[0:P, t * NE:(t + 1) * NE], tD[:, c, t * P:(t + 1) * P],
                                               gates[:, layer, c, :], start=c == 0, stop=c == KC - 1)
                ins.then_inc(s_lg, 1)
                pe.wait_ge(s_rd, 1 if layer == 0 else N_RD + 2 * N_ATT + 1)
                for t in range(NT + 1):
                    o = bank(0)[0:P, 64 + t * NE:64 + (t + 1) * NE] if t < NT else bank(0)[0:P, 128:128 + NE]
                    for k in range(min(t, NT)):
                        ins = nc.tensor.matmul(o, ones[0:P, 0:P], sm[:, 4, k, :], start=k == 0,
                                               stop=t == NT and k == NT - 1)
                    if t < NT:
                        ins = nc.tensor.matmul(o, tri[:, :], sm[:, 4, t, :], start=t == 0, stop=True)
                ins.then_inc(s_rk, 1)

            route(0, 2, R_XF0)
            fence(pe, F_ROUTE0)
            ffn_tensor(pe, ph_s, NG)
            fence(pe, F_SHARED)
            ffn_tensor(pe, ph_0, passes(pe))
            fence(pe, F_EXP0)
            pe.wait_ge(s_cm, 1)
            for t in range(NT):
                ins = nc.tensor.transpose(bank(0, 2)[0:NE + 1, t * 128:t * 128 + P], cmb[:, t, :], ident[0:P, 0:P])
            ins.then_inc(s_cmT, 1)
            pe.wait_ge(s_cmTv, 1)
            for t in range(NT):
                if t >= 2:
                    pe.wait_ge(s_add, t - 1)
                for n0, n1 in ((0, BANK), (BANK, D)):
                    ins = nc.tensor.matmul(ps[0:P, (1 + t % 2) * 1024 + n0:(1 + t % 2) * 1024 + n1],
                                           cmbT[:, t * P:(t + 1) * P], bout[:, n0:n1], start=True, stop=True)
                ins.then_inc(s_bo, 1)
            fence(pe, F_LAYER0)

            pe.wait_ge(s_rowsok, R_Z1)
            transpose_rows(z)
            transposed(3)
            pe.wait_ge(s_al, 16 * 6)
            for n in range(NT * KC):
                t, c = divmod(n, KC)
                if n >= 4:
                    pe.wait_ge(s_fta, n - 3)
                nc.tensor.matmul(bank(n % 4)[0:P, 0:256], tD[:, c, t * P:(t + 1) * P], wheads,
                                 start=True, stop=True).then_inc(s_ft, 1)
            pe.wait_ge(s_am, 1)
            for t in range(NT):
                ins = nc.tensor.transpose(bank(4, 2)[0:H, t * 128:t * 128 + P], a12[:, 0, t, 0:H],
                                          ident[0:P, 0:P])
            ins.then_inc(s_aT, 1)

            def source_term(h, q):
                pe.wait_ge(s_am, h + 2)
                pe.wait_ge(s_r, h * NT + NT)
                for n0, n1 in ((0, BANK), (BANK, T)):
                    ins = nc.tensor.matmul(ps[0:P, q * 1024 + n0:q * 1024 + n1], ones[0:H, 0:P],
                                           a1m[:, q, n0:n1], start=True, stop=True)
                ins.then_inc(s_ab, 1)

            pe.wait_ge(s_fta, NT * KC)
            source_term(0, 0)
            def gat_transposed(j, m):
                n = j * 10 + m
                pe.wait_ge(s_pc, n + 1)
                if m % 2:
                    pe.wait_ge(s_evv, j * 5 + m // 2 + 2)
                else:
                    pe.wait_ge(s_eva, j * 5 + m // 2 + 1)
                prob_transposed(m)

            def gat_rows(j, m):
                pe.wait_ge(s_eva if m % 2 else s_evv, j * 5 + m // 2 + 2)
                pe.wait_ge(s_pvv, j * 10 + m + 1)
                weighted_rows(j, m, HD + 1)

            def gat_turn(j, first):
                for m in range(10):
                    if m % 5 == 0:
                        source_term(j * 2 + m // 5 + 1, 1 - m // 5)
                    lagged(gat_transposed, j, m, 3, first)
                    lagged(gat_rows, j, m, 4, first)

            gat_turn(0, True)
            with pe.Fori(1, H // 2) as j:
                gat_turn(j, False)
            for m in range(10, 14):
                if m < 13:
                    gat_transposed(H // 2 - 1, m - 3)
                gat_rows(H // 2 - 1, m - 4)
            route(1, 4, R_XF1)
            fence(pe, F_GAT)
            fence(pe, F_ROUTE1)
            ffn_tensor(pe, ph_1, passes(pe))
            fence(pe, F_EXP1)


def kernel(x, src, dst, L0_gnn_W, L0_gnn_b, L0_ffn_norm1_w, L0_ffn_norm3_w, L0_ffn_gate_w, L0_ffn_w1, L0_ffn_b1,
           L0_ffn_w2, L0_ffn_b2, L0_ffn_w3, L0_ffn_b3, L0_ffn_fc1_w, L0_ffn_fc1_b, L0_ffn_fc2_w, L0_ffn_fc2_b,
           L1_gnn_W_fc, L1_gnn_attn_l, L1_gnn_attn_r, L1_gnn_W_res, L1_ffn_norm_w, L1_ffn_router_w,
           L1_ffn_gate_w, L1_ffn_up_w, L1_ffn_down_w):
    import numpy as np
    import concourse.bacc as bacc
    from concourse.bass_utils import run_bass_kernel_spmd

    def up_cols(w):
        w = np.asarray(w)
        lead = w.shape[:-2]
        w = w.reshape(*lead, w.shape[-2] // 128, 128, KC, 128)
        n = len(lead)
        w = w.transpose(*range(n), n, n + 3, n + 2, n + 1)
        return w.reshape(*w.shape[:n + 2], D)

    def down_rows(w):
        w = np.asarray(w)
        w = np.swapaxes(w, -1, -2)
        return w.reshape(*w.shape[:-2], w.shape[-2] // 128, 128, D)

    def bias_col(b):
        b = np.asarray(b)
        return b.reshape(*b.shape[:-1], b.shape[-1] // 128, 128, 1)

    b1s = bias_col(L0_ffn_fc1_b)
    arrays = {
        "x": np.asarray(x), "src": np.asarray(src), "dst": np.asarray(dst), "gnn_w": np.asarray(L0_gnn_W),
        "vecs": np.stack([np.asarray(v) for v in (L0_gnn_b, L0_ffn_norm1_w, L0_ffn_norm3_w, L1_ffn_norm_w)]),
        "gate0": np.asarray(L0_ffn_gate_w).T, "gate1": np.asarray(L1_ffn_router_w).T,
        "units0": np.concatenate([up_cols(L0_ffn_w1), up_cols(L0_ffn_w3), down_rows(L0_ffn_w2),
                                  bias_col(L0_ffn_b1), bias_col(L0_ffn_b3)], -1),
        "units_s": np.concatenate([up_cols(L0_ffn_fc1_w), down_rows(L0_ffn_fc2_w), b1s, b1s], -1),
        "units1": np.concatenate([up_cols(L1_ffn_gate_w), up_cols(L1_ffn_up_w), down_rows(L1_ffn_down_w)], -1),
        "bias_out": np.concatenate([np.asarray(L0_ffn_b2), np.asarray(L0_ffn_fc2_b)[None]], 0),
        "w_heads": np.stack([np.asarray(L1_gnn_W_fc).T, np.asarray(L1_gnn_W_res).T], 1),
        "attn_lr": np.stack([np.asarray(L1_gnn_attn_l).reshape(D), np.asarray(L1_gnn_attn_r).reshape(D)]),
    }
    arrays = {f"in_{k}": np.ascontiguousarray(v) for k, v in arrays.items()}
    nc = bacc.Bacc("TRN2", target_bir_lowering=False, num_devices=1)
    args = [nc.dram_tensor(k, v.shape, mybir.dt.from_np(v.dtype), kind="ExternalInput").ap()
            for k, v in arrays.items()]
    result = nc.dram_tensor("out_0", (T, D), F32, kind="ExternalOutput").ap()
    bass_gnn_moe_stack(nc, *args, result)
    r = run_bass_kernel_spmd(nc, [arrays], core_ids=[0])
    return r.results[0]["out_0"]
```

```python
import concourse.bass as bass
from concourse import mybir
from contextlib import ExitStack

F32 = mybir.dt.float32
F16 = mybir.dt.float16
BF16 = mybir.dt.bfloat16
I32 = mybir.dt.int32
ALU = mybir.AluOpType
ACT = mybir.ActivationFunctionType
AX = mybir.AxisListType

T, D, H = 625, 768, 12
HD = D // H
EDGES = 20625
NE = 8
I0, IS, I1 = 1024, 2048, 1536

P, NT = 125, 5
KC = D // 128
EC = EDGES // P
EU = 3
B = 176
NPMAX = NE + (2 * T - NE) // B
NTAB = NPMAX + 1
GS = 214
NG = 3
RING = 4
WS = 64.0
NEG = -1e30
BANK = 512

C_ZERO, C_ALL = 2, 11
F_GRAPH, F_MHA, F_ROUTE0, F_SHARED, F_EXP0, F_LAYER0, F_GAT, F_ROUTE1, F_EXP1 = range(1, 10)
R_Z0, R_HS, R_XN0, R_XF0, R_Z1, R_XF1 = range(1, 7)
N_RD = 1


class Phase:

    def __init__(self, sem, name, ic, gated, bias, n, rows):
        self.ic, self.gated, self.bias, self.n, self.rows = ic, gated, bias, n, rows
        self.lead = 1 if gated else 0
        self.wide = D * (3 if gated else 2)
        self.cols = self.wide + (2 if bias else 0)
        self.raw = [sem(f"{name}_unit_loaded{r}") for r in range(RING)]
        self.hi = sem(f"{name}_unit_high")
        self.lo = sem(f"{name}_unit_low")
        self.up = sem(f"{name}_up_done")
        self.silu = sem(f"{name}_silu_done")
        self.hseq = sem(f"{name}_hidden_steps")
        self.h = sem(f"{name}_hidden_split")
        self.down = sem(f"{name}_down_done")
        self.xrows = sem(f"{name}_rows_loaded")
        self.xt = sem(f"{name}_rows_transposed")
        self.xhi = sem(f"{name}_x_high")
        self.xlo = sem(f"{name}_x_low")
        self.ya = sem(f"{name}_sums_out0")
        self.yv = sem(f"{name}_sums_out1")
        self.yt = sem(f"{name}_out_transposed")
        self.yr = sem(f"{name}_out_rows")
        self.stored = sem(f"{name}_out_stored")
        self.yfree = sem(f"{name}_out_free")


def bass_gnn_moe_stack(nc, x, src, dst, gnn_w, vecs, gate0, gate1, units0, units_s, units1,
                       bias_out, w_heads, attn_lr, out):
    ctx = ExitStack()
    with ctx:
        def sb(name, shape, dt=F32):
            return ctx.enter_context(nc.sbuf_tensor(name, shape, dt))

        def sem(name):
            return ctx.enter_context(nc.semaphore(name))

        x_slots = nc.dram_tensor("x_slots", [(NTAB + 1) * B, D], F32, kind="Internal").ap()
        y_slots = nc.dram_tensor("y_slots", [(NPMAX + 1) * B, D], F32, kind="Internal").ap()
        x_shared = nc.dram_tensor("x_shared", [(NG + 1) * GS, D], F32, kind="Internal").ap()
        y_shared = nc.dram_tensor("y_shared", [(NG + 1) * GS, D], F32, kind="Internal").ap()

        xres = sb("xres", [P, NT, D])
        z = sb("z", [P, NT, D])
        xf = sb("xf", [P, NT, D])
        big = sb("big", [128, 7500])
        ext = sb("ext", [128, 6500])
        cds = sb("cds", [P, NT, T])
        mask = sb("mask", [P, NT, T], BF16)
        raw01 = sb("raw01", [128, 2, 3 * D + 2])
        wh = sb("wh", [128, RING, 3 * D], F16)
        wl = sb("wl", [128, RING, 3 * D], F16)
        ident = sb("ident", [128, 128])
        ones = sb("ones", [128, 128])
        tri = sb("tri", [P, P])
        vec = sb("vec", [P, 2, D])
        gates = sb("gates", [128, 2, KC, NE])
        bout = sb("bout", [NE + 1, D])
        edges_i = sb("edges_i", [P, 2, EC], I32)
        edges_f = sb("edges_f", [P, 2, EC])
        st = sb("st", [P, NT, 2, 6])
        mv = sb("mv", [P, NT, 2])
        rs = sb("rs", [P, 4, NT])
        dinv = sb("dinv", [P, NT])
        sm = sb("sm", [P, 16, NT, NE])
        s8 = sb("s8", [P, 8, NE])
        cst8 = sb("cst8", [P, 3, NT, NE])
        tabf = sb("tabf", [1, 3, NTAB, NE])
        tab1 = sb("tab1", [1, 4, NTAB + 1])
        tabi = sb("tabi", [1, 2, NTAB + 1], I32)
        slots_f = sb("slots_f", [P, 2, NT])
        slots_i = sb("slots_i", [P, 2, NT], I32)
        wts = sb("wts", [P, 2, NT])
        dot = sb("dot", [1, 1])
        cmb = sb("cmb", [P, NT, NE + 1])
        cmbT = sb("cmbT", [NE + 1, T])
        cols = sb("cols", [P, 12, NT])
        a12 = sb("a12", [P, 2, NT, H + 1])

        region = lambda t, a, n: t[:, a:a + n]
        tD = region(big, 0, KC * T).rearrange("p (c n) -> p c n", c=KC)
        CT = big[0:P, 3750:3750 + NT * T].rearrange("p (t n) -> p t n", t=NT)
        a1T = big[0:H, 3750:4375]
        a1m = big[0:H, 4375:5625].rearrange("p (s n) -> p s n", s=2)
        xrows = region(big, 0, 2 * D).rearrange("p (t d) -> p t d", t=2)
        yrows = region(big, 1536, 2 * D).rearrange("p (t d) -> p t d", t=2)
        xTh = region(big, 3072, 768).bitcast(F16).rearrange("p (c n) -> p c n", c=KC)
        xTl = region(big, 3840, 768).bitcast(F16).rearrange("p (c n) -> p c n", c=KC)
        sbuf = region(big, 4608, 512).rearrange("p (s n) -> p s n", s=2)
        tbuf = region(big, 5120, 512).rearrange("p (s n) -> p s n", s=2)
        hh = region(big, 5632, 256).bitcast(F16).rearrange("p (s n) -> p s n", s=2)
        hl = region(big, 5888, 256).bitcast(F16).rearrange("p (s n) -> p s n", s=2)
        bsm = region(big, 6144, 8).rearrange("p (s n) -> p s n", s=RING)
        wg = region(ext, 0, KC * D).rearrange("p (c n) -> p c n", c=KC)
        hot = ext[0:P, 4608:4608 + 1875].bitcast(F16).rearrange("p (s a n) -> p s a n", s=EU, a=2)
        vst = [(wh if t < 3 else wl)[0:P, :, :].rearrange("p a n -> p (a n)")
               [:, (t % 3) * H * 256:(t % 3 + 1) * H * 256].rearrange("p (h c e) -> p h c e", h=H, c=4)
               for t in range(NT)]
        sides = region(big, 3840, 1875).bitcast(F16).rearrange("p (s q n) -> p s q n", s=3, q=2)
        outT = region(big, 5715, T)
        outn = big[0:P, 6340:6340 + NT * HD].rearrange("p (t e) -> p t e", t=NT)
        pT = ext[0:P, 0:6250].bitcast(F16).rearrange("p (s q k n) -> p s q k n", s=2, q=2, k=NT)
        ident16 = sb("ident16", [128, 128], F16)
        both = sb("both", [128, HD])
        raw32 = raw01[0:P, :, :].rearrange("p a n -> p (a n)")
        wl32 = wl[:, :, :].rearrange("p a n -> p (a n)").bitcast(F32)
        prob = raw32[:, 0:NT * T].rearrange("p (s n) -> p s n", s=NT)
        slow = raw32[:, NT * T:(NT + 2) * T].rearrange("p (s n) -> p s n", s=2)
        terms = [wl32[0:P, 0:NT * T].rearrange("p (s n) -> p s n", s=NT),
                 big[0:P, 0:NT * T].rearrange("p (s n) -> p s n", s=NT)]
        values = wh[0:P, :, :].rearrange("p a n -> p (a n)")[:, 0:NT * 2 * D]\
            .rearrange("p (t h e) -> p t h e", t=NT, h=H)
        wheads = wl32[:, 640:896]
        alr = ext[0:P, 0:2 * D].rearrange("p (a n) -> p a n", a=2)
        prod = ext[0:P, 1536:1536 + 2 * D].rearrange("p (a n) -> p a n", a=2)
        rows = [[(big if t < 4 else ext)[0:P, (t % 4 * 2 + k) * D:(t % 4 * 2 + k + 1) * D] for k in range(2)]
                for t in range(NT)]
        raw = [raw01[:, 0, :], raw01[:, 1, :], region(ext, 0, 3 * D + 2), region(ext, 2400, 3 * D + 2)]
        iota16 = sb("iota16", [P, T], F16)

        ps = ctx.enter_context(nc.psum_tensor("ps", [128, 8 * BANK], F32))

        def bank(b, n=1):
            return ps[:, b * BANK:(b + n) * BANK]

        def tiles5(two_banks, parts):
            return two_banks[0:parts, 0:NT * 128].rearrange("p (t n) -> p t n", t=NT)[:, :, 0:P]

        prob32 = prob

        def heads_twice(t):
            v = xf[:, t, :].rearrange("p (h e) -> p h e", h=H)
            return v.unsqueeze(2).to_broadcast([P, H, 2, HD])

        def score_bank(m, n0=0, n1=T):
            at = (0, 1, 0, 0, 1)[m % 5] * 1024
            return ps[0:P, at + n0:at + n1]

        def side_bank(s, t=None):
            v = bank(2, 2).bitcast(F16)[:, s * NT * 128:(s + 1) * NT * 128].rearrange("p (t n) -> p t n", t=NT)
            return v[:, :, 0:P] if t is None else v[:, t, 0:P]

        def yT(ph):
            return region(big, 6152, KC * ph.n).rearrange("p (c n) -> p c n", c=KC)

        def y_bank(b, n, ph):
            return bank(b, n).rearrange("p (c n) -> p c n", c=2 * n)[:, :, 0:ph.n]

        s_const = sem("s_const")
        s_fence = sem("s_fence")
        s_x = sem("s_x")
        s_edge = sem("s_edge")
        s_wg = sem("s_wg")
        s_vec = [sem(f"s_vec{i}") for i in range(2)]
        s_small = sem("s_small")
        s_zero = sem("s_zero")
        s_v = sem("s_v")
        s_sq = sem("s_sq")
        s_var = sem("s_var")
        s_hot = sem("s_hot")
        s_cmm = sem("s_cmm")
        s_ct = sem("s_ct")
        s_ctv = sem("s_ctv")
        s_cT = sem("s_cT")
        s_cda = sem("s_cda")
        s_cdv = sem("s_cdv")
        s_rowsok = sem("s_rowsok")
        s_tp = sem("s_tp")
        s_tpe = sem("s_tpe")
        s_hmm = sem("s_hmm")
        s_hev = sem("s_hev")
        s_agg = sem("s_agg")
        s_aggv = sem("s_aggv")
        s_vh = sem("s_vh")
        s_vl = sem("s_vl")
        s_sides = sem("s_sides")
        s_sidea = sem("s_sidea")
        s_sidev = sem("s_sidev")
        s_mT = sem("s_mT")
        s_mTh = sem("s_mTh")
        s_mTl = sem("s_mTl")
        s_mpv = sem("s_mpv")
        s_mout = sem("s_mout")
        s_mback = sem("s_mback")
        s_mrec = sem("s_mrec")
        s_mfin = sem("s_mfin")
        s_madd = sem("s_madd")
        s_s = sem("s_s")
        s_mx = sem("s_mx")
        s_exp = sem("s_exp")
        s_pT = sem("s_pT")
        s_pv = sem("s_pv")
        s_rd = sem("s_rd")
        s_lg = sem("s_lg")
        s_lge = sem("s_lge")
        s_lx = sem("s_lx")
        s_sel = sem("s_sel")
        s_rk = sem("s_rk")
        s_slot = sem("s_slot")
        s_scat = sem("s_scat")
        s_cmT = sem("s_cmT")
        s_cmTv = sem("s_cmTv")
        s_bo = sem("s_bo")
        s_bov = sem("s_bov")
        s_gat = [sem(f"s_gat{t}") for t in range(NT)]
        s_ys = sem("s_ys")
        s_joined = sem("s_joined")
        s_add = sem("s_add")
        s_wh = sem("s_wh")
        s_ft = sem("s_ft")
        s_ftv = sem("s_ftv")
        s_al = sem("s_al")
        s_aT = sem("s_aT")
        s_am = sem("s_am")
        s_ab = sem("s_ab")
        s_gm = sem("s_gm")
        s_gb = sem("s_gb")
        s_rm = sem("s_rm")
        s_ge = sem("s_ge")
        s_pc = sem("s_pc")
        s_gseq = sem("s_gseq")
        s_done = sem("s_done")
        s_tpa = sem("s_tpa")
        s_fta = sem("s_fta")
        s_gs = sem("s_gs")
        s_gvh = sem("s_gvh")
        s_gvl = sem("s_gvl")
        s_gTh = sem("s_gTh")
        s_gTl = sem("s_gTl")
        s_gout = sem("s_gout")
        s_gback = sem("s_gback")
        s_gfin = sem("s_gfin")
        s_gadd = sem("s_gadd")
        s_cm = sem("s_cm")
        ph_s = Phase(sem, "shared", IS // 128, False, True, GS, x_shared)
        ph_0 = Phase(sem, "layer0", I0 // 128, True, True, B, x_slots)
        ph_1 = Phase(sem, "layer1", I1 // 128, True, False, B, x_slots)
        units = {id(ph_s): units_s, id(ph_0): units0, id(ph_1): units1}
        outs = {id(ph_s): y_shared, id(ph_0): y_slots, id(ph_1): y_slots}

        block = ctx.enter_context(nc.Block())

        ENGINES = 4

        def fence(eng, k):
            if k > 1:
                eng.wait_ge(s_fence, ENGINES * (k - 1))
            eng.drain().then_inc(s_fence, 1)
            eng.wait_ge(s_fence, ENGINES * k)

        def passes(eng):
            return eng.value_load(tabi[0:1, 0:1, NTAB:NTAB + 1].rearrange("p a n -> p (a n)"),
                                  min_val=NE, max_val=NPMAX)

        def ffn_sync(sp, ph, n_pass, routed):
            def expert(i):
                if not routed:
                    return 0
                return sp.value_load(tabi[0:1, 0:1, bass.ds(i, 1)].rearrange("p a n -> p (a n)"),
                                     min_val=0, max_val=NE - 1)

            def load(i, e, u):
                g = i * ph.ic + u
                sp.wait_ge(ph.hi, g + 1)
                sp.wait_ge(ph.lo, g + 1)
                w = units[id(ph)]
                unit = w[bass.ds(e, 1), u, :, :].rearrange("a p n -> p (a n)") if routed else w[u, :, :]
                sp.dma_start(raw[u % RING][:, 0:ph.cols], unit).then_inc(ph.raw[u % RING], 16)

            with sp.Fori(0, n_pass) as i:
                e = expert(i)
                for u in range(ph.ic):
                    load(i, e, u)
            e = expert(n_pass)
            for u in range(2):
                load(n_pass, e, u)

        def ffn_pool(pool, ph, n_pass, meanwhile=None):
            ahead = ph.lead

            def rows_in(i):
                i = i + ahead
                source = ph.rows[bass.ds(i * ph.n, ph.n), :] if not isinstance(i, int) \
                    else ph.rows[i * ph.n:(i + 1) * ph.n, :]
                pool.dma_start(xrows[0:ph.n // 2, :, :],
                               source.rearrange("(t p) d -> p t d", t=2)).then_inc(ph.xrows, 16)

            def rows_out(i):
                pool.wait_ge(ph.yr, i * 3 + 4)
                pool.dma_start(outs[id(ph)][bass.ds(i * ph.n, ph.n), :].rearrange("(t p) d -> p t d", t=2),
                               yrows[0:ph.n // 2, :, :]).then_inc(ph.stored, 16)
                pool.wait_ge(ph.stored, i * 16 + 16)
                pool.sem_inc(ph.yfree, 1)

            rows_in(0)
            if meanwhile is not None:
                meanwhile()
            with pool.Fori(0, n_pass) as i:
                pool.wait_ge(ph.xt, i * 3 + 3)
                rows_in(i + 1)
                rows_out(i)

            rows_out(n_pass)

        def ffn_scalar(act, ph, n_pass):
            half = ph.n // 2

            def high(i, u):
                g = i * ph.ic + u
                act.wait_ge(ph.raw[u % RING], i * (16 * ph.ic // RING) + 16 * (u // RING) + 16)
                act.wait_ge(ph.down, g + 1)
                if ph.bias:
                    nc.scalar.activation(bsm[:, u % RING, 0:1], raw[u % RING][:, ph.wide:ph.wide + 1], ACT.Copy)
                nc.scalar.activation(wh[:, u % RING, 0:ph.wide], raw[u % RING][:, 0:ph.wide], ACT.Copy,
                                     scale=WS).then_inc(ph.hi, 1)

            def x_high(i):
                for k in range(3):
                    act.wait_ge(ph.xt, i * 3 + k + 1)
                    src_ = bank(6 + k % 2).rearrange("p (c n) -> p c n", c=2)[:, :, 0:ph.n]
                    nc.scalar.activation(xTh[:, 2 * k:2 * k + 2, 0:ph.n], src_, ACT.Copy).then_inc(ph.xhi, 1)

            def rows_out(i, r):
                act.wait_ge(ph.yt, i * 3 + r + 1)
                act.wait_ge(ph.yfree, i + 1)
                nc.scalar.activation(yrows.rearrange("p t d -> p (t d)")[0:half, r * BANK:(r + 1) * BANK],
                                     bank(3)[0:half, :], ACT.Copy).then_inc(ph.yr, 1)

            x_high(0)
            high(0, 0)
            high(0, 1)
            with act.Fori(0, n_pass) as i:
                for u in range(ph.ic):
                    g = i * ph.ic + u
                    high(i, u + 2)
                    act.wait_ge(ph.up, g + 1)
                    if ph.bias:
                        act.wait_ge(ph.hi, g + 1 + RING)
                        bias = bsm[:, u % RING, 0:1]
                    else:
                        bias = 0.0
                    a = bank(4 + u % 2)[:, 0:ph.n]
                    nc.scalar.activation(sbuf[:, u % 2, 0:ph.n], a, ACT.Silu, bias=bias,
                                         scale=1.0 / WS).then_inc(ph.silu, 1)
                    if 1 <= u <= 3:
                        rows_out(i, u - 1)
                x_high(i + 1)
                act.wait_ge(ph.down, (i + 1) * ph.ic + RING)
                act.wait_ge(ph.yt, i * 3 + 3)
                nc.scalar.activation(yT(ph)[:, 0:4, :], y_bank(0, 2, ph), ACT.Copy,
                                     scale=1.0 / WS).then_inc(ph.ya, 1)
            for r in range(3):
                rows_out(n_pass, r)

        def ffn_vector(dve, ph, n_pass):
            def low(i, u):
                g = i * ph.ic + u
                dve.wait_ge(ph.hi, g + 1 + RING)
                if ph.bias and ph.gated:
                    nc.vector.tensor_scalar(bsm[:, u % RING, 1:2], raw[u % RING][:, ph.wide + 1:ph.wide + 2],
                                            WS, None, ALU.mult)
                nc.vector.scalar_tensor_tensor(
                    out=wl[:, u % RING, 0:ph.wide], in0=raw[u % RING][:, 0:ph.wide], scalar=WS,
                    in1=wh[:, u % RING, 0:ph.wide], op0=ALU.mult, op1=ALU.subtract).then_inc(ph.lo, 1)

            def x_low(i):
                for k in range(3):
                    dve.wait_ge(ph.xhi, i * 3 + k + 1)
                    src_ = bank(6 + k % 2).rearrange("p (c n) -> p c n", c=2)[:, :, 0:ph.n]
                    nc.vector.tensor_tensor(xTl[:, 2 * k:2 * k + 2, 0:ph.n], src_,
                                            xTh[:, 2 * k:2 * k + 2, 0:ph.n], ALU.subtract).then_inc(ph.xlo, 1)

            nc.vector.memset(yT(ph), 0.0).then_inc(ph.yv, 1)
            x_low(0)
            low(0, 0)
            low(0, 1)
            with dve.Fori(0, n_pass) as i:
                for u in range(ph.ic):
                    g = i * ph.ic + u
                    low(i, u + 2)
                    dve.wait_ge(ph.silu, g + 1)
                    s_ = sbuf[:, u % 2, 0:ph.n]
                    h_, l_ = hh[:, u % 2, 0:ph.n], hl[:, u % 2, 0:ph.n]
                    if ph.gated:
                        gate = bank(4 + u % 2)[:, 256:256 + ph.n]
                        t_ = tbuf[:, u % 2, 0:ph.n]
                        if ph.bias:
                            dve.wait_ge(ph.lo, g + 1 + RING)
                            nc.vector.scalar_tensor_tensor(out=t_, in0=gate, scalar=bsm[:, u % RING, 1:2],
                                                           in1=s_, op0=ALU.add, op1=ALU.mult).then_inc(ph.hseq, 1)
                        else:
                            nc.vector.tensor_tensor(t_, gate, s_, ALU.mult).then_inc(ph.hseq, 1)
                        dve.wait_ge(ph.hseq, g * 2 + 1)
                        nc.vector.tensor_scalar(h_, t_, 1.0 / WS, None, ALU.mult).then_inc(ph.hseq, 1)
                        dve.wait_ge(ph.hseq, g * 2 + 2)
                        nc.vector.scalar_tensor_tensor(out=l_, in0=t_, scalar=1.0 / WS, in1=h_, op0=ALU.mult,
                                                       op1=ALU.subtract).then_inc(ph.h, 1)
                    else:
                        nc.vector.tensor_copy(h_, s_).then_inc(ph.hseq, 1)
                        dve.wait_ge(ph.hseq, g + 1)
                        nc.vector.tensor_tensor(l_, s_, h_, ALU.subtract).then_inc(ph.h, 1)
                x_low(i + 1)
                dve.wait_ge(ph.down, (i + 1) * ph.ic + RING)
                dve.wait_ge(ph.yt, i * 3 + 3)
                nc.vector.tensor_scalar(yT(ph)[:, 4:6, :], y_bank(2, 1, ph), 1.0 / WS, None,
                                        ALU.mult).then_inc(ph.yv, 1)

        def ffn_tensor(pe, ph, n_pass):
            half = ph.n // 2

            def three(out_, pairs, n_all, n, last=False):
                ins = None
                for k, (l_, r_) in enumerate(pairs):
                    ins = nc.tensor.matmul(out_, l_, r_, start=(n == 0 and k == 0),
                                           stop=(n == n_all - 1 and k == len(pairs) - 1))
                return ins

            def rows_transposed(k, wait):
                if wait is not None:
                    pe.wait_ge(ph.xlo, wait)
                for c in range(2):
                    for t in range(2):
                        ins = nc.tensor.transpose(
                            bank(6 + k % 2)[:, c * 256 + t * half:c * 256 + (t + 1) * half],
                            xrows[0:half, t, (2 * k + c) * 128:(2 * k + c + 1) * 128], ident[0:half, 0:half])
                ins.then_inc(ph.xt, 1)

            def up(i, u):
                g = i * ph.ic + u
                pe.wait_ge(ph.lo, g + 1 + RING)
                pe.wait_ge(ph.h, g + 1)
                for m in range(2 if ph.gated else 1):
                    for c in range(KC):
                        w0 = m * D + c * 128
                        ins = three(bank(4 + u % 2)[:, m * 256:m * 256 + ph.n],
                                    [(wh[:, u % RING, w0:w0 + 128], xTh[:, c, 0:ph.n]),
                                     (wh[:, u % RING, w0:w0 + 128], xTl[:, c, 0:ph.n]),
                                     (wl[:, u % RING, w0:w0 + 128], xTh[:, c, 0:ph.n])], KC, c)
                ins.then_inc(ph.up, 1)

            def down(i, u, first, last):
                g = i * ph.ic + u
                if first:
                    pe.wait_ge(ph.ya, i + 1)
                    pe.wait_ge(ph.yv, i + 1)
                pe.wait_ge(ph.h, g + 3)
                w0 = ph.wide - D
                hs, ls = hh[:, u % 2, 0:ph.n], hl[:, u % 2, 0:ph.n]
                for c in range(KC):
                    o = ps[:, c * 256:c * 256 + ph.n]
                    w_ = slice(w0 + c * 128, w0 + (c + 1) * 128)
                    for k, (r_, l_) in enumerate(((hs, wh), (ls, wh), (hs, wl))):
                        ins = nc.tensor.matmul(o, l_[:, u % RING, w_], r_, start=first and k == 0 and c % 2 == 0,
                                               stop=last and k == 2, skip_group_check=True)
                ins.then_inc(ph.down, 1)

            def out_transposed(i, r):
                if r == 0:
                    pe.wait_ge(ph.ya, i + 1)
                    pe.wait_ge(ph.yv, i + 1)
                pe.wait_ge(ph.yr, i * 3 + r + 1)
                for b in range(4):
                    t, c = divmod(4 * r + b, KC)
                    ins = nc.tensor.transpose(bank(3)[0:half, b * 128:(b + 1) * 128],
                                              yT(ph)[:, c, t * half:(t + 1) * half], ident[:, :])
                ins.then_inc(ph.yt, 1)

            pe.wait_ge(ph.xrows, 16)
            rows_transposed(0, None)
            rows_transposed(1, None)
            rows_transposed(2, 1)
            with pe.Fori(0, n_pass) as i:
                pe.wait_ge(ph.xlo, i * 3 + 3)
                for u in range(ph.ic):
                    up(i, u)
                    if u:
                        down(i, u - 1, u == 1, False)
                    if 1 <= u <= 3:
                        out_transposed(i, u - 1)
                pe.wait_ge(ph.xrows, i * 16 + 32)
                rows_transposed(0, i * 3 + 3)
                rows_transposed(1, None)
                down(i, ph.ic - 1, False, True)
                rows_transposed(2, i * 3 + 4)
            for r in range(3):
                out_transposed(n_pass, r)

        def lagged(op, j, m, lag, first):
            if m >= lag:
                op(j, m - lag)
            elif not first:
                op(j - 1, m - lag + 10)

        @block.sync
        def _(sp):
            sp.dma_start(xres[:, :, :], x.rearrange("(t p) d -> p t d", p=P)).then_inc(s_x, 16)
            sp.dma_start(edges_i[:, 0, :], src.rearrange("(p c) -> p c", p=P)).then_inc(s_edge, 16)
            sp.dma_start(edges_i[:, 1, :], dst.rearrange("(p c) -> p c", p=P)).then_inc(s_edge, 16)
            sp.dma_start(wg[:, :, :], gnn_w.rearrange("(c p) n -> p c n", p=128)).then_inc(s_wg, 16)
            for v in range(2):
                sp.dma_start(vec[:, v, :], vecs[v, :].partition_broadcast(P)).then_inc(s_vec[v], 16)
            sp.dma_start(gates[:, 0, :, :], gate0.rearrange("(c p) e -> p c e", p=128)).then_inc(s_small, 16)
            sp.dma_start(gates[:, 1, :, :], gate1.rearrange("(c p) e -> p c e", p=128)).then_inc(s_small, 16)
            sp.dma_start(bout[:, :], bias_out).then_inc(s_small, 16)
            sp.wait_ge(s_const, C_ZERO)
            sp.dma_start(x_slots.rearrange("(t p) d -> p t d", p=B // 2),
                         raw01[0:B // 2, 0:1, 0:D].to_broadcast([B // 2, 2 * NTAB + 2, D])).then_inc(s_zero, 16)
            sp.dma_start(x_shared.rearrange("(t p) d -> p t d", p=GS // 2),
                         raw01[0:GS // 2, 0:1, 0:D].to_broadcast([GS // 2, 2 * NG + 2, D])).then_inc(s_zero, 16)
            sp.dma_start(y_slots[(NE + 1) * B:(NPMAX + 1) * B, :].rearrange("(t p) d -> p t d", p=B // 2),
                         raw01[0:B // 2, 0:1, 0:D].to_broadcast([B // 2, 2 * (NPMAX - NE), D])).then_inc(s_zero, 16)
            sp.wait_ge(s_zero, 48)

            sp.wait_ge(s_fence, ENGINES * F_GRAPH)
            sp.dma_start(vec[:, 0, :], vecs[2, :].partition_broadcast(P)).then_inc(s_vec[0], 16)
            sp.wait_ge(s_fence, ENGINES * F_MHA)
            sp.dma_start(vec[:, 1, :], vecs[3, :].partition_broadcast(P)).then_inc(s_vec[1], 16)
            sp.wait_ge(s_rowsok, R_XF0)
            sp.dma_start(x_shared[0:T, :].rearrange("(t p) d -> p t d", p=P), xf[:, :, :]).then_inc(s_lx, 16)
            ffn_sync(sp, ph_s, NG, False)
            sp.wait_ge(s_fence, ENGINES * F_SHARED)
            sp.dma_start(xf[:, :, :], y_shared[GS:GS + T, :].rearrange("(t p) d -> p t d", p=P)).then_inc(s_ys, 16)
            ffn_sync(sp, ph_0, passes(sp), True)
            sp.wait_ge(s_wh, 1)
            for q in range(2):
                for m in range(2):
                    sp.dma_start(wheads[64 * q:64 * q + 64, 128 * m + 64 * q:128 * m + 64 * q + 64],
                                 w_heads[:, m, :]).then_inc(s_al, 16)
            for a in range(2):
                sp.dma_start(alr[:, a, :], attn_lr[a, :].partition_broadcast(P)).then_inc(s_al, 16)
            sp.wait_ge(s_fence, ENGINES * F_ROUTE1)
            ffn_sync(sp, ph_1, passes(sp), True)
            for t in range(NT):
                sp.wait_ge(s_add, NT + t + 1)
                sp.dma_start(out[t * P:(t + 1) * P, :], xres[:, t, :]).then_inc(s_done, 16)
            sp.wait_ge(s_done, 16 * NT)

        @block.gpsimd
        def _(pool):
            for ph in (ph_s, ph_0, ph_1):
                pool.sem_inc(ph.hi, RING)
                pool.sem_inc(ph.lo, RING)
                pool.sem_inc(ph.down, RING)
                pool.sem_inc(ph.h, 2)
                pool.sem_inc(ph.ya, 1)
                pool.sem_inc(ph.yr, 1)
                pool.sem_inc(ph.yfree, 1)
            pool.sem_inc(s_pT, NT)
            for s_ in (s_exp, s_rm):
                pool.sem_inc(s_, 2)
            for s_ in (s_mTl, s_mfin, s_madd, s_gTl, s_gfin, s_gadd):
                pool.sem_inc(s_, 1)
            for s_ in (s_mpv, s_pv):
                pool.sem_inc(s_, 2 * NT)
            nc.gpsimd.iota(iota16[:, :], pattern=[[1, T]], base=0, channel_multiplier=0,
                           allow_small_or_imprecise_dtypes=True).then_inc(s_const, 1)
            nc.gpsimd.memset(raw01[:, 0, 0:D], 0.0).then_inc(s_const, 1)
            nc.gpsimd.memset(ident[:, :], 0.0).then_inc(s_const, 1)
            nc.gpsimd.memset(ones[:, :], 1.0).then_inc(s_const, 1)
            pool.wait_ge(s_const, 4)
            nc.gpsimd.affine_select(out=ident[:, :], in_=ident[:, :], compare_op=ALU.not_equal, fill=1.0, base=0,
                                    pattern=[[-1, 128]], channel_multiplier=1).then_inc(s_const, 1)
            nc.gpsimd.affine_select(out=tri[:, :], in_=ones[0:P, 0:P], compare_op=ALU.is_gt, fill=0.0, base=0,
                                    pattern=[[1, P]], channel_multiplier=-1).then_inc(s_const, 1)
            for k, (base, step) in enumerate(((0, 1), (B, B), ((NE - 1) * B, -B))):
                nc.gpsimd.iota(cst8[:, k, :, :], pattern=[[0, NT], [step, NE]], base=base, channel_multiplier=0,
                               allow_small_or_imprecise_dtypes=True).then_inc(s_const, 1)
            nc.gpsimd.iota(tabf[:, 0, :, :], pattern=[[1, NTAB], [0, NE]], base=-NE, channel_multiplier=0,
                           allow_small_or_imprecise_dtypes=True).then_inc(s_const, 1)
            nc.gpsimd.iota(tab1[:, 0, :], pattern=[[1, NTAB + 1]], base=0, channel_multiplier=0,
                           allow_small_or_imprecise_dtypes=True).then_inc(s_const, 1)

            def scatter(layer):
                pool.wait_ge(s_slot, layer + 1)
                pool.wait_ge(s_zero, 48)
                for k in range(2):
                    for t in range(NT):
                        pool.indirect_dma_start(
                            out=x_slots, out_offset=bass.IndirectOffsetOnAxis(ap=slots_i[:, k, t:t + 1], axis=0),
                            in_=xf[:, t, :], in_offset=None).then_inc(s_scat, 16)
                pool.wait_ge(s_scat, (layer + 1) * 16 * 2 * NT)

            def gather():
                for t in range(NT):
                    for k in range(2):
                        pool.indirect_dma_start(
                            out=rows[t][k], out_offset=None, in_=y_slots,
                            in_offset=bass.IndirectOffsetOnAxis(ap=slots_i[:, k, t:t + 1], axis=0)
                        ).then_inc(s_gat[t], 16)

            def join(layer):
                if layer == 0:
                    pool.wait_ge(s_ys, 16)
                    for t in range(NT):
                        nc.gpsimd.tensor_tensor(z[:, t, :], z[:, t, :], xf[:, t, :], ALU.add).then_inc(s_joined, 1)
                for t in range(NT):
                    pool.wait_ge(s_joined, t + 1 if layer == 0 else 2 * NT)
                    nc.gpsimd.tensor_tensor(xres[:, t, :], xres[:, t, :], z[:, t, :], ALU.add)\
                        .then_inc(s_joined, 1)

            fence(pool, F_GRAPH)
            with pool.Fori(0, H) as h:
                pool.wait_ge(s_mfin, h + 2)
                at = z[:, :, bass.ds(h * HD, HD)]
                nc.gpsimd.tensor_tensor(at, at, outn, ALU.add).then_inc(s_madd, 1)
            fence(pool, F_MHA)
            pool.wait_ge(s_lx, 16)
            scatter(0)
            fence(pool, F_ROUTE0)
            ffn_pool(pool, ph_s, NG)
            fence(pool, F_SHARED)
            ffn_pool(pool, ph_0, passes(pool), lambda: join(0))
            fence(pool, F_EXP0)
            gather()
            fence(pool, F_LAYER0)

            def head_added(h):
                pool.wait_ge(s_gfin, h + 2)
                at = z[:, :, bass.ds(h * HD, HD)] if not isinstance(h, int) else z[:, :, h * HD:(h + 1) * HD]
                nc.gpsimd.tensor_tensor(at, at, outn, ALU.add).then_inc(s_gadd, 1)

            def gat_turn(j, first):
                for m in range(10):
                    q, t = divmod(m, 5)
                    pool.wait_ge(s_rm, j * 10 + m + 3)
                    nc.gpsimd.tensor_tensor(prob[:, m % 5, :], prob[:, m % 5, :], cds[:, m % 5, :],
                                            ALU.mult).then_inc(s_pc, 1)
                    if t == 2 and not first:
                        head_added(j * 2 + q - 2)

            gat_turn(0, True)
            with pool.Fori(1, H // 2) as j:
                gat_turn(j, False)
            head_added(H - 2)
            head_added(H - 1)
            fence(pool, F_GAT)
            scatter(1)
            fence(pool, F_ROUTE1)
            ffn_pool(pool, ph_1, passes(pool), lambda: join(1))
            fence(pool, F_EXP1)
            gather()

        @block.scalar
        def _(act):
            count = {"sq": 0, "tpa": 0}

            def root():
                count["sq"] += 1
                act.wait_ge(s_var, count["sq"])
                nc.scalar.activation(rs[:, 1, :], rs[:, 0, :], ACT.Sqrt).then_inc(s_sq, 1)

            def squares():
                count["sq"] += 1
                act.wait_ge(s_var, count["sq"])
                for t in range(NT):
                    ins = nc.scalar.activation(xf[:, t, :], z[:, t, :], ACT.Square, accum_out=rs[:, 0, t:t + 1])
                ins.then_inc(s_sq, 1)

            def transposed_out():
                for c in range(1, KC, 2):
                    act.wait_ge(s_tp, KC * (count["tpa"] // 3) + c + 1)
                    nc.scalar.activation(tD[:, c, :].rearrange("p (t n) -> p t n", t=NT),
                                         tiles5(bank(6, 2), 128), ACT.Copy).then_inc(s_tpa, 1)
                    count["tpa"] += 1

            root()
            transposed_out()
            for t in range(NT):
                act.wait_ge(s_hmm, t + 1)
                nc.scalar.activation(xf[:, t, :], ps[0:P, (t % 2) * 1024:(t % 2) * 1024 + D], ACT.Copy)\
                    .then_inc(s_hev, 1)
            act.wait_ge(s_cmm, EC)
            for i in range(NT):
                nc.scalar.activation(CT[:, i, 0:4 * P], ps[0:P, i * BANK:i * BANK + 4 * P], ACT.Copy)\
                    .then_inc(s_ct, 1)
            for i in range(NT):
                act.wait_ge(s_cT, i + 1)
                nc.scalar.activation(cds[:, i, :].rearrange("p (k n) -> p k n", k=NT),
                                     tiles5(bank(4 + 2 * (i % 2), 2), P), ACT.Copy).then_inc(s_cda, 1)
            root()
            fence(act, F_GRAPH)

            root()
            squares()
            root()
            act.wait_ge(s_rowsok, R_XN0)
            for t in range(NT):
                nc.scalar.activation(vst[t][:, :, 0:2, :], heads_twice(t), ACT.Copy).then_inc(s_vh, 1)
            act.wait_ge(s_zero, 48)

            def sides_out(h, q):
                act.wait_ge(s_sides, h + 1)
                for s, scale in ((0, 0.5), (1, 0.25)):
                    ins = nc.scalar.activation(sides[:, s, q, :].rearrange("p (t n) -> p t n", t=NT),
                                               side_bank(s), ACT.Copy, scale=scale)
                ins.then_inc(s_sidea, 1)

            def exp(j, m):
                act.wait_ge(s_mx, j * 10 + m + 1)
                nc.scalar.activation(prob32[:, m % 2, :], score_bank(m), ACT.Exp,
                                     bias=cols[:, m // 5, m % 5:m % 5 + 1],
                                     accum_out=cols[:, 2 + m // 5, m % 5:m % 5 + 1]).then_inc(s_exp, 1)

            def high(j, m):
                q, t = divmod(m, 5)
                act.wait_ge(s_mT, j * 10 + m + 1)
                act.wait_ge(s_mpv, j * 10 + 5 * q + 5)
                nc.scalar.activation(pT[:, 0, q, :, t * P:(t + 1) * P], tiles5(bank(4, 2), P), ACT.Copy)\
                    .then_inc(s_mTh, 1)

            def sum_out(j, m):
                act.wait_ge(s_mpv, j * 10 + 5 * (m // 5) + 10)
                nc.scalar.activation(outT, bank(6, 2)[:, 0:T], ACT.Copy).then_inc(s_mout, 1)

            def mha_turn(j, first, last):
                for m in range(10):
                    q, t = divmod(m, 5)
                    if t == NT - 1 and not (first and q == 0):
                        sum_out(j, m)
                    lagged(high, j, m, 1, first)
                    exp(j, m)
                    if t == 2 and not (last and q == 1):
                        sides_out(j * 2 + q + 1, 1 - q)

            sides_out(0, 0)
            mha_turn(0, True, False)
            with act.Fori(1, H // 2 - 1) as j:
                mha_turn(j, False, False)
            mha_turn(H // 2 - 1, False, True)
            high(H // 2 - 1, 9)
            sum_out(H // 2, 0)
            fence(act, F_MHA)

            def route():
                transposed_out()
                act.wait_ge(s_lge, count_route[0] + 1)
                nc.scalar.activation(sm[:, 1, :, :], sm[:, 0, :, :], ACT.Exp).then_inc(s_sel, 1)
                count_route[0] += 1

            count_route = [0]
            squares()
            root()
            route()
            fence(act, F_ROUTE0)
            ffn_scalar(act, ph_s, NG)
            fence(act, F_SHARED)
            ffn_scalar(act, ph_0, passes(act))
            fence(act, F_EXP0)
            fence(act, F_LAYER0)

            root()
            transposed_out()
            for n in range(NT * KC):
                act.wait_ge(s_ftv, n + 1)
                t, c = divmod(n, KC)
                nc.scalar.activation(z[:, t, 128 * c:128 * c + 128], bank(n % 4)[0:P, 128:256], ACT.Copy)\
                    .then_inc(s_fta, 1)
            act.wait_ge(s_ftv, NT * KC)
            for t in range(NT):
                nc.scalar.activation(values[:, t, :, 0:HD], xf[:, t, :].rearrange("p (h e) -> p h e", h=H),
                                     ACT.Copy).then_inc(s_gvh, 1)

            def branches(j, m):
                n = j * 10 + m
                q = m // 5
                if m % 5 == 0:
                    act.wait_ge(s_gb, j * 2 + q + 1)
                act.wait_ge(s_pT, n + 1)
                act.wait_ge(s_rm, n + 1)
                nc.scalar.activation(prob[:, m % 5, :], terms[q][:, m % 5, :], ACT.Exp,
                                     bias=cols[:, 2 + q, m % 5:m % 5 + 1])
                nc.scalar.activation(slow[:, m % 2, :], terms[q][:, m % 5, :], ACT.Exp, scale=0.2,
                                     bias=cols[:, 4 + q, m % 5:m % 5 + 1]).then_inc(s_ge, 1)

            def summed(j, m):
                act.wait_ge(s_pc, j * 10 + m + 1)
                nc.scalar.activation(prob[:, m % 5, :], prob[:, m % 5, :], ACT.Copy,
                                     accum_out=cols[:, 6 + m // 5, m % 5:m % 5 + 1]).then_inc(s_gs, 1)

            def gat_high(j, m):
                q, t = divmod(m, 5)
                act.wait_ge(s_pT, j * 10 + m + 1 + NT)
                act.wait_ge(s_pv, j * 10 + 5 * q + 5)
                nc.scalar.activation(pT[:, 0, q, :, t * P:(t + 1) * P], tiles5(bank(4, 2), P), ACT.Copy)\
                    .then_inc(s_gTh, 1)

            def gat_sum_out(h):
                act.wait_ge(s_pv, h * 5 + 15)
                nc.scalar.activation(outT, bank(6, 2)[:, 0:T], ACT.Copy).then_inc(s_gout, 1)

            def gat_turn(j, first):
                for m in range(10):
                    q, t = divmod(m, 5)
                    branches(j, m)
                    if t == 1 and not first:
                        gat_sum_out(j * 2 + q - 2)
                    lagged(gat_high, j, m, 3, first)
                    lagged(summed, j, m, 2, first)

            gat_turn(0, True)
            with act.Fori(1, H // 2) as j:
                gat_turn(j, False)
            gat_high(H // 2 - 1, 7)
            summed(H // 2 - 1, 8)
            gat_sum_out(H - 2)
            gat_high(H // 2 - 1, 8)
            summed(H // 2 - 1, 9)
            gat_high(H // 2 - 1, 9)
            gat_sum_out(H - 1)
            root()
            squares()
            root()
            route()
            fence(act, F_GAT)
            fence(act, F_ROUTE1)
            ffn_scalar(act, ph_1, passes(act))
            fence(act, F_EXP1)

        @block.vector
        def _(dve):
            count = {"v": 0, "sq": 0, "tp": 0, "route": 0}

            def step(ins):
                count["v"] += 1
                ins.then_inc(s_v, 1)
                dve.wait_ge(s_v, count["v"])

            def root_of(dst_):
                count["sq"] += 1
                dve.wait_ge(s_sq, count["sq"])
                step(nc.vector.reciprocal(dst_, rs[:, 1, :]))
                step(nc.vector.tensor_tensor(rs[:, 2, :], dst_, dst_, ALU.mult))
                step(nc.vector.tensor_tensor(rs[:, 2, :], rs[:, 2, :], rs[:, 0, :], ALU.mult))
                step(nc.vector.tensor_scalar(rs[:, 2, :], rs[:, 2, :], -0.5, 1.5, ALU.mult, ALU.add))
                step(nc.vector.tensor_tensor(dst_, dst_, rs[:, 2, :], ALU.mult))

            def layernorm():
                for t in range(NT):
                    for k in range(2):
                        ins = nc.vector.bn_stats(st[:, t, k, :], xres[:, t, k * D // 2:(k + 1) * D // 2])
                step(ins)
                for t in range(NT):
                    ins = nc.vector.bn_aggr(mv[:, t, :], st[:, t, :, :].rearrange("p a b -> p (a b)"))
                step(ins)
                nc.vector.tensor_scalar(rs[:, 0, :], mv[:, :, 1], 1e-5, None, ALU.add).then_inc(s_var, 1)
                root_of(rs[:, 3, :])
                for t in range(NT):
                    ins = nc.vector.tensor_scalar(z[:, t, :], xres[:, t, :], mv[:, t, 0:1], rs[:, 3, t:t + 1],
                                                  ALU.subtract, ALU.mult)
                step(ins)

            def rmsnorm(eps, v, n_vec):
                nc.vector.tensor_scalar(rs[:, 2, :], rs[:, 3, :], 1.0, None, ALU.mult).then_inc(s_var, 1)
                count["sq"] += 1
                dve.wait_ge(s_sq, count["sq"])
                nc.vector.tensor_scalar(rs[:, 0, :], rs[:, 0, :], 1.0 / D, eps, ALU.mult, ALU.add)\
                    .then_inc(s_var, 1)
                root_of(rs[:, 3, :])
                dve.wait_ge(s_vec[v], n_vec)
                for t in range(NT):
                    ins = nc.vector.scalar_tensor_tensor(out=xf[:, t, :], in0=z[:, t, :], scalar=rs[:, 3, t:t + 1],
                                                         in1=vec[:, v, :], op0=ALU.mult, op1=ALU.mult)
                ins.then_inc(s_rowsok, 1)

            def transposed_out():
                for c in range(0, KC, 2):
                    dve.wait_ge(s_tp, KC * (count["tp"] // 3) + c + 1)
                    nc.vector.tensor_copy(tD[:, c, :].rearrange("p (t n) -> p t n", t=NT),
                                          tiles5(bank(4, 2), 128)).then_inc(s_tpe, 1)
                    count["tp"] += 1

            dve.wait_ge(s_edge, 32)
            nc.vector.tensor_copy(edges_f[:, :, :], edges_i[:, :, :])
            dve.wait_ge(s_x, 16)
            layernorm()
            nc.vector.memset(a12[:, :, :, :], 0.0).then_inc(s_rowsok, 1)
            transposed_out()
            dve.wait_ge(s_vec[0], 16)
            dve.wait_ge(s_const, C_ALL)
            nc.vector.tensor_copy(ident16[:, :], ident[:, :])
            for a in range(2):
                nc.vector.tensor_copy(both[64 * a:64 * a + 64, :], ident[64 * a:64 * a + 64, 64 * a:64 * a + 64])
            for t in range(NT):
                ins = nc.vector.tensor_tensor(xres[:, t, :], xres[:, t, :], vec[:, 0, :], ALU.add)
            step(ins)

            def one_hot(j, s, first=False):
                c = j * EU + s
                if not first:
                    dve.wait_ge(s_cmm, c - EU + 1)
                for a in range(2):
                    col = edges_f[:, a, bass.ds(c, 1)] if not isinstance(c, int) else edges_f[:, a, c:c + 1]
                    ins = nc.vector.tensor_scalar(hot[:, s, a, :], iota16[:, :], col, None, ALU.is_equal)
                ins.then_inc(s_hot, 1)

            for s in range(EU):
                one_hot(0, s, True)
            with dve.Fori(1, EC // EU) as j:
                for s in range(EU):
                    one_hot(j, s)
            dve.wait_ge(s_cmm, EC)
            nc.vector.tensor_copy(CT[:, 0:4, 4 * P:T], bank(5)[0:P, 0:4 * P].rearrange("p (t n) -> p t n", t=4))
            nc.vector.tensor_copy(CT[:, 4, 4 * P:T], bank(6)[0:P, 0:P]).then_inc(s_ctv, 1)
            for i in range(NT):
                dve.wait_ge(s_cda, i + 1)
                nc.vector.tensor_scalar(mask[:, i, :], cds[:, i, :], 0.0, NEG, ALU.is_equal, ALU.mult)
                ins = nc.vector.tensor_reduce(rs[:, 0, i:i + 1], cds[:, i, :], AX.X, ALU.add)
                ins.then_inc(s_cdv, 1)
            dve.wait_ge(s_cdv, NT)
            nc.vector.tensor_scalar(rs[:, 0, :], rs[:, 0, :], 1.0, None, ALU.add).then_inc(s_var, 1)
            root_of(dinv[:, :])
            dve.wait_ge(s_hev, NT)
            for t in range(NT):
                ins = nc.vector.tensor_scalar(xf[:, t, :], xf[:, t, :], dinv[:, t:t + 1], None, ALU.mult)
            count["v"] += 1
            ins.then_inc(s_v, 1)
            dve.wait_ge(s_v, count["v"])
            nc.vector.memset(dot[0:1, 0:1], 0.0).then_inc(s_rowsok, 1)
            for i in range(NT):
                dve.wait_ge(s_agg, i + 1)
                step(nc.vector.tensor_tensor(z[:, i, :], ps[0:P, (i % 2) * 1024:(i % 2) * 1024 + D], xf[:, i, :],
                                             ALU.add))
                nc.vector.scalar_tensor_tensor(out=xres[:, i, :], in0=z[:, i, :], scalar=dinv[:, i:i + 1],
                                               in1=xres[:, i, :], op0=ALU.mult, op1=ALU.add).then_inc(s_aggv, 1)
            dve.wait_ge(s_aggv, NT)
            fence(dve, F_GRAPH)

            layernorm()
            rmsnorm(1e-5, 1, 16)
            for t in range(NT):
                dve.wait_ge(s_vh, t + 1)
                nc.vector.tensor_tensor(vst[t][:, :, 2:4, :], heads_twice(t), vst[t][:, :, 0:2, :],
                                        ALU.subtract).then_inc(s_vl, 1)

            def side_out(h, q):
                dve.wait_ge(s_sidea, h + 1)
                nc.vector.tensor_scalar(sides[:, 2, q, :].rearrange("p (t n) -> p t n", t=NT), side_bank(2),
                                        0.25, None, ALU.mult).then_inc(s_sidev, 1)

            def top(j, m):
                dve.wait_ge(s_s, j * 10 + m + 1)
                nc.vector.tensor_reduce(cols[:, m // 5, m % 5:m % 5 + 1], score_bank(m), AX.X, ALU.max,
                                        negate=True).then_inc(s_mx, 1)

            def low(j, m):
                q, t = divmod(m, 5)
                dve.wait_ge(s_mTh, j * 10 + m + 1)
                nc.vector.tensor_tensor(pT[:, 1, q, :, t * P:(t + 1) * P], tiles5(bank(4, 2), P),
                                        pT[:, 0, q, :, t * P:(t + 1) * P], ALU.subtract).then_inc(s_mTl, 1)

            def sums_inverted(h, q):
                dve.wait_ge(s_exp, h * 5 + 7)
                nc.vector.reciprocal(cols[:, 4 + q, :], cols[:, 2 + q, :]).then_inc(s_mrec, 1)

            def fin(h, q):
                dve.wait_ge(s_mback, h + 1)
                dve.wait_ge(s_mrec, h + 1)
                dve.wait_ge(s_madd, h + 1)
                nc.vector.tensor_tensor(outn, bank(6)[0:P, 0:NT * HD].rearrange("p (t e) -> p t e", t=NT),
                                        cols[:, 4 + q, :].unsqueeze(2).to_broadcast([P, NT, HD]), ALU.mult)\
                    .then_inc(s_mfin, 1)

            def mha_turn(j, first, last):
                for m in range(10):
                    q, t = divmod(m, 5)
                    if t == 0 and not first:
                        fin(j * 2 + q - 2, q)
                    top(j, m)
                    if t == 3 and not (last and q == 1):
                        side_out(j * 2 + q + 1, 1 - q)
                    lagged(low, j, m, 1, first)
                    if t == 1 and not (first and q == 0):
                        sums_inverted(j * 2 + q - 1, 1 - q)

            side_out(0, 0)
            mha_turn(0, True, False)
            with dve.Fori(1, H // 2 - 1) as j:
                mha_turn(j, False, False)
            mha_turn(H // 2 - 1, False, True)
            fin(H - 2, 0)
            low(H // 2 - 1, 9)
            sums_inverted(H - 1, 1)
            fin(H - 1, 1)
            fence(dve, F_MHA)

            def route(layer):
                transposed_out()
                bc = lambda a: a.unsqueeze(2).to_broadcast([P, NT, NE])
                per_t = lambda a: a.unsqueeze(1).to_broadcast([P, NT, NE])
                tmp, p, oh, sel, cand = sm[:, 0], sm[:, 1], [sm[:, 2], sm[:, 3]], sm[:, 4], sm[:, 5]
                p2, slot = sm[:, 6], sm[:, 7]
                top, best = rs[:, 0, :], rs[:, 1, :]
                dve.wait_ge(s_lg, layer + 1)
                lg = bank(0)[0:P, 0:NT * NE].rearrange("p (t e) -> p t e", t=NT)
                step(nc.vector.tensor_reduce(top, lg, AX.X, ALU.max))
                nc.vector.tensor_tensor(tmp, lg, bc(top), ALU.subtract).then_inc(s_lge, 1)
                dve.wait_ge(s_sel, layer + 1)
                step(nc.vector.tensor_reduce(top, p, AX.X, ALU.add))
                step(nc.vector.reciprocal(top, top))
                step(nc.vector.tensor_tensor(p, p, bc(top), ALU.mult))
                for k in range(2):
                    of = p if k == 0 else p2
                    step(nc.vector.tensor_reduce(wts[:, k, :], of, AX.X, ALU.max))
                    step(nc.vector.tensor_tensor(cand, of, bc(wts[:, k, :]), ALU.is_equal))
                    step(nc.vector.tensor_scalar(cand, cand, -float(NE), float(NE), ALU.mult, ALU.add))
                    step(nc.vector.tensor_tensor(cand, cand, cst8[:, 0], ALU.add))
                    step(nc.vector.tensor_reduce(best, cand, AX.X, ALU.min))
                    step(nc.vector.tensor_tensor(oh[k], cst8[:, 0], bc(best), ALU.is_equal))
                    if k == 0:
                        step(nc.vector.scalar_tensor_tensor(out=p2, in0=oh[0], scalar=-2.0, in1=p, op0=ALU.mult,
                                                            op1=ALU.add))
                nc.vector.tensor_tensor(sel, oh[0], oh[1], ALU.add).then_inc(s_rd, 1)
                if layer == 0:
                    step(nc.vector.tensor_scalar(wts[:, :, :], wts[:, :, :], 1e-7, None, ALU.max))
                    step(nc.vector.memset(cmb[:, :, :], 1.0))
                    step(nc.vector.tensor_tensor(tmp, oh[0], bc(wts[:, 0, :]), ALU.mult))
                    step(nc.vector.tensor_tensor(cand, oh[1], bc(wts[:, 1, :]), ALU.mult))
                    nc.vector.tensor_tensor(cmb[:, :, 0:NE], tmp, cand, ALU.add).then_inc(s_cm, 1)
                dve.wait_ge(s_rk, layer + 1)
                rank = bank(0)[0:P, 64:64 + NT * NE].rearrange("p (t e) -> p t e", t=NT)
                step(nc.vector.tensor_copy(s8[:, 0, :], bank(0)[0:P, 128:128 + NE]))
                step(nc.vector.tensor_scalar(s8[:, 1, :], s8[:, 0, :], float(B), None, ALU.is_gt))
                for k in range(2, (T - 1) // B + 1):
                    step(nc.vector.scalar_tensor_tensor(out=s8[:, 1, :], in0=s8[:, 0, :], scalar=float(k * B),
                                                        in1=s8[:, 1, :], op0=ALU.is_gt, op1=ALU.add))
                at = 1
                for k, d in enumerate((1, 2, 4)):
                    step(nc.vector.tensor_copy(s8[:, 2 + k, :], s8[:, at, :]))
                    step(nc.vector.tensor_tensor(s8[:, 2 + k, d:NE], s8[:, at, d:NE], s8[:, at, 0:NE - d], ALU.add))
                    at = 2 + k
                step(nc.vector.tensor_tensor(s8[:, 5, :], s8[:, at, :], s8[:, 1, :], ALU.subtract))
                step(nc.vector.scalar_tensor_tensor(out=s8[:, 6, :], in0=s8[:, 5, :], scalar=float(B),
                                                    in1=cst8[:, 2, 0, :], op0=ALU.mult, op1=ALU.add))
                step(nc.vector.tensor_scalar(cand, rank, float(B), None, ALU.is_ge))
                step(nc.vector.tensor_tensor(cand, cand, per_t(s8[:, 6, :]), ALU.mult))
                step(nc.vector.tensor_tensor(slot, rank, cst8[:, 1], ALU.add))
                step(nc.vector.tensor_tensor(slot, slot, cand, ALU.add))
                for k in range(2):
                    step(nc.vector.tensor_tensor(cand, slot, oh[k], ALU.mult))
                    step(nc.vector.tensor_reduce(slots_f[:, k, :], cand, AX.X, ALU.add))
                nc.vector.tensor_copy(slots_i[:, :, :], slots_f[:, :, :]).then_inc(s_slot, 1)
                step(nc.vector.tensor_tensor(tabf[:, 1, :, :], s8[0:1, at:at + 1, :].to_broadcast([1, NTAB, NE]),
                                             tabf[:, 0, :, :], ALU.is_le))
                step(nc.vector.tensor_reduce(tab1[:, 1, 0:NTAB], tabf[:, 1, :, :], AX.X, ALU.add))
                step(nc.vector.tensor_scalar(tab1[:, 1, 0:NTAB], tab1[:, 1, 0:NTAB], float(NE - 1), None, ALU.min))
                step(nc.vector.tensor_scalar(tab1[:, 2, :], tab1[:, 0, :], float(NE), None, ALU.is_lt))
                step(nc.vector.tensor_tensor(tab1[:, 2, :], tab1[:, 2, :], tab1[:, 0, :], ALU.mult))
                step(nc.vector.tensor_tensor(tab1[:, 1, 0:NTAB], tab1[:, 1, 0:NTAB], tab1[:, 2, 0:NTAB], ALU.add))
                step(nc.vector.tensor_scalar(tab1[:, 1, NTAB:NTAB + 1], s8[0:1, at, NE - 1:NE], float(NE), None,
                                             ALU.add))
                step(nc.vector.tensor_copy(tabi[:, 0, :], tab1[:, 1, :]))

            def combine(layer):
                if layer == 0:
                    dve.wait_ge(s_cmT, 1)
                    nc.vector.tensor_copy(cmbT[:, :].rearrange("e (t n) -> e t n", t=NT),
                                          tiles5(bank(0, 2), NE + 1)).then_inc(s_cmTv, 1)
                    for t in range(NT):
                        dve.wait_ge(s_bo, t + 1)
                        ins = nc.vector.tensor_tensor(xres[:, t, :], xres[:, t, :],
                                                      ps[0:P, (1 + t % 2) * 1024:(1 + t % 2) * 1024 + D], ALU.add)
                        ins.then_inc(s_bov, 1)
                    dve.wait_ge(s_bov, NT)
                for t in range(NT):
                    dve.wait_ge(s_gat[t], 32 * (layer + 1))
                    step(nc.vector.scalar_tensor_tensor(out=xres[:, t, :], in0=rows[t][0],
                                                        scalar=wts[:, 0, t:t + 1], in1=xres[:, t, :],
                                                        op0=ALU.mult, op1=ALU.add))
                    nc.vector.scalar_tensor_tensor(out=xres[:, t, :], in0=rows[t][1],
                                                   scalar=wts[:, 1, t:t + 1], in1=xres[:, t, :],
                                                   op0=ALU.mult, op1=ALU.add).then_inc(s_add, 1)

            rmsnorm(1e-5, 0, 32)
            dve.wait_ge(s_rowsok, R_XF0)
            dve.wait_ge(s_small, 48)
            route(0)
            fence(dve, F_ROUTE0)
            ffn_vector(dve, ph_s, NG)
            fence(dve, F_SHARED)
            ffn_vector(dve, ph_0, passes(dve))
            fence(dve, F_EXP0)
            combine(0)
            dve.wait_ge(s_add, NT)
            step(nc.vector.memset(wheads, 0.0))
            nc.vector.memset(dot[0:1, 0:1], 0.0).then_inc(s_wh, 1)
            fence(dve, F_LAYER0)

            layernorm()
            nc.vector.memset(dot[0:1, 0:1], 0.0).then_inc(s_rowsok, 1)
            transposed_out()
            for n in range(NT * KC):
                dve.wait_ge(s_ft, n + 1)
                t, c = divmod(n, KC)
                nc.vector.tensor_copy(xf[:, t, 128 * c:128 * c + 128], bank(n % 4)[0:P, 0:128]).then_inc(s_ftv, 1)
            dve.wait_ge(s_ftv, NT * KC)
            dve.wait_ge(s_al, 16 * 6)
            for t in range(NT):
                step(nc.vector.tensor_tensor(prod, xf[:, t:t + 1, :].to_broadcast([P, 2, D]), alr, ALU.mult))
                step(nc.vector.tensor_reduce(a12[:, :, t, 0:H],
                                             prod.rearrange("p a (h e) -> p a h e", h=H), AX.X, ALU.add))
            nc.vector.memset(dot[0:1, 0:1], 0.0).then_inc(s_am, 1)
            dve.wait_ge(s_aT, 1)
            step(nc.vector.tensor_copy(a1T.rearrange("h (t n) -> h t n", t=NT), tiles5(bank(4, 2), H)))

            for t in range(NT):
                dve.wait_ge(s_gvh, t + 1)
                nc.vector.tensor_tensor(values[:, t, :, HD:2 * HD], xf[:, t, :].rearrange("p (h e) -> p h e", h=H),
                                        values[:, t, :, 0:HD], ALU.subtract).then_inc(s_gvl, 1)

            def own_row(h, q):
                col = ident[0:H, bass.ds(h, 1)] if not isinstance(h, int) else ident[0:H, h:h + 1]
                nc.vector.tensor_scalar(a1m[:, q, :], a1T, col, None, ALU.mult).then_inc(s_am, 1)

            def edge_top(h, q, t):
                nc.vector.tensor_tensor_reduce(out=terms[q][:, t, :], in0=ps[0:P, q * 1024:q * 1024 + T],
                                               in1=mask[:, t, :], scale=1.0, scalar=-1e28, op0=ALU.add,
                                               op1=ALU.max, accum_out=cols[:, q, t:t + 1]).then_inc(s_gm, 1)

            def shifts(h, q):
                a2 = a12[:, 1, :, bass.ds(h, 1)] if not isinstance(h, int) else a12[:, 1, :, h:h + 1]
                a2 = a2.rearrange("p t a -> p (t a)")
                dve.wait_ge(s_gm, h * NT + NT)
                nc.vector.tensor_tensor(cols[:, 8, :], cols[:, q, :], a2, ALU.add).then_inc(s_gseq, 1)
                dve.wait_ge(s_gseq, h * 3 + 1)
                nc.vector.scalar_tensor_tensor(out=cols[:, 9, :], in0=cols[:, 8, :], scalar=0.2, in1=cols[:, 8, :],
                                               op0=ALU.mult, op1=ALU.max).then_inc(s_gseq, 1)
                dve.wait_ge(s_gseq, h * 3 + 2)
                nc.vector.tensor_tensor(cols[:, 2 + q, :], a2, cols[:, 9, :], ALU.subtract).then_inc(s_gseq, 1)
                nc.vector.scalar_tensor_tensor(out=cols[:, 4 + q, :], in0=a2, scalar=0.2, in1=cols[:, 9, :],
                                               op0=ALU.mult, op1=ALU.subtract).then_inc(s_gb, 1)

            own_row(0, 0)
            own_row(1, 1)
            dve.wait_ge(s_ab, 1)
            for t in range(NT):
                edge_top(0, 0, t)
            shifts(0, 0)

            def merge(j, m):
                dve.wait_ge(s_ge, j * 10 + m + 1)
                nc.vector.tensor_tensor(prob[:, m % 5, :], prob[:, m % 5, :], slow[:, m % 2, :],
                                        ALU.max).then_inc(s_rm, 1)

            def gat_low(j, m):
                q, t = divmod(m, 5)
                dve.wait_ge(s_gTh, j * 10 + m + 1)
                nc.vector.tensor_tensor(pT[:, 1, q, :, t * P:(t + 1) * P], tiles5(bank(4, 2), P),
                                        pT[:, 0, q, :, t * P:(t + 1) * P], ALU.subtract).then_inc(s_gTl, 1)

            def gat_sums_inverted(h, q):
                dve.wait_ge(s_gs, h * 5 + 5)
                nc.vector.tensor_scalar(cols[:, 10 + q, :], cols[:, 6 + q, :], 1e-37, None, ALU.max)\
                    .then_inc(s_rd, 1)
                dve.wait_ge(s_rd, h * 2 + N_RD + 1)
                nc.vector.reciprocal(cols[:, 10 + q, :], cols[:, 10 + q, :]).then_inc(s_rd, 1)

            def gat_fin(h, q):
                dve.wait_ge(s_gback, h + 1)
                dve.wait_ge(s_rd, h * 2 + N_RD + 2)
                dve.wait_ge(s_gadd, h + 1)
                nc.vector.tensor_tensor(outn, bank(6)[0:P, 0:NT * HD].rearrange("p (t e) -> p t e", t=NT),
                                        cols[:, 10 + q, :].unsqueeze(2).to_broadcast([P, NT, HD]), ALU.mult)\
                    .then_inc(s_gfin, 1)

            def gat_turn(j, first):
                for m in range(10):
                    q, t = divmod(m, 5)
                    h = j * 2 + q
                    lagged(merge, j, m, 1, first)
                    if t == 0:
                        dve.wait_ge(s_ab, h + 2)
                        own_row(h + 2, q)
                    edge_top(h + 1, 1 - q, t)
                    if t == 2 and not first:
                        gat_fin(h - 2, q)
                    lagged(gat_low, j, m, 3, first)
                    if t == 3 and not (first and q == 0):
                        gat_sums_inverted(h - 1, 1 - q)
                    if t == NT - 1:
                        shifts(h + 1, 1 - q)

            gat_turn(0, True)
            with dve.Fori(1, H // 2) as j:
                gat_turn(j, False)
            merge(H // 2 - 1, 9)
            gat_low(H // 2 - 1, 7)
            gat_low(H // 2 - 1, 8)
            gat_fin(H - 2, 0)
            gat_low(H // 2 - 1, 9)
            gat_sums_inverted(H - 1, 1)
            gat_fin(H - 1, 1)
            dve.wait_ge(s_gadd, H + 1)
            for t in range(NT):
                ins = nc.vector.scalar_tensor_tensor(out=xres[:, t, :], in0=z[:, t, :], scalar=0.0,
                                                     in1=xres[:, t, :], op0=ALU.max, op1=ALU.add)
            step(ins)
            layernorm()
            rmsnorm(1e-6, 1, 32)
            dve.wait_ge(s_rowsok, R_XF1)
            route(1)
            fence(dve, F_GAT)
            fence(dve, F_ROUTE1)
            ffn_vector(dve, ph_1, passes(dve))
            fence(dve, F_EXP1)
            combine(1)

        @block.tensor
        def _(pe):
            count = {"tp": 0}

            def transpose_rows(rows_):
                for c in range(KC):
                    k = count["tp"]
                    done = s_tpe if c % 2 == 0 else s_tpa
                    if k >= 2:
                        pe.wait_ge(done, (k - c) // 2 + c // 2)
                    o = bank(4 + 2 * (c % 2), 2)
                    for t in range(NT):
                        ins = nc.tensor.transpose(o[:, t * 128:t * 128 + P], rows_[:, t, c * 128:(c + 1) * 128],
                                                  ident[0:P, 0:P])
                    ins.then_inc(s_tp, 1)
                    count["tp"] += 1

            def transposed(k):
                pe.wait_ge(s_tpe, 3 * k)
                pe.wait_ge(s_tpa, 3 * k)

            pe.wait_ge(s_const, C_ALL)
            pe.wait_ge(s_rowsok, R_Z0)
            transpose_rows(z)
            transposed(1)
            pe.wait_ge(s_wg, 16)
            for t in range(NT):
                if t >= 2:
                    pe.wait_ge(s_hev, t - 1)
                for n0, n1 in ((0, BANK), (BANK, D)):
                    for c in range(KC):
                        ins = nc.tensor.matmul(ps[0:P, (t % 2) * 1024 + n0:(t % 2) * 1024 + n1],
                                               tD[:, c, t * P:(t + 1) * P], wg[:, c, n0:n1],
                                               start=c == 0, stop=c == KC - 1)
                ins.then_inc(s_hmm, 1)

            def edge_chunk(j, s, first, last):
                pe.wait_ge(s_hot, j * EU + s + 1)
                for i in range(NT):
                    src_ = hot[:, s, 0, i * P:(i + 1) * P]
                    nc.tensor.matmul(ps[0:P, i * BANK:i * BANK + 4 * P], src_, hot[:, s, 1, 0:4 * P],
                                     start=first, stop=last, skip_group_check=True)
                    at = 5 * BANK + i * P if i < 4 else 6 * BANK
                    ins = nc.tensor.matmul(ps[0:P, at:at + P], src_, hot[:, s, 1, 4 * P:T],
                                           start=first and i in (0, 4), stop=last, skip_group_check=True)
                ins.then_inc(s_cmm, 1)

            pe.wait_ge(s_hev, NT)
            for s in range(EU):
                edge_chunk(0, s, s == 0, False)
            with pe.Fori(1, EC // EU - 1) as j:
                for s in range(EU):
                    edge_chunk(j, s, False, False)
            for s in range(EU):
                edge_chunk(EC // EU - 1, s, False, s == EU - 1)
            pe.wait_ge(s_ct, NT)
            pe.wait_ge(s_ctv, 1)
            for i in range(NT):
                if i >= 2:
                    pe.wait_ge(s_cda, i - 1)
                o = bank(4 + 2 * (i % 2), 2)
                for k in range(NT):
                    ins = nc.tensor.transpose(o[0:P, k * 128:k * 128 + P], CT[:, k, i * P:(i + 1) * P],
                                              ident[0:P, 0:P])
                ins.then_inc(s_cT, 1)
            pe.wait_ge(s_rowsok, R_HS)
            for i in range(NT):
                if i >= 2:
                    pe.wait_ge(s_aggv, i - 1)
                for n0, n1 in ((0, BANK), (BANK, D)):
                    for k in range(NT):
                        ins = nc.tensor.matmul(ps[0:P, (i % 2) * 1024 + n0:(i % 2) * 1024 + n1],
                                               CT[:, k, i * P:(i + 1) * P], xf[:, k, n0:n1],
                                               start=k == 0, stop=k == NT - 1)
                ins.then_inc(s_agg, 1)
            fence(pe, F_GRAPH)

            pe.wait_ge(s_vl, NT)

            def parts(t, h, part):
                v = vst[t][:, bass.ds(h, 1), part:part + 2, :] if not isinstance(h, int) \
                    else vst[t][:, h:h + 1, part:part + 2, :]
                return v.rearrange("p a c e -> p (a c e)")

            def sides_transposed(h):
                for s, part in enumerate((1, 0, 2)):
                    for t in range(NT):
                        ins = nc.tensor.transpose(side_bank(s, t), parts(t, h, part), ident16[0:P, 0:P])
                ins.then_inc(s_sides, 1)

            def scores(j, m, last):
                q, t = divmod(m, 5)
                if t == 0:
                    pe.wait_ge(s_sidev, j * 2 + q + 1)
                if t == 4 and not (last and q == 1):
                    pe.wait_ge(s_sidev, j * 2 + q + 2)
                else:
                    pe.wait_ge(s_exp, j * 10 + m + (1, 1, 1, 2, 1)[t])
                for n0, n1 in ((0, BANK), (BANK, T)):
                    for s in (1, 2):
                        ins = nc.tensor.matmul(score_bank(m, n0, n1), sides[:, 0, q, t * P:(t + 1) * P],
                                               sides[:, s, q, n0:n1], start=s == 1, stop=s == 2)
                ins.then_inc(s_s, 1)

            def mha_transposed(j, m):
                n = j * 10 + m
                pe.wait_ge(s_exp, n + 3)
                pe.wait_ge(s_mTl, n + 1)
                for k in range(NT):
                    ins = nc.tensor.transpose(bank(4, 2)[0:P, k * 128:k * 128 + P],
                                              prob32[:, m % 2, k * P:(k + 1) * P], ident[0:P, 0:P])
                ins.then_inc(s_mT, 1)

            def weighted_chunk(h, q, k):
                if k == 0:
                    pe.wait_ge(s_mfin, h + 1)
                    pe.wait_ge(s_mTl, h * 5 + 6)
                v = parts(k, h, 1)
                for s in range(2):
                    for n0, n1 in ((0, BANK), (BANK, T)):
                        ins = nc.tensor.matmul(bank(6, 2)[:, n0:n1], v, pT[:, s, q, k, n0:n1],
                                               start=k == 0 and s == 0, stop=k == NT - 1 and s == 1)
                ins.then_inc(s_mpv, 1)

            def sum_back(h):
                pe.wait_ge(s_mout, h + 1)
                for t in range(NT):
                    ins = nc.tensor.matmul(bank(6)[0:P, t * HD:(t + 1) * HD], outT[:, t * P:(t + 1) * P],
                                           both[:, :], start=True, stop=True)
                ins.then_inc(s_mback, 1)

            def mha_turn(j, first, last):
                for m in range(10):
                    q, t = divmod(m, 5)
                    h = j * 2 + q
                    scores(j, m, last)
                    if t == 2 and not (last and q == 1):
                        pe.wait_ge(s_exp, j * 10 + m + 2)
                        sides_transposed(h + 1)
                    lagged(mha_transposed, j, m, 1, first)
                    if not (first and q == 0):
                        for k in ((), (0, 1), (2,), (3, 4), ())[t]:
                            weighted_chunk(h - 1, 1 - q, k)
                        if t == NT - 1:
                            sum_back(h - 1)

            sides_transposed(0)
            mha_turn(0, True, False)
            with pe.Fori(1, H // 2 - 1) as j:
                mha_turn(j, False, False)
            mha_turn(H // 2 - 1, False, True)
            mha_transposed(H // 2 - 1, 9)
            for k in range(NT):
                weighted_chunk(H - 1, 1, k)
            sum_back(H - 1)
            fence(pe, F_MHA)

            def route(layer, n_transposed, ok):
                pe.wait_ge(s_rowsok, ok)
                transpose_rows(xf)
                transposed(n_transposed)
                pe.wait_ge(s_small, 48)
                for t in range(NT):
                    for c in range(KC):
                        ins = nc.tensor.matmul(bank(0)[0:P, t * NE:(t + 1) * NE], tD[:, c, t * P:(t + 1) * P],
                                               gates[:, layer, c, :], start=c == 0, stop=c == KC - 1)
                ins.then_inc(s_lg, 1)
                pe.wait_ge(s_rd, 1 if layer == 0 else N_RD + 2 * H + 1)
                for t in range(NT + 1):
                    o = bank(0)[0:P, 64 + t * NE:64 + (t + 1) * NE] if t < NT else bank(0)[0:P, 128:128 + NE]
                    for k in range(min(t, NT)):
                        ins = nc.tensor.matmul(o, ones[0:P, 0:P], sm[:, 4, k, :], start=k == 0,
                                               stop=t == NT and k == NT - 1)
                    if t < NT:
                        ins = nc.tensor.matmul(o, tri[:, :], sm[:, 4, t, :], start=t == 0, stop=True)
                ins.then_inc(s_rk, 1)

            route(0, 2, R_XF0)
            fence(pe, F_ROUTE0)
            ffn_tensor(pe, ph_s, NG)
            fence(pe, F_SHARED)
            ffn_tensor(pe, ph_0, passes(pe))
            fence(pe, F_EXP0)
            pe.wait_ge(s_cm, 1)
            for t in range(NT):
                ins = nc.tensor.transpose(bank(0, 2)[0:NE + 1, t * 128:t * 128 + P], cmb[:, t, :], ident[0:P, 0:P])
            ins.then_inc(s_cmT, 1)
            pe.wait_ge(s_cmTv, 1)
            for t in range(NT):
                if t >= 2:
                    pe.wait_ge(s_bov, t - 1)
                for n0, n1 in ((0, BANK), (BANK, D)):
                    ins = nc.tensor.matmul(ps[0:P, (1 + t % 2) * 1024 + n0:(1 + t % 2) * 1024 + n1],
                                           cmbT[:, t * P:(t + 1) * P], bout[:, n0:n1], start=True, stop=True)
                ins.then_inc(s_bo, 1)
            fence(pe, F_LAYER0)

            pe.wait_ge(s_rowsok, R_Z1)
            transpose_rows(z)
            transposed(3)
            pe.wait_ge(s_al, 16 * 6)
            for n in range(NT * KC):
                t, c = divmod(n, KC)
                if n >= 4:
                    pe.wait_ge(s_fta, n - 3)
                nc.tensor.matmul(bank(n % 4)[0:P, 0:256], tD[:, c, t * P:(t + 1) * P], wheads,
                                 start=True, stop=True).then_inc(s_ft, 1)
            pe.wait_ge(s_am, 1)
            for t in range(NT):
                ins = nc.tensor.transpose(bank(4, 2)[0:H, t * 128:t * 128 + P], a12[:, 0, t, 0:H],
                                          ident[0:P, 0:P])
            ins.then_inc(s_aT, 1)

            def source_term(h, q, fresh=False):
                pe.wait_ge(s_am, h + 2)
                if not fresh:
                    pe.wait_ge(s_gm, h * NT - NT)
                for n0, n1 in ((0, BANK), (BANK, T)):
                    ins = nc.tensor.matmul(ps[0:P, q * 1024 + n0:q * 1024 + n1], ones[0:H, 0:P],
                                           a1m[:, q, n0:n1], start=True, stop=True)
                ins.then_inc(s_ab, 1)

            def gat_transposed(j, m):
                n = j * 10 + m
                pe.wait_ge(s_gs, n + 1)
                pe.wait_ge(s_gTl, n + 1)
                for k in range(NT):
                    ins = nc.tensor.transpose(bank(4, 2)[0:P, k * 128:k * 128 + P],
                                              prob[:, m % 5, k * P:(k + 1) * P], ident[0:P, 0:P])
                ins.then_inc(s_pT, 1)

            def gat_chunk(h, q, k):
                if k == 0:
                    pe.wait_ge(s_gfin, h + 1)
                    pe.wait_ge(s_gTl, h * 5 + 6)
                v = values[:, k, bass.ds(h, 1), :].rearrange("p a e -> p (a e)") if not isinstance(h, int) \
                    else values[:, k, h, :]
                for s in range(2):
                    for n0, n1 in ((0, BANK), (BANK, T)):
                        ins = nc.tensor.matmul(bank(6, 2)[:, n0:n1], v, pT[:, s, q, k, n0:n1],
                                               start=k == 0 and s == 0, stop=k == NT - 1 and s == 1)
                ins.then_inc(s_pv, 1)

            def gat_back(h):
                pe.wait_ge(s_gout, h + 1)
                for t in range(NT):
                    ins = nc.tensor.matmul(bank(6)[0:P, t * HD:(t + 1) * HD], outT[:, t * P:(t + 1) * P],
                                           both[:, :], start=True, stop=True)
                ins.then_inc(s_gback, 1)

            def gat_turn(j, first):
                for m in range(10):
                    q, t = divmod(m, 5)
                    h = j * 2 + q
                    if t == 3:
                        source_term(h + 2, q)
                    lagged(gat_transposed, j, m, 2, first)
                    if t >= 3 and not (first and q == 0):
                        for k in ((0, 1), (2, 3))[t - 3]:
                            gat_chunk(h - 1, 1 - q, k)
                    if t == 0 and not first:
                        gat_chunk(h - 2, q, NT - 1)
                    if t == 1 and not first:
                        gat_back(h - 2)

            pe.wait_ge(s_fta, NT * KC)
            source_term(0, 0, True)
            source_term(1, 1, True)
            pe.wait_ge(s_gvl, NT)
            gat_turn(0, True)
            with pe.Fori(1, H // 2) as j:
                gat_turn(j, False)
            gat_transposed(H // 2 - 1, 8)
            gat_chunk(H - 2, 0, NT - 1)
            gat_transposed(H // 2 - 1, 9)
            gat_back(H - 2)
            for k in range(NT):
                gat_chunk(H - 1, 1, k)
            gat_back(H - 1)
            route(1, 4, R_XF1)
            fence(pe, F_GAT)
            fence(pe, F_ROUTE1)
            ffn_tensor(pe, ph_1, passes(pe))
            fence(pe, F_EXP1)


def kernel(x, src, dst, L0_gnn_W, L0_gnn_b, L0_ffn_norm1_w, L0_ffn_norm3_w, L0_ffn_gate_w, L0_ffn_w1, L0_ffn_b1,
           L0_ffn_w2, L0_ffn_b2, L0_ffn_w3, L0_ffn_b3, L0_ffn_fc1_w, L0_ffn_fc1_b, L0_ffn_fc2_w, L0_ffn_fc2_b,
           L1_gnn_W_fc, L1_gnn_attn_l, L1_gnn_attn_r, L1_gnn_W_res, L1_ffn_norm_w, L1_ffn_router_w,
           L1_ffn_gate_w, L1_ffn_up_w, L1_ffn_down_w):
    import numpy as np
    import concourse.bacc as bacc
    from concourse.bass_utils import run_bass_kernel_spmd

    def up_cols(w):
        w = np.asarray(w)
        lead = w.shape[:-2]
        w = w.reshape(*lead, w.shape[-2] // 128, 128, KC, 128)
        n = len(lead)
        w = w.transpose(*range(n), n, n + 3, n + 2, n + 1)
        return w.reshape(*w.shape[:n + 2], D)

    def down_rows(w):
        w = np.asarray(w)
        w = np.swapaxes(w, -1, -2)
        return w.reshape(*w.shape[:-2], w.shape[-2] // 128, 128, D)

    def bias_col(b):
        b = np.asarray(b)
        return b.reshape(*b.shape[:-1], b.shape[-1] // 128, 128, 1)

    b1s = bias_col(L0_ffn_fc1_b)
    arrays = {
        "x": np.asarray(x), "src": np.asarray(src), "dst": np.asarray(dst), "gnn_w": np.asarray(L0_gnn_W),
        "vecs": np.stack([np.asarray(v) for v in (L0_gnn_b, L0_ffn_norm1_w, L0_ffn_norm3_w, L1_ffn_norm_w)]),
        "gate0": np.asarray(L0_ffn_gate_w).T, "gate1": np.asarray(L1_ffn_router_w).T,
        "units0": np.concatenate([up_cols(L0_ffn_w1), up_cols(L0_ffn_w3), down_rows(L0_ffn_w2),
                                  bias_col(L0_ffn_b1), bias_col(L0_ffn_b3)], -1),
        "units_s": np.concatenate([up_cols(L0_ffn_fc1_w), down_rows(L0_ffn_fc2_w), b1s, b1s], -1),
        "units1": np.concatenate([up_cols(L1_ffn_gate_w), up_cols(L1_ffn_up_w), down_rows(L1_ffn_down_w)], -1),
        "bias_out": np.concatenate([np.asarray(L0_ffn_b2), np.asarray(L0_ffn_fc2_b)[None]], 0),
        "w_heads": np.stack([np.asarray(L1_gnn_W_fc).T, np.asarray(L1_gnn_W_res).T], 1),
        "attn_lr": np.stack([np.asarray(L1_gnn_attn_l).reshape(D), np.asarray(L1_gnn_attn_r).reshape(D)]),
    }
    arrays = {f"in_{k}": np.ascontiguousarray(v) for k, v in arrays.items()}
    nc = bacc.Bacc("TRN2", target_bir_lowering=False, num_devices=1)
    args = [nc.dram_tensor(k, v.shape, mybir.dt.from_np(v.dtype), kind="ExternalInput").ap()
            for k, v in arrays.items()]
    result = nc.dram_tensor("out_0", (T, D), F32, kind="ExternalOutput").ap()
    bass_gnn_moe_stack(nc, *args, result)
    r = run_bass_kernel_spmd(nc, [arrays], core_ids=[0])
    return r.results[0]["out_0"]
```
